# Optimizing a Trainium2 kernel written in Bass

```python
import numpy as np
import jax
import jax.numpy as jnp

def _softmax(x, axis=-1):
    return jax.nn.softmax(x, axis=axis)

def _gelu(x):
    return jax.nn.gelu(x, approximate=True)

def _silu(x):
    return jax.nn.silu(x)

def _sigmoid(x):
    return jax.nn.sigmoid(x)

def _layernorm(x, axis=-1, eps=1e-05):
    m = jnp.mean(x, axis=axis, keepdims=True)
    v = jnp.var(x, axis=axis, keepdims=True)
    return (x - m) / jnp.sqrt(v + eps)

def _scatter_add(tgt, idx, src, axis=0):
    return tgt.at[idx].add(src)

def _segment_sum(src, seg, n):
    return jax.ops.segment_sum(src, seg, n)
kernel_name = 'mk_gnn_preln_d4_gnn_r16_2db554'

def setup_inputs(seed: int=0):
    np.random.seed(seed)
    _w = jnp.asarray

    def _rec_inputs():
        import jax
        import jax.numpy as jnp
        _gk = jax.random.key(seed)
        x = -8.776e-05 + 1 * jax.random.normal(jax.random.fold_in(_gk, 1), (6250, 256), jnp.float32)
        src = jax.random.randint(jax.random.fold_in(_gk, 2), (100000,), 0, 6250, jnp.int32)
        dst = jnp.minimum((6250 * jax.random.uniform(jax.random.fold_in(_gk, 3), (100000,)) ** 2.0).astype(jnp.int32), 99999)
        _o = jnp.argsort(dst, stable=True)
        src = src[_o]
        dst = dst[_o]
        edge_attr_64 = 0.000279952 + 1.00013 * jax.random.normal(jax.random.fold_in(_gk, 12), (100000, 64), jnp.float32)
        edge_type_64 = jax.random.randint(jax.random.fold_in(_gk, 14), (100000,), 0, 64, jnp.int32)
        return (x, src, dst, edge_attr_64, edge_type_64)
    x, src, dst, edge_attr_64, edge_type_64 = _rec_inputs()

    def _L0_gnn_setup():
        import jax, jax.numpy as jnp
        import numpy as np
        N, E = (1250, 20000)
        IN_CH, EDGE_DIM = (256, 64)
        HEADS, OUT_CH = (8, 32)
        HC = HEADS * OUT_CH
        key = jax.random.key(seed)
        ks = jax.random.split(key, 12)
        s_in = 1.0 / np.sqrt(IN_CH)
        s_e = 1.0 / np.sqrt(EDGE_DIM)
        return {'x': jax.random.normal(ks[0], (N, IN_CH), dtype=jnp.float32), 'edge_index': jax.random.randint(ks[1], (2, E), 0, N, dtype=jnp.int64), 'edge_attr': jax.random.normal(ks[2], (E, EDGE_DIM), dtype=jnp.float32), 'Wq': jax.random.uniform(ks[3], (HC, IN_CH), jnp.float32, -s_in, s_in), 'bq': jnp.zeros((HC,), jnp.float32), 'Wk': jax.random.uniform(ks[4], (HC, IN_CH), jnp.float32, -s_in, s_in), 'bk': jnp.zeros((HC,), jnp.float32), 'Wv': jax.random.uniform(ks[5], (HC, IN_CH), jnp.float32, -s_in, s_in), 'bv': jnp.zeros((HC,), jnp.float32), 'We': jax.random.uniform(ks[6], (HC, EDGE_DIM), jnp.float32, -s_e, s_e), 'Wskip': jax.random.uniform(ks[7], (HC, IN_CH), jnp.float32, -s_in, s_in), 'bskip': jnp.zeros((HC,), jnp.float32)}
    _L0_gnn_all = _L0_gnn_setup()
    _L0_gnn_in = {k: v for k, v in _L0_gnn_all.items() if k in ('Wq', 'bq', 'Wk', 'bk', 'Wv', 'bv', 'We', 'Wskip', 'bskip')}
    del _L0_gnn_all

    def _L1_gnn_setup():
        import jax, jax.numpy as jnp
        import numpy as np
        N_NODES = 3125
        N_EDGES = 31250
        IN_DIM = 256
        HID = 64
        HEADS = 4
        N_REL = 64
        key = jax.random.key(seed)
        ks = jax.random.split(key, 16)
        s = 0.02
        return {'node_features': jax.random.normal(ks[0], (N_NODES, IN_DIM), jnp.float32), 'edge_index': jax.random.randint(ks[1], (2, N_EDGES), 0, N_NODES, jnp.int32), 'edge_relations': jax.random.randint(ks[2], (N_EDGES,), 0, N_REL, jnp.int32), 'query_emb': jax.random.normal(ks[3], (IN_DIM,), jnp.float32), 'Wq': jax.random.normal(ks[4], (IN_DIM, HID * HEADS), jnp.float32) * s, 'bq': jnp.zeros((HID * HEADS,), jnp.float32), 'Wk': jax.random.normal(ks[5], (IN_DIM, HID * HEADS), jnp.float32) * s, 'bk': jnp.zeros((HID * HEADS,), jnp.float32), 'Wv': jax.random.normal(ks[6], (IN_DIM, HID * HEADS), jnp.float32) * s, 'bv': jnp.zeros((HID * HEADS,), jnp.float32), 'rel_w': jax.random.normal(ks[7], (N_REL, HID), jnp.float32) * s, 'Wo': jax.random.normal(ks[8], (HID * HEADS, IN_DIM), jnp.float32) * s, 'bo': jnp.zeros((IN_DIM,), jnp.float32), 'gamma': jnp.ones((IN_DIM,), jnp.float32), 'beta': jnp.zeros((IN_DIM,), jnp.float32)}
    _L1_gnn_all = _L1_gnn_setup()
    _L1_gnn_in = {k: v for k, v in _L1_gnn_all.items() if k in ('query_emb', 'Wq', 'bq', 'Wk', 'bk', 'Wv', 'bv', 'rel_w', 'Wo', 'bo', 'gamma', 'beta')}
    del _L1_gnn_all

    def _L2_gnn_setup():
        import jax, jax.numpy as jnp
        import numpy as np
        N_NODES = 6250
        N_EDGES = 100000
        IN_FEATS = 256
        OUT_FEATS = 64
        NHEAD = 4
        ALPHA = 0.2
        key = jax.random.key(seed)
        k1, k2, k3, k4, k5, k6 = jax.random.split(key, 6)
        stdv_w = np.sqrt(6.0 / (IN_FEATS + OUT_FEATS * NHEAD))
        stdv_a = np.sqrt(6.0 / (NHEAD + OUT_FEATS))
        return {'x': jax.random.normal(k1, (N_NODES, IN_FEATS), dtype=jnp.float32), 'W': jax.random.uniform(k2, (IN_FEATS, OUT_FEATS * NHEAD), minval=-stdv_w, maxval=stdv_w, dtype=jnp.float32), 'a_l': jax.random.uniform(k3, (1, NHEAD, OUT_FEATS), minval=-stdv_a, maxval=stdv_a, dtype=jnp.float32), 'a_r': jax.random.uniform(k4, (1, NHEAD, OUT_FEATS), minval=-stdv_a, maxval=stdv_a, dtype=jnp.float32), 'row': jax.random.randint(k5, (N_EDGES,), 0, N_NODES, dtype=jnp.int32), 'col': jax.random.randint(k6, (N_EDGES,), 0, N_NODES, dtype=jnp.int32)}
    _L2_gnn_all = _L2_gnn_setup()
    _L2_gnn_in = {k: v for k, v in _L2_gnn_all.items() if k in ('W', 'a_l', 'a_r')}
    del _L2_gnn_all

    def _L3_gnn_setup():
        import jax, jax.numpy as jnp
        import numpy as np
        LN2 = 0.6931471805599453
        N_ATOMS = 3125
        N_PAIRS = 50000
        F = 256
        RBF = 64
        N_RES = 3
        key = jax.random.key(seed)
        ks = jax.random.split(key, 16)
        inp = {'atomic_embedding': jax.random.normal(ks[0], (N_ATOMS, F), dtype=jnp.float32), 'f_ij': jax.random.normal(ks[1], (N_PAIRS, RBF), dtype=jnp.float32), 'idx_i': jax.random.randint(ks[2], (N_PAIRS,), 0, N_ATOMS, dtype=jnp.int32), 'idx_j': jax.random.randint(ks[3], (N_PAIRS,), 0, N_ATOMS, dtype=jnp.int32), 'G': jax.random.normal(ks[4], (F, RBF), dtype=jnp.float32), 'Wi': jax.random.normal(ks[5], (F, F), dtype=jnp.float32) * 0.05, 'bi': jax.random.normal(ks[6], (F,), dtype=jnp.float32) * 0.05, 'Wj': jax.random.normal(ks[7], (F, F), dtype=jnp.float32) * 0.05, 'bj': jax.random.normal(ks[8], (F,), dtype=jnp.float32) * 0.05, 'res_w1': jax.random.normal(ks[9], (N_RES, F, F), dtype=jnp.float32) * 0.05, 'res_b1': jax.random.normal(ks[10], (N_RES, F), dtype=jnp.float32) * 0.05, 'res_w2': jax.random.normal(ks[11], (N_RES, F, F), dtype=jnp.float32) * 0.05, 'res_b2': jax.random.normal(ks[12], (N_RES, F), dtype=jnp.float32) * 0.05, 'Wv': jax.random.normal(ks[13], (F, F), dtype=jnp.float32) * 0.05, 'bv': jax.random.normal(ks[14], (F,), dtype=jnp.float32) * 0.05}
        return inp
    _L3_gnn_all = _L3_gnn_setup()
    _L3_gnn_in = {k: v for k, v in _L3_gnn_all.items() if k in ('G', 'Wi', 'bi', 'Wj', 'bj', 'res_w1', 'res_b1', 'res_w2', 'res_b2', 'Wv', 'bv')}
    del _L3_gnn_all
    return {'x': x, 'src': src, 'dst': dst, 'edge_attr_64': edge_attr_64, 'edge_type_64': edge_type_64, 'L0_gnn_Wq': _L0_gnn_in['Wq'], 'L0_gnn_bq': _L0_gnn_in['bq'], 'L0_gnn_Wk': _L0_gnn_in['Wk'], 'L0_gnn_bk': _L0_gnn_in['bk'], 'L0_gnn_Wv': _L0_gnn_in['Wv'], 'L0_gnn_bv': _L0_gnn_in['bv'], 'L0_gnn_We': _L0_gnn_in['We'], 'L0_gnn_Wskip': _L0_gnn_in['Wskip'], 'L0_gnn_bskip': _L0_gnn_in['bskip'], 'L1_gnn_query_emb': _L1_gnn_in['query_emb'], 'L1_gnn_Wq': _L1_gnn_in['Wq'], 'L1_gnn_bq': _L1_gnn_in['bq'], 'L1_gnn_Wk': _L1_gnn_in['Wk'], 'L1_gnn_bk': _L1_gnn_in['bk'], 'L1_gnn_Wv': _L1_gnn_in['Wv'], 'L1_gnn_bv': _L1_gnn_in['bv'], 'L1_gnn_rel_w': _L1_gnn_in['rel_w'], 'L1_gnn_Wo': _L1_gnn_in['Wo'], 'L1_gnn_bo': _L1_gnn_in['bo'], 'L1_gnn_gamma': _L1_gnn_in['gamma'], 'L1_gnn_beta': _L1_gnn_in['beta'], 'L2_gnn_W': _L2_gnn_in['W'], 'L2_gnn_a_l': _L2_gnn_in['a_l'], 'L2_gnn_a_r': _L2_gnn_in['a_r'], 'L3_gnn_G': _L3_gnn_in['G'], 'L3_gnn_Wi': _L3_gnn_in['Wi'], 'L3_gnn_bi': _L3_gnn_in['bi'], 'L3_gnn_Wj': _L3_gnn_in['Wj'], 'L3_gnn_bj': _L3_gnn_in['bj'], 'L3_gnn_res_w1': _L3_gnn_in['res_w1'], 'L3_gnn_res_b1': _L3_gnn_in['res_b1'], 'L3_gnn_res_w2': _L3_gnn_in['res_w2'], 'L3_gnn_res_b2': _L3_gnn_in['res_b2'], 'L3_gnn_Wv': _L3_gnn_in['Wv'], 'L3_gnn_bv': _L3_gnn_in['bv']}

def reference(x, src, dst, edge_attr_64, edge_type_64, L0_gnn_Wq, L0_gnn_bq, L0_gnn_Wk, L0_gnn_bk, L0_gnn_Wv, L0_gnn_bv, L0_gnn_We, L0_gnn_Wskip, L0_gnn_bskip, L1_gnn_query_emb, L1_gnn_Wq, L1_gnn_bq, L1_gnn_Wk, L1_gnn_bk, L1_gnn_Wv, L1_gnn_bv, L1_gnn_rel_w, L1_gnn_Wo, L1_gnn_bo, L1_gnn_gamma, L1_gnn_beta, L2_gnn_W, L2_gnn_a_l, L2_gnn_a_r, L3_gnn_G, L3_gnn_Wi, L3_gnn_bi, L3_gnn_Wj, L3_gnn_bj, L3_gnn_res_w1, L3_gnn_res_b1, L3_gnn_res_w2, L3_gnn_res_b2, L3_gnn_Wv, L3_gnn_bv):
    import jax
    import jax.numpy as jnp

    def _L0_gnn_ref(x, edge_index, edge_attr, Wq, bq, Wk, bk, Wv, bv, We, Wskip, bskip):
        import jax, jax.numpy as jnp
        import numpy as np
        N, E = (1250, 20000)
        IN_CH, EDGE_DIM = (256, 64)
        HEADS, OUT_CH = (8, 32)
        HC = HEADS * OUT_CH
        n = x.shape[0]
        src, dst = (edge_index[0], edge_index[1])
        q = (x @ Wq.T + bq).reshape(n, HEADS, OUT_CH)
        k = (x @ Wk.T + bk).reshape(n, HEADS, OUT_CH)
        v = (x @ Wv.T + bv).reshape(n, HEADS, OUT_CH)
        e = (edge_attr @ We.T).reshape(-1, HEADS, OUT_CH)
        k_e = k[src] + e
        v_e = v[src] + e
        alpha = jnp.einsum('ehc,ehc->eh', q[dst], k_e) / jnp.sqrt(jnp.float32(OUT_CH))
        m = jax.ops.segment_max(alpha, dst, num_segments=n)
        m = jnp.where(jnp.isfinite(m), m, 0.0)
        p = jnp.exp(alpha - m[dst])
        s = jax.ops.segment_sum(p, dst, num_segments=n)
        w = p / (s[dst] + 1e-16)
        out = jax.ops.segment_sum(v_e * w[:, :, None], dst, num_segments=n)
        out = out.reshape(n, HC) + (x @ Wskip.T + bskip)
        return out

    def _L1_gnn_ref(node_features, edge_index, edge_relations, query_emb, Wq, bq, Wk, bk, Wv, bv, rel_w, Wo, bo, gamma, beta):
        import jax, jax.numpy as jnp
        import numpy as np
        N_NODES = 3125
        N_EDGES = 31250
        IN_DIM = 256
        HID = 64
        HEADS = 4
        N_REL = 64
        N = node_features.shape[0]
        D = rel_w.shape[1]
        H = Wq.shape[1] // D
        enh = node_features + 0.1 * query_emb[None, :]
        Q = (enh @ Wq + bq).reshape(N, H, D)
        K = (enh @ Wk + bk).reshape(N, H, D)
        V = (enh @ Wv + bv).reshape(N, H, D)
        src, dst = (edge_index[0], edge_index[1])
        rel = rel_w[edge_relations]
        mod_k = K[src] + 0.2 * rel[:, None, :]
        scores = jnp.einsum('ehd,ehd->eh', Q[dst], mod_k) / D ** 0.5
        seg_max = jax.ops.segment_max(scores, dst, num_segments=N)
        ex = jnp.exp(scores - seg_max[dst])
        denom = jax.ops.segment_sum(ex, dst, num_segments=N)
        w = ex / denom[dst]
        agg = jax.ops.segment_sum(w[:, :, None] * V[src], dst, num_segments=N)
        deg = jax.ops.segment_sum(jnp.ones((src.shape[0],), jnp.float32), dst, num_segments=N)
        msgs = jnp.where(deg[:, None, None] > 0, agg, V)
        out = msgs.reshape(N, H * D) @ Wo + bo
        x = out + node_features
        mu = jnp.mean(x, axis=-1, keepdims=True)
        var = jnp.var(x, axis=-1, keepdims=True)
        return (x - mu) / jnp.sqrt(var + 1e-05) * gamma + beta

    def _L2_gnn_ref(x, W, a_l, a_r, row, col):
        import jax, jax.numpy as jnp
        import numpy as np
        N_NODES = 6250
        N_EDGES = 100000
        IN_FEATS = 256
        OUT_FEATS = 64
        NHEAD = 4
        ALPHA = 0.2
        n = x.shape[0]
        h = (x @ W).reshape(n, NHEAD, OUT_FEATS)
        h = jnp.where(jnp.isnan(h), 0.0, h)
        h_l = (a_l * h).sum(-1)
        h_r = (a_r * h).sum(-1)
        e = h_l[row] + h_r[col]
        e = jnp.where(e > 0, e, ALPHA * e)
        m = jax.ops.segment_max(e, row, num_segments=n)
        m = jnp.where(jnp.isfinite(m), m, 0.0)
        ex = jnp.exp(e - m[row])
        denom = jax.ops.segment_sum(ex, row, num_segments=n)
        att = ex / (denom[row] + 1e-16)
        msg = att[:, :, None] * h[col]
        out = jax.ops.segment_sum(msg, row, num_segments=n)
        return out.reshape(n, NHEAD * OUT_FEATS)

    def _L3_gnn_ref(atomic_embedding, f_ij, idx_i, idx_j, G, Wi, bi, Wj, bj, res_w1, res_b1, res_w2, res_b2, Wv, bv):
        import jax, jax.numpy as jnp
        import numpy as np
        LN2 = 0.6931471805599453
        N_ATOMS = 3125
        N_PAIRS = 50000
        F = 256
        RBF = 64
        N_RES = 3
        sp = jax.nn.softplus
        x = sp(atomic_embedding) - LN2
        x_i_prime = sp(x @ Wi.T + bi)
        x_j_all = sp(x @ Wj.T + bj)
        x_j_prime = x_j_all[idx_j]
        f_ij_prime = f_ij @ G.T
        msg = x_j_prime * f_ij_prime
        summed = jax.ops.segment_sum(msg, idx_i, num_segments=atomic_embedding.shape[0])
        v = x_i_prime + summed
        for k in range(res_w1.shape[0]):
            h = sp(v @ res_w1[k].T + res_b1[k])
            v = v + h @ res_w2[k].T + res_b2[k]
        return sp(v) @ Wv.T + bv
    edge_index = jnp.stack([src, dst])
    h = jnp.maximum(_layernorm(x, axis=-1), 0.0)
    x = x + _L0_gnn_ref(h, edge_index, edge_attr_64, L0_gnn_Wq, L0_gnn_bq, L0_gnn_Wk, L0_gnn_bk, L0_gnn_Wv, L0_gnn_bv, L0_gnn_We, L0_gnn_Wskip, L0_gnn_bskip)
    h = jnp.maximum(_layernorm(x, axis=-1), 0.0)
    x = x + _L1_gnn_ref(h, edge_index, edge_type_64, L1_gnn_query_emb, L1_gnn_Wq, L1_gnn_bq, L1_gnn_Wk, L1_gnn_bk, L1_gnn_Wv, L1_gnn_bv, L1_gnn_rel_w, L1_gnn_Wo, L1_gnn_bo, L1_gnn_gamma, L1_gnn_beta)
    h = jnp.maximum(_layernorm(x, axis=-1), 0.0)
    x = x + _L2_gnn_ref(h, L2_gnn_W, L2_gnn_a_l, L2_gnn_a_r, src, dst)
    h = jnp.maximum(_layernorm(x, axis=-1), 0.0)
    x = x + _L3_gnn_ref(h, edge_attr_64, src, dst, L3_gnn_G, L3_gnn_Wi, L3_gnn_bi, L3_gnn_Wj, L3_gnn_bj, L3_gnn_res_w1, L3_gnn_res_b1, L3_gnn_res_w2, L3_gnn_res_b2, L3_gnn_Wv, L3_gnn_bv)
    return x

_drawn_inputs = setup_inputs


def setup_inputs(seed=0):
    import zlib

    import numpy as np

    out = dict(_drawn_inputs(seed))
    spreads = {'L0_gnn_bq': (0.0, 0.8),
     'L0_gnn_bk': (0.0, 2.0),
     'L0_gnn_bv': (0.0, 0.331),
     'L0_gnn_bskip': (0.0, 0.328),
     'L1_gnn_bq': (0.0, 2.0),
     'L1_gnn_bk': (0.0, 2.0),
     'L1_gnn_bv': (0.0, 0.8),
     'L1_gnn_bo': (0.0, 1.469),
     'L1_gnn_gamma': (1.0, 0.2),
     'L1_gnn_beta': (0.0, 0.563)}
    factors = {'L0_gnn_Wq': 3.435,
     'L0_gnn_Wk': 7.513,
     'L1_gnn_query_emb': 8.0,
     'L1_gnn_Wq': 8.0,
     'L1_gnn_Wk': 8.0,
     'L1_gnn_Wv': 5.414,
     'L1_gnn_rel_w': 200.0,
     'L1_gnn_Wo': 4.718,
     'L2_gnn_a_l': 90.677,
     'L2_gnn_a_r': 3.305,
     'L3_gnn_Wi': 5.968,
     'L3_gnn_bi': 43.242,
     'L3_gnn_res_b1': 33.164,
     'L3_gnn_res_b2': 8.0,
     'L3_gnn_bv': 8.0}
    for name, (base, spread) in spreads.items():
        noise = np.random.default_rng([zlib.crc32(name.encode()), seed]).standard_normal(out[name].shape)
        drawn = base * np.exp(spread * noise) if base else spread * noise
        out[name] = jnp.asarray(drawn.astype(out[name].dtype))
    for name, factor in factors.items():
        out[name] = (out[name] * factor).astype(out[name].dtype)
    return out
```

```python
import concourse.bass as bass
from concourse import mybir
from contextlib import ExitStack

F32 = mybir.dt.float32
BF16 = mybir.dt.bfloat16
I32 = mybir.dt.int32
U8 = mybir.dt.uint8
ALU = mybir.AluOpType
ACT = mybir.ActivationFunctionType
AX = mybir.AxisListType

P = 128
N = 6250
F = 256
E = 100000
EA = 64
NB = -(-N // P)
G = 2
SE = G * P
S = -(-((E + NB * (SE - 1)) // SE) // 4) * 4
EP = 125
EC = E // EP
RW = EA + 4
CH = 8
BIG = float(2 ** 100)
MMIN = -float(2 ** 99)
KEY_SHIFT = 7
STEP_SHIFT = 8
assert 1 << KEY_SHIFT == P and 1 << STEP_SHIFT == SE and EP * EC == E and EC % (2 * CH) == 0




def pipelined(e, n, stages, unroll, table=None):
    most = max(stage[0] for stage in stages)
    first = most + 4
    loops = (n - first) // unroll
    last = first + loops * unroll

    def turn(t, r, loaded=None):
        for lag, stage, *asks in stages:
            if isinstance(t, int) and not 0 <= t - lag < n:
                continue
            more = []
            if asks:
                more = [loaded[most + r_turn[0] - lag] if loaded else entry(e, table, t - lag)]
            stage(t - lag, ((r if loaded or not isinstance(t, int) else t) - lag) % unroll, *more)

    r_turn = [0]
    for t in range(first):
        turn(t, t % unroll)
    with e.Fori(0, loops) as k:
        loaded = None
        if table is not None:
            loaded = entries(e, table, k * unroll + (first - most), most + unroll)
        for u in range(unroll):
            r_turn[0] = u
            turn(k * unroll + (first + u), (first + u) % unroll, loaded)
    for t in range(last, n + most):
        turn(t, t % unroll)




def entry(e, table, i):
    return e.value_load(table[0:1, i:i + 1], min_val=0, max_val=NB - 1)




def entries(e, table, i, count):
    return e.bass.values_load_multi_w_load_instructions(
        table[0:1, bass.ds(i, count)], engines=[e.engine], min_val=0, max_val=NB - 1,
        skip_runtime_bounds_check_because="the sort clamps them")[1]




def phase_semaphores(nc, ctx, named):
    given = []

    def give(name):
        given.append(nc.alloc_semaphore(named(name)))
        return given[-1]

    def clear():
        with nc.Block() as block:
            @block.gpsimd
            def _(pool):
                for semaphore in given:
                    pool.sem_clear(semaphore)
        for semaphore in given:
            nc.release_semaphore(semaphore)

    ctx.callback(clear)
    return give


def step_aside(e, passed):
    e.sem_inc(passed, 1)


def late(i, k):
    return not isinstance(i, int) or i >= k




def landed(i, r, ring):
    return (i - r) * (16 // ring) + 16




def sort_phase(nc, d, keep):
    pos, gidx, local, rel, steps = keep["pos"], keep["gidx"], keep["local"], keep["rel"], keep["steps"]
    with ExitStack() as ctx:
        sb = lambda name, shape, dt: ctx.enter_context(nc.sbuf_tensor(name, shape, dt))
        sem = phase_semaphores(nc, ctx, lambda name: name)
        key_i = sb("key_i", [EP, 2, EC], I32)
        typ_i = sb("typ_i", [EP, EC], I32)
        blk_i = sb("blk_i", [EP, EC], I32)
        blk_f = sb("blk_f", [EP, EC], F32)
        eq = sb("eq", [EP, EC], U8)
        rank = sb("rank", [EP, EC], F32)
        pos_f = sb("pos_f", [EP, EC], F32)
        cnt = sb("cnt", [EP, NB], F32)
        offs = sb("offs", [EP, NB], F32)
        iota_i = sb("iota_i", [P, S], I32)
        iota_f = sb("iota_f", [P, S], F32)
        ones = sb("ones", [P, P], F32)
        below = sb("below", [P, P], F32)
        tot_i = sb("tot_i", [P, NB], I32)
        need = sb("need", [P, NB], F32)
        ends = sb("ends", [P, NB], F32)
        zero = sb("zero", [P, NB], F32)
        endT = sb("endT", [NB, 1], F32)
        past = sb("past", [NB, S], F32)
        blank = sb("blank", [P, 2, CH * RW], F32)
        ps_off = ctx.enter_context(nc.psum_tensor("ps_off", [P, 512], F32))
        ps_tot = ctx.enter_context(nc.psum_tensor("ps_tot", [P, 512], F32))
        ps_end = ctx.enter_context(nc.psum_tensor("ps_end", [P, 512], F32))
        ps_blk = ctx.enter_context(nc.psum_tensor("ps_blk", [P, 512], F32))
        edges_in = sem("sort_edges_in")
        consts = sem("sort_consts")
        iota_done = sem("sort_iota")
        blanked = sem("sort_blank")
        filled = sem("sort_filled")
        chain = sem("sort_chain")
        passed = sem("sort_passed")
        cnt_ready = sem("sort_cnt")
        off_ready = sem("sort_off")
        end_ready = sem("sort_end")
        endT_ready = sem("sort_endT")
        past_ready = sem("sort_past")
        blk_ready = sem("sort_blk")
        block = ctx.enter_context(nc.Block())

        @block.sync
        def _(sp):
            sp.dma_start(key_i[:, 0, :], d["dst"].rearrange("(p c) -> p c", p=EP)).then_inc(edges_in, 16)
            sp.dma_start(key_i[:, 1, :], d["src"].rearrange("(p c) -> p c", p=EP)).then_inc(edges_in, 16)
            sp.dma_start(typ_i[:], d["edge_type_64"].rearrange("(p c) -> p c", p=EP)).then_inc(edges_in, 16)
            sp.wait_ge(blanked, 3)
            rows = S * SE // P
            for k in range(2):
                sp.dma_start(
                    d["rec"][k].rearrange("(p a c) w -> p a (c w)", p=P, c=CH),
                    blank[:, k, :].unsqueeze(1).to_broadcast([P, rows // CH, CH * RW]),
                ).then_inc(filled, 16)
            sp.wait_ge(filled, 32)

        @block.gpsimd
        def _(pool):
            pool.iota(iota_i[:], pattern=[[1, S]], base=0, channel_multiplier=0).then_inc(iota_done, 1)
            pool.memset(below[:], 1.0).then_inc(consts, 1)
            pool.memset(ones[:], 1.0).then_inc(consts, 1)
            pool.wait_ge(consts, 2)
            pool.affine_select(out=below[:], in_=below[:], compare_op=ALU.is_gt, fill=0.0, base=0,
                               pattern=[[1, P]], channel_multiplier=-1).then_inc(consts, 1)
            pool.memset(blank[:], 0.0).then_inc(blanked, 1)
            pool.wait_ge(blanked, 1)
            for k, word in enumerate((1, EA + 1)):
                pool.memset(blank[:, k, :].rearrange("p (c w) -> p c w", c=CH)[:, :, word:word + 1], -1.0).then_inc(blanked, 1)

        @block.tensor
        def _(pe):
            pe.wait_ge(consts, 3)
            for k in range(2):
                pe.wait_ge(cnt_ready, k + 1)
                nc.tensor.matmul(ps_off[0:EP, 0:NB], below[0:EP, 0:EP], cnt[:], start=True, stop=True).then_inc(off_ready, 1)
                nc.tensor.matmul(ps_tot[:, 0:NB], ones[0:EP, :], cnt[:], start=True, stop=True).then_inc(off_ready, 1)
                pe.wait_ge(end_ready, k + 1)
                nc.tensor.matmul(ps_end[0:NB, 0:1], ends[0:1, :], ones[0:1, 0:1], start=True, stop=True).then_inc(endT_ready, 1)
                pe.wait_ge(past_ready, k + 1)
                nc.tensor.matmul(ps_blk[:, 0:S], ones[0:NB, :], past[:], start=True, stop=True).then_inc(blk_ready, 1)

        @block.vector
        def _(dve):
            n = [0]

            def link(ins):
                n[0] += 1
                ins.then_inc(chain, 1)
                dve.wait_ge(chain, n[0])

            v = nc.vector
            dve.wait_ge(iota_done, 1)
            link(v.tensor_copy(iota_f[:], iota_i[:]))
            link(v.memset(zero[:], 0.0))
            dve.wait_ge(edges_in, 48)
            link(v.tensor_copy(rel[:], typ_i[:]))
            for k in range(2):
                other = 1 - k
                link(v.tensor_copy(gidx[:, k, :], key_i[:, other, :]))
                link(v.tensor_scalar(blk_i[:], key_i[:, k, :], P - 1, None, ALU.bitwise_and))
                link(v.tensor_copy(local[:, k, :], blk_i[:]))
                link(v.tensor_scalar(blk_i[:], key_i[:, k, :], KEY_SHIFT, None, ALU.logical_shift_right))
                link(v.tensor_copy(blk_f[:], blk_i[:]))
                start = n[0]
                with dve.Fori(0, NB) as b:
                    v.tensor_tensor(eq[:], blk_f[:], iota_f[0:EP, bass.ds(b, 1)].to_broadcast([EP, EC]),
                                    ALU.is_equal).then_inc(chain, 1)
                    dve.wait_ge(chain, b * 2 + (start + 1))
                    v.tensor_reduce(cnt[:, bass.ds(b, 1)], eq[:], AX.X, ALU.add).then_inc(chain, 1)
                    dve.wait_ge(chain, b * 2 + (start + 2))
                n[0] += 2 * NB
                v.engine_nop().then_inc(cnt_ready, 1)
                dve.wait_ge(off_ready, 2 * k + 2)
                link(v.tensor_copy(tot_i[:], ps_tot[:, 0:NB]))
                link(v.tensor_scalar(tot_i[:], tot_i[:], SE - 1, None, ALU.add))
                link(v.tensor_scalar(tot_i[:], tot_i[:], STEP_SHIFT, None, ALU.logical_shift_right))
                link(v.tensor_copy(need[:], tot_i[:]))
                link(v.tensor_tensor_scan(ends[:], need[:], zero[:], 0.0, ALU.add, ALU.add))
                v.engine_nop().then_inc(end_ready, 1)
                link(v.tensor_tensor(need[:], ends[:], need[:], ALU.subtract))
                link(v.tensor_scalar(need[:], need[:], float(SE), -1.0, ALU.mult, ALU.add))
                link(v.tensor_tensor(offs[:], ps_off[0:EP, 0:NB], need[0:EP, :], ALU.add))
                start = n[0]
                with dve.Fori(0, NB) as b:
                    v.tensor_tensor(eq[:], blk_f[:], iota_f[0:EP, bass.ds(b, 1)].to_broadcast([EP, EC]),
                                    ALU.is_equal).then_inc(chain, 1)
                    dve.wait_ge(chain, b * 3 + (start + 1))
                    v.tensor_tensor_scan(rank[:], eq[:], blk_f[:], offs[:, bass.ds(b, 1)],
                                         ALU.add, ALU.bypass).then_inc(chain, 1)
                    dve.wait_ge(chain, b * 3 + (start + 2))
                    step_aside(dve, passed)
                    v.copy_predicated(pos_f[:], eq[:], rank[:]).then_inc(chain, 1)
                    dve.wait_ge(chain, b * 3 + (start + 3))
                n[0] += 3 * NB
                link(v.tensor_copy(pos[:, k, :], pos_f[:]))
                dve.wait_ge(endT_ready, k + 1)
                link(v.tensor_copy(endT[:], ps_end[0:NB, 0:1]))
                v.tensor_scalar(past[:], iota_f[0:NB, :], endT[:], None, ALU.is_ge).then_inc(past_ready, 1)
                dve.wait_ge(blk_ready, k + 1)
                link(v.tensor_scalar(steps[0:1, k, :], ps_blk[0:1, 0:S], float(NB - 1), None, ALU.min))




def scatter_phase(nc, d, keep):
    pos, gidx, local, rel = keep["pos"], keep["gidx"], keep["local"], keep["rel"]
    attr = d["edge_attr_64"].rearrange("(p c) w -> p c w", p=EP)
    with ExitStack() as ctx:
        sem = phase_semaphores(nc, ctx, lambda name: name)
        row = ctx.enter_context(nc.sbuf_tensor("sc_row", [EP, 2, CH, RW + 4], F32))
        idx = ctx.enter_context(nc.sbuf_tensor("sc_idx", [EP, 2, 2, CH], I32))
        attr_in = [sem(f"sc_attr{r}") for r in range(2)]
        sent = keep["scatter_dma"]
        zeroed = sem("sc_zeroed")
        meta_done = sem("sc_meta")
        passed = sem("sc_passed")
        per_chunk = 7
        block = ctx.enter_context(nc.Block())

        def free(e, c, r):
            if late(c, 2):
                e.wait_ge(sent[r], (c - r) * (16 * CH))

        @block.sync
        def _(sp):
            def load(c, r):
                free(sp, c, r)
                sp.dma_start(row[:, r, :, 4:4 + EA], attr[:, bass.ds(c * CH, CH), :]).then_inc(attr_in[r], 16)
            pipelined(sp, EC // CH, [(0, load)], 2)

        @block.vector
        def _(dve):
            v = nc.vector
            v.memset(row[:, :, :, 0:4], 0.0).then_inc(zeroed, 1)
            v.memset(row[:, :, :, 4 + EA:8 + EA], 0.0).then_inc(zeroed, 1)
            dve.wait_ge(zeroed, 2)

            def meta(c, r):
                free(dve, c, r)
                cols = bass.ds(c * CH, CH)
                one = lambda w: row[:, r, :, w:w + 1].rearrange("p c o -> p (c o)")
                v.tensor_copy(one(0).bitcast(I32), gidx[:, 0, cols]).then_inc(meta_done, 1)
                v.tensor_copy(one(1), local[:, 0, cols]).then_inc(meta_done, 1)
                v.tensor_copy(one(2), rel[:, cols]).then_inc(meta_done, 1)
                v.tensor_copy(one(4 + EA).bitcast(I32), gidx[:, 1, cols]).then_inc(meta_done, 1)
                v.tensor_copy(one(5 + EA), local[:, 1, cols]).then_inc(meta_done, 1)
                for k in range(2):
                    v.tensor_copy(idx[:, r, k, :], pos[:, k, cols]).then_inc(meta_done, 1)
            pipelined(dve, EC // CH, [(0, meta)], 2)

        @block.gpsimd
        def _(pool):
            def send(c, r):
                pool.wait_ge(attr_in[r], landed(c, r, 2))
                pool.wait_ge(meta_done, c * per_chunk + per_chunk)
                step_aside(pool, passed)
                for j in range(CH):
                    for k in range(2):
                        pool.indirect_dma_start(
                            d["rec"][k], bass.IndirectOffsetOnAxis(ap=idx[:, r, k, j:j + 1], axis=0),
                            row[:, r, j, 4 * k:4 * k + RW], None).then_inc(sent[r], 16)
            pipelined(pool, EC // CH, [(0, send)], 2)
            for r in range(2):
                pool.wait_ge(sent[r], EC // CH // 2 * 2 * CH * 16)


def edge_phase(nc, d, keep, name, order, heads, kind):
    C = F // heads
    attention = kind != "conv"
    attrs = kind != "gat"
    width = {"edge": 2 * F, "rel": 2 * F, "gat": F + heads, "conv": F}[kind]
    v0 = F if kind in ("edge", "rel") else 0
    meta, ao = ((0, 4), (EA, 0))[order]
    acc_w = heads * (C + 1) if attention else F
    q_scale = float(C) ** -0.5
    steps = keep["steps"][:, order, :]
    acc, q, mx = keep["acc"], keep["q"], keep["mx"]
    iota, ident, ident_b = keep["iota"], keep["ident"], keep["ident_b"]
    rec_d = d["rec"][order].rearrange("(s p g) w -> s p g w", p=P, g=G)
    R = 4
    with ExitStack() as ctx:
        sb = lambda n, shape, dt: ctx.enter_context(nc.sbuf_tensor(f"{name}_{n}", shape, dt))
        psum = lambda n, dt=F32: ctx.enter_context(
            nc.psum_tensor(f"{name}_{n}", [P, 512 if dt is F32 else 1024], dt))
        sem = phase_semaphores(nc, ctx, lambda n: f"{name}_{n}")
        rec = sb("rec", [P, R, G, RW], F32)
        kv = sb("kv", [P, R, G, width], F32)
        oh = sb("oh", [P, R, G, P], F32)
        oht = sb("oht", [P, R, SE], F32)
        mask = sb("mask", [P, R, SE], BF16)
        attrT = sb("attrT", [EA, 2, SE], F32)
        e_sb = sb("e_sb", [P, 2, G, F], F32)
        prod = sb("prod", [P, G, F], F32)
        alpha = sb("alpha", [P, 2, G, heads], F32)
        split = sb("split", [P, 2, G, 2 * heads], BF16)
        aT = sb("aT", [2 * heads, 2, SE], BF16)
        sel = sb("sel", [2 * heads, heads, P], BF16)
        tmax = sb("tmax", [P, 2, heads], F32)
        mnew = sb("mnew", [P, 2, heads], F32)
        mdiff = sb("mdiff", [P, 2, heads], F32)
        scale = sb("scale", [P, R, heads], F32)
        down = sb("down", [P, 2, G, heads], F32)
        pv = sb("pv", [P, 2, G, acc_w], F32)
        w_e = sb("w_e", [EA, F], F32)
        bank_t, bank_q, bank_e, bank_o, bank_x = (psum(n) for n in ("ps_t", "ps_q", "ps_e", "ps_o", "ps_x"))
        bank_m = [psum(f"ps_m{i}") for i in range(2)]
        bank_a = psum("ps_a", BF16)
        passed, pe_passed = sem("passed"), sem("pe_passed")
        we_in, we_scaled, sel_done = sem("we_in"), sem("we_scaled"), sem("sel_done")
        rec_in = [sem(f"rec_in{r}") for r in range(R)]
        kv_in = keep["pool_dma"]
        before = keep["edge_phases"] * (S // R) * 16 * G
        keep["edge_phases"] += 1
        gathered = lambda i, r: (i - r) * (16 * G // R) + (16 * G + before)
        oh_ready, rel_ready = sem("oh_ready"), sem("rel_ready")
        turned, oht_ready = sem("turned"), sem("oht_ready")
        q_ready, e_ready, e_copied, kv_ready = sem("q_ready"), sem("e_ready"), sem("e_copied"), sem("kv_ready")
        multiplied, alpha_ready, hi_ready, split_ready = sem("multiplied"), sem("alpha_ready"), sem("hi_ready"), sem("split_ready")
        aT_turned, aT_ready = sem("aT_turned"), sem("aT_ready")
        m_filled, m_read = sem("m_filled"), sem("m_read")
        mnew_ready, mdiff_ready, mx_kept = sem("mnew_ready"), sem("mdiff_ready"), sem("mx_kept")
        mexp_ready, down_ready, scale_ready, p_ready = sem("mexp_ready"), sem("down_ready"), sem("scale_ready"), sem("p_ready")
        pv_ready, out_ready, acc_scaled, acc_done = sem("pv_ready"), sem("out_ready"), sem("acc_scaled"), sem("acc_done")
        by_head = lambda ap: ap.rearrange("p g (h c) -> p g h c", h=heads)
        pv_view = lambda i2: by_head(pv[:, i2])
        banks = heads // 2
        block = ctx.enter_context(nc.Block())

        @block.sync
        def _(sp):
            if attrs:
                if kind == "rel":
                    sp.dma_start(w_e[:].rearrange("k (h c) -> k h c", h=heads), d["L1_gnn_rel_w"].unsqueeze(1).to_broadcast([EA, heads, C])).then_inc(we_in, 16)
                else:
                    sp.dma_start(w_e[:], d["L0_gnn_We" if kind == "edge" else "L3_gnn_G"]).then_inc(we_in, 16)

            def load(i, r):
                if late(i, R):
                    sp.wait_ge(oh_ready, i - (R - 1))
                    if attrs:
                        sp.wait_ge(turned, i - (R - 1))
                    sp.wait_ge(kv_in[r], gathered(i, r) - 16 * G)
                if kind in ("rel", "gat"):
                    sp.dma_start(rec[:, r, :, meta:meta + 4], rec_d[bass.ds(i, 1), :, :, meta:meta + 4].rearrange("s p g w -> (s p) g w")).then_inc(rec_in[r], 16)
                else:
                    sp.dma_start(rec[:, r], rec_d[bass.ds(i, 1)].rearrange("s p g w -> (s p) g w")).then_inc(rec_in[r], 16)
            pipelined(sp, S, [(0, load)], R)

        @block.gpsimd
        def _(pool):
            if attention:
                pool.memset(sel[:], 0.0).then_inc(sel_done, 1)
                for k in range(2):
                    pool.wait_ge(sel_done, k + 1)
                    pool.affine_select(out=sel[:], in_=sel[:], compare_op=ALU.not_equal, fill=1.0,
                                       base=-heads * k, pattern=[[-1, heads], [0, P]],
                                       channel_multiplier=1).then_inc(sel_done, 1)

            def gather(i, r):
                pool.wait_ge(rec_in[r], landed(i, r, R))
                if late(i, R):
                    pool.wait_ge(pv_ready, i - (R - 1))
                step_aside(pool, passed)
                for g in range(G):
                    pool.indirect_dma_start(
                        kv[:, r, g, :], None, d[f"{name}_table"],
                        bass.IndirectOffsetOnAxis(ap=rec[:, r, g, meta:meta + 1].bitcast(I32), axis=0),
                    ).then_inc(kv_in[r], 16)

            def add_edge(i, r):
                pool.wait_ge(e_copied, i + 1)
                pool.wait_ge(kv_in[r], gathered(i, r))
                if kind == "edge":
                    both = kv[:, r].rearrange("p g (k f) -> p g k f", k=2)
                    nc.gpsimd.tensor_tensor(both, both, e_sb[:, r % 2].unsqueeze(2).to_broadcast([P, G, 2, F]), ALU.add).then_inc(kv_ready, 1)
                else:
                    nc.gpsimd.tensor_tensor(kv[:, r, :, 0:F], kv[:, r, :, 0:F], e_sb[:, r % 2], ALU.add).then_inc(kv_ready, 1)
            pipelined(pool, S, [(0, gather)] + [(1, add_edge)] * (kind in ("edge", "rel")), R)

        @block.scalar
        def _(act):
            a = nc.scalar

            def copy_turned(i, r):
                act.wait_ge(turned, i + 1)
                if late(i, R) and attention:
                    act.wait_ge(mexp_ready, i - (R - 1))
                if attention:
                    a.copy(oht[:, r, :], bank_t[:, 0:SE])
                    last = a.activation(mask[:, r, :], bank_t[:, 0:SE], ACT.Copy, bias=-BIG, scale=BIG)
                if attrs:
                    if late(i, 2):
                        act.wait_ge(e_ready, i - 1)
                    last = a.copy(attrT[:, r % 2, :], bank_t[0:EA, SE:2 * SE])
                last.then_inc(oht_ready, 1)

            def copy_e(i, r):
                act.wait_ge(e_ready, i + 1)
                if late(i, 2):
                    act.wait_ge(kv_ready, i - 1)
                a.copy(e_sb[:, r % 2].rearrange("p g f -> p (g f)"), bank_e[:]).then_inc(e_copied, 1)

            def rescale(i, r):
                act.wait_ge(mdiff_ready, i + 1)
                if late(i, R):
                    act.wait_ge(acc_scaled, i - (R - 1))
                a.activation(scale[:, r, :], mdiff[:, r % 2, :], ACT.Exp).then_inc(scale_ready, 1)

            def weights(i, r):
                act.wait_ge(down_ready, i + 1)
                if late(i, 2):
                    act.wait_ge(out_ready, i - 1)
                a.activation(pv_view(r % 2)[:, :, :, C:C + 1].rearrange("p g h o -> p g (h o)"), down[:, r % 2], ACT.Exp).then_inc(p_ready, 1)

            def copy_aT(i, r):
                act.wait_ge(aT_turned, i + 1)
                if late(i, 2):
                    act.wait_ge(m_filled, (i - 1) * banks)
                a.copy(aT[:, r % 2, :], bank_a[0:2 * heads, 0:SE]).then_inc(aT_ready, 1)

            stages = [(0, copy_turned)]
            if attention:
                stages += [(2, rescale)] + [(0, copy_e)] * (kind != "gat") + [(2, weights), (1, copy_aT)]
            pipelined(act, S, stages, R)

        @block.tensor
        def _(pe):
            t = nc.tensor
            if attrs:
                pe.wait_ge(we_scaled, 1)
            if attention:
                pe.wait_ge(sel_done, 3)

            def fill_max(i, r):
                pe.wait_ge(aT_ready, i + 1)
                for b in range(banks):
                    if late(i, 1) or b >= 2:
                        pe.wait_ge(m_read, i * banks + (b - 1))
                    bank = bank_m[b % 2]
                    t.matmul(bank[:].rearrange("p (h e) -> p h e", h=2), ident_b[:],
                             mask[:, r, :].unsqueeze(1).to_broadcast([P, 2, SE]), start=True, stop=False)
                    for h in range(2):
                        last = t.matmul(bank[:, h * SE:(h + 1) * SE], sel[:, 2 * b + h, :], aT[:, r % 2, :],
                                        start=False, stop=h == 1)
                    last.then_inc(m_filled, 1)

            def turn_edges(i, r):
                pe.wait_ge(oh_ready, i + 1)
                if attrs:
                    pe.wait_ge(rel_ready if kind == "rel" else rec_in[r], i + 1 if kind == "rel" else landed(i, r, R))
                if late(i, 1):
                    pe.wait_ge(oht_ready, i)
                if not attention:
                    step_aside(pe, pe_passed)
                for g in range(G):
                    if attention:
                        last = t.transpose(bank_t[:, g * P:(g + 1) * P], oh[:, r, g, :], ident[:])
                    if attrs:
                        last = t.transpose(bank_t[0:EA, SE + g * P:SE + (g + 1) * P], rec[:, r, g, ao:ao + EA], ident[:])
                last.then_inc(turned, 1)

            def sum_nodes(i, r):
                pe.wait_ge(pv_ready, i + 1)
                if late(i, 1):
                    pe.wait_ge(acc_done, i)
                for g in range(G):
                    last = t.matmul(bank_o[:, 0:acc_w], oh[:, r, g, :], pv[:, r % 2, g, :], start=g == 0, stop=g == G - 1)
                last.then_inc(out_ready, 1)

            def spread_max(i, r):
                pe.wait_ge(mnew_ready, i + 1)
                if late(i, 1):
                    pe.wait_ge(down_ready, i)
                for g in range(G):
                    last = t.matmul(bank_x[:, g * heads:(g + 1) * heads], oht[:, r, g * P:(g + 1) * P],
                                    mnew[:, r % 2, :], start=True, stop=True)
                last.then_inc(mexp_ready, 1)

            def products(i, r, *b):
                pe.wait_ge(oht_ready, i + 1)
                if attrs:
                    if late(i, 1):
                        pe.wait_ge(pv_ready if kind == "conv" else e_copied, i)
                    for g in range(G):
                        last = t.matmul(bank_e[:, g * F:(g + 1) * F], attrT[:, r % 2, g * P:(g + 1) * P], w_e[:],
                                        start=True, stop=True)
                    last.then_inc(e_ready, 1)
                if attention:
                    if late(i, 1):
                        pe.wait_ge(multiplied, i)
                    w = F if kind != "gat" else heads
                    for g in range(G):
                        last = t.matmul(bank_q[:, g * w:(g + 1) * w], oht[:, r, g * P:(g + 1) * P],
                                        q[:, bass.ds(b[0], 1), 0:w].rearrange("p o f -> p (o f)"), start=True, stop=True)
                    last.then_inc(q_ready, 1)

            def turn_scores(i, r):
                pe.wait_ge(split_ready, i + 1)
                if late(i, 1):
                    pe.wait_ge(aT_ready, i)
                for g in range(G):
                    last = t.transpose(bank_a[0:2 * heads, g * P:(g + 1) * P], split[:, r % 2, g, :], ident_b[:])
                last.then_inc(aT_turned, 1)

            if attention:
                pipelined(pe, S, [(2, fill_max), (0, turn_edges), (3, sum_nodes), (2, spread_max),
                                  (0, products, True), (1, turn_scores)], R, steps)
            else:
                pipelined(pe, S, [(0, turn_edges), (0, products), (1, sum_nodes)], R)

        @block.vector
        def _(dve):
            v = nc.vector
            if attrs:
                dve.wait_ge(we_in, 16)
                v.tensor_scalar(w_e[:], w_e[:], 0.2 if kind == "rel" else 1.0, None, ALU.mult).then_inc(we_scaled, 1)

            def select(i, r):
                dve.wait_ge(rec_in[r], landed(i, r, R))
                if late(i, R):
                    dve.wait_ge(out_ready, i - (R - 1))
                    if kind == "rel":
                        dve.wait_ge(turned, i - (R - 1))
                v.tensor_tensor(oh[:, r], iota[:, 0:P].unsqueeze(1).to_broadcast([P, G, P]),
                                rec[:, r, :, meta + 1:meta + 2].to_broadcast([P, G, P]), ALU.is_equal).then_inc(oh_ready, 1)
                if kind == "rel":
                    v.tensor_tensor(rec[:, r, :, ao:ao + EA], iota[:, 0:EA].unsqueeze(1).to_broadcast([P, G, EA]),
                                    rec[:, r, :, meta + 2:meta + 3].to_broadcast([P, G, EA]), ALU.is_equal).then_inc(rel_ready, 1)

            def weigh(i, r):
                dve.wait_ge(p_ready, i + 1)
                if kind == "gat":
                    pass
                v.tensor_tensor(pv_view(r % 2)[:, :, :, 0:C], by_head(kv[:, r, :, v0:v0 + F]),
                                pv_view(r % 2)[:, :, :, C:C + 1].to_broadcast([P, G, heads, C]), ALU.mult).then_inc(pv_ready, 1)

            def multiply(i, r):
                dve.wait_ge(e_ready, i + 1)
                dve.wait_ge(kv_in[r], gathered(i, r))
                if late(i, 2):
                    dve.wait_ge(out_ready, i - 1)
                v.tensor_tensor(pv[:, r % 2], kv[:, r], bank_e[:].rearrange("p (g f) -> p g f", g=G), ALU.mult).then_inc(pv_ready, 1)

            def accumulate(i, r, b):
                dve.wait_ge(out_ready, i + 1)
                mine = acc[:, bass.ds(b, 1), 0:acc_w]
                if attention:
                    mine = mine.rearrange("p o (h c) -> p (o h) c", h=heads)
                    dve.wait_ge(scale_ready, i + 1)
                    if late(i, 1):
                        dve.wait_ge(acc_done, i)
                    v.tensor_tensor(mine, mine, scale[:, r, :].unsqueeze(2).to_broadcast([P, heads, C + 1]), ALU.mult).then_inc(acc_scaled, 1)
                    dve.wait_ge(acc_scaled, i + 1)
                    v.tensor_tensor(mine, mine, bank_o[:, 0:acc_w].rearrange("p (h c) -> p h c", h=heads), ALU.add).then_inc(acc_done, 1)
                else:
                    if late(i, 1):
                        dve.wait_ge(acc_done, i)
                    mine = mine.rearrange("p o f -> p (o f)")
                    v.tensor_tensor(mine, mine, bank_o[:, 0:acc_w], ALU.add).then_inc(acc_done, 1)

            def maximum(i, r, b):
                for k in range(banks):
                    dve.wait_ge(m_filled, i * banks + (k + 1))
                    if k == 0 and late(i, 2):
                        dve.wait_ge(mnew_ready, i - 1)
                    v.tensor_reduce(tmax[:, r % 2, 2 * k:2 * k + 2], bank_m[k % 2][:].rearrange("p (h e) -> p h e", h=2),
                                    AX.X, ALU.max).then_inc(m_read, 1)
                dve.wait_ge(m_read, (i + 1) * banks)
                old = mx[:, bass.ds(b, 1), 0:heads].rearrange("p o h -> p (o h)")
                if late(i, 1):
                    dve.wait_ge(mx_kept, i)
                if late(i, 2):
                    dve.wait_ge(mexp_ready, i - 1)
                    dve.wait_ge(scale_ready, i - 1)
                v.tensor_tensor(mnew[:, r % 2, :], old, tmax[:, r % 2, :], ALU.max).then_inc(mnew_ready, 1)
                dve.wait_ge(mnew_ready, i + 1)
                v.tensor_tensor(mdiff[:, r % 2, :], old, mnew[:, r % 2, :], ALU.subtract).then_inc(mdiff_ready, 1)
                dve.wait_ge(mdiff_ready, i + 1)
                v.tensor_tensor(old, mnew[:, r % 2, :], mnew[:, r % 2, :], ALU.max).then_inc(mx_kept, 1)

            def score(i, r):
                dve.wait_ge(q_ready, i + 1)
                if late(i, 1):
                    dve.wait_ge(alpha_ready, i)
                if late(i, 2):
                    dve.wait_ge(down_ready, i - 1)
                if kind == "gat":
                    dve.wait_ge(kv_in[r], gathered(i, r))
                    part = prod[:, :, 0:heads]
                    v.tensor_tensor(part, kv[:, r, :, F:F + heads], bank_q[:, 0:G * heads].rearrange("p (g h) -> p g h", g=G),
                                    ALU.add).then_inc(multiplied, 1)
                    dve.wait_ge(multiplied, i + 1)
                    v.scalar_tensor_tensor(out=alpha[:, r % 2], in0=part, scalar=0.2, in1=part, op0=ALU.mult, op1=ALU.max).then_inc(alpha_ready, 1)
                else:
                    dve.wait_ge(kv_ready, i + 1)
                    v.scalar_tensor_tensor(out=prod[:], in0=bank_q[:].rearrange("p (g f) -> p g f", g=G), scalar=q_scale,
                                           in1=kv[:, r, :, 0:F], op0=ALU.mult, op1=ALU.mult).then_inc(multiplied, 1)
                    dve.wait_ge(multiplied, i + 1)
                    v.tensor_reduce(alpha[:, r % 2].rearrange("p g h -> p (g h)"),
                                    prod[:].rearrange("p g (h c) -> p (g h) c", h=heads), AX.X, ALU.add).then_inc(alpha_ready, 1)

            def split_scores(i, r):
                dve.wait_ge(alpha_ready, i + 1)
                if late(i, 2):
                    dve.wait_ge(aT_turned, i - 1)
                v.tensor_copy(split[:, r % 2, :, 0:heads], alpha[:, r % 2]).then_inc(hi_ready, 1)
                dve.wait_ge(hi_ready, i + 1)
                v.tensor_tensor(split[:, r % 2, :, heads:2 * heads], alpha[:, r % 2], split[:, r % 2, :, 0:heads], ALU.subtract).then_inc(split_ready, 1)

            def lower(i, r):
                dve.wait_ge(mexp_ready, i + 1)
                if late(i, 2):
                    dve.wait_ge(p_ready, i - 1)
                v.tensor_tensor(down[:, r % 2], alpha[:, r % 2], bank_x[:, 0:G * heads].rearrange("p (g h) -> p g h", g=G),
                                ALU.subtract).then_inc(down_ready, 1)

            if attention:
                pipelined(dve, S, [(0, select), (3, weigh), (4, accumulate, True), (2, maximum, True), (2, lower),
                                   (1, score), (1, split_scores)], R, steps)
            else:
                pipelined(dve, S, [(0, select), (1, multiply), (2, accumulate, True)], R, steps)


def node_phase(nc, d, keep, layer):
    acc, q, mx, ident = keep["acc"], keep["q"], keep["mx"], keep["ident"]
    adds = layer in (1, 3)
    heads_before, heads = (0, 8, 4, 4)[layer], (8, 4, 4, 1)[layer]
    x_in, x_out = d["xs"][layer], d["xs_updated"][layer]
    weights = ([("L0_gnn_Wq", "L0_gnn_bq"), ("L0_gnn_Wskip", "L0_gnn_bskip"), ("L0_gnn_Wk", "L0_gnn_bk"), ("L0_gnn_Wv", "L0_gnn_bv")],
               [("L1_gnn_Wq", "L1_gnn_bq"), ("L1_gnn_Wk", "L1_gnn_bk"), ("L1_gnn_Wv", "L1_gnn_bv")],
               [("L2_gnn_W", None)],
               [("L3_gnn_Wi", "L3_gnn_bi"), ("L3_gnn_Wj", "L3_gnn_bj")])[layer]
    first_bank = (2, 1, 1, 2)[layer]
    W = len(weights)
    width = (2 * F, 2 * F, F + 4, F)[layer]
    K = F // P
    R = 4
    name = f"n{layer}"
    with ExitStack() as ctx:
        sb = lambda n, shape, dt=F32: ctx.enter_context(nc.sbuf_tensor(f"{name}_{n}", shape, dt))
        sem = phase_semaphores(nc, ctx, lambda n: f"{name}_{n}")
        psum = lambda n: ctx.enter_context(nc.psum_tensor(f"{name}_{n}", [P, 512], F32))
        w = sb("w", [P, W, K, F])
        bias = sb("bias", [P, W, F])
        extra = sb("extra", [P, 2, F])
        x = sb("x", [P, R, F])
        stats = sb("stats", [P, 2, 6])
        mean = sb("mean", [P, 2, 2])
        rstd = sb("rstd", [P, 2, 1])
        inv = sb("inv", [P, 2, 8])
        part = sb("part", [P, 2, F])
        hn = sb("hn", [P, 2, F])
        h = sb("h", [P, R, F])
        h2 = sb("h2", [P, 2, F])
        expd = sb("expd", [P, 2, F])
        hT = sb("hT", [P, 2, K, P])
        row = sb("row", [P, R, width])
        made = sb("made", [P, 2, 2 * F])
        made2 = sb("made2", [P, 2, 2 * F])
        same = sb("same", [P, F], I32)
        xi = sb("xi", [P, R, F])
        bank_t = psum("ps_t")
        banks = [[psum(f"ps_{b}{r}") for r in range(2)] for b in range(2)]
        eps_added, passed, pool_passed = sem("eps_added"), sem("passed"), sem("pool_passed")
        w_in, extra_ready = sem("w_in"), sem("extra_ready")
        x_in_sem = [sem(f"x_in{r}") for r in range(R)]
        x_sent = [sem(f"x_sent{r}") for r in range(R)]
        xi_sent = [sem(f"xi_sent{r}") for r in range(R)]
        h_sent = [sem(f"h_sent{r}") for r in range(R)]
        row_sent = [sem(f"row_sent{r}") for r in range(R)]
        s_ready, inv_ready, part_ready, x_ready = sem("s_ready"), sem("inv_ready"), sem("part_ready"), sem("x_ready")
        cleared, stats_ready, mean_ready, rstd_ready = sem("cleared"), sem("stats_ready"), sem("mean_ready"), sem("rstd_ready")
        hn_ready, h_ready, h2_ready, exp_ready, ln_ready = sem("hn_ready"), sem("h_ready"), sem("h2_ready"), sem("exp_ready"), sem("ln_ready")
        turned, hT_ready, product_ready = sem("turned"), sem("hT_ready"), sem("product_ready")
        evacuated, row_ready, chain = sem("evacuated"), sem("row_ready"), sem("chain")
        if layer in (0, 1):
            row_ready = evacuated
        abs_ready, made_exp, made_ln = sem("abs_ready"), sem("made_exp"), sem("made_ln")
        block = ctx.enter_context(nc.Block())
        rows = lambda t, i: t[bass.ds(i * P, P), :]
        operand_ready = h2_ready if layer in (1, 3) else h_ready

        @block.sync
        def _(sp):
            for n, (wn, bn) in enumerate(weights):
                sp.dma_start(w[:, n], d[wn].rearrange("(k p) f -> p k f", p=P)).then_inc(w_in, 16)
                if bn:
                    sp.dma_start(bias[:, n], d[bn].partition_broadcast(P)).then_inc(w_in, 16)
            if layer == 1:
                sp.dma_start(extra[:, 0], d["L1_gnn_query_emb"].partition_broadcast(P)).then_inc(w_in, 16)
            if layer == 2:
                for n, an in enumerate(("L2_gnn_a_l", "L2_gnn_a_r")):
                    sp.dma_start(extra[:, n], d[an].rearrange("o h c -> (o h c)").partition_broadcast(P)).then_inc(w_in, 16)

            def load(i, r):
                if late(i, R):
                    sp.wait_ge(hn_ready, i - (R - 1))
                    if x_out is not None:
                        sp.wait_ge(x_sent[r], (i - r) * (16 // R))
                sp.dma_start(x[:, r], rows(x_in, i)).then_inc(x_in_sem[r], 16)
            pipelined(sp, NB, [(0, load)], R)

        loads = 16 * (sum(1 + bool(bn) for _, bn in weights) + (0, 1, 2, 0)[layer])

        @block.gpsimd
        def _(pool):
            def clear(i, r):
                if adds:
                    pool.wait_ge(part_ready, i + 1)
                if layer != 2:
                    nc.gpsimd.tensor_copy(acc[:, bass.ds(i, 1), :], keep["zeros"][:].unsqueeze(1))
                nc.gpsimd.tensor_copy(mx[:, bass.ds(i, 1), :], keep["lowest"][:].unsqueeze(1)).then_inc(cleared, 1)

            def inverse_deviation(i, r):
                pool.wait_ge(mean_ready, i + 1)
                step_aside(pool, pool_passed)
                nc.gpsimd.tensor_scalar(rstd[:, r % 2], mean[:, r % 2, 1:2], 1e-5, None, ALU.add).then_inc(eps_added, 1)
                pool.wait_ge(eps_added, i + 1)
                nc.gpsimd.tensor_tensor(rstd[:, r % 2], rstd[:, r % 2], keep["minus_half"][:], ALU.pow).then_inc(rstd_ready, 1)

            pipelined(pool, NB, [(0, inverse_deviation), (0, clear)], R)

        @block.tensor
        def _(pe):
            t = nc.tensor
            pe.wait_ge(w_in, loads)

            def turn(i, r):
                pe.wait_ge(operand_ready, i + 1)
                if late(i, 1):
                    pe.wait_ge(hT_ready, i)
                src = h2[:, r % 2] if layer in (1, 3) else h[:, r]
                for k in range(K):
                    last = t.transpose(bank_t[:, k * P:(k + 1) * P], src[:, k * P:(k + 1) * P], ident[:])
                last.then_inc(turned, 1)

            def multiply(i, r):
                pe.wait_ge(hT_ready, i + 1)
                if late(i, 2):
                    pe.wait_ge(evacuated, i - 1)
                for n in range(W):
                    bank = banks[n >= first_bank][r % 2]
                    c = n - first_bank * (n >= first_bank)
                    for k in range(K):
                        last = t.matmul(bank[:, c * F:(c + 1) * F], hT[:, r % 2, k, :], w[:, n, k, :],
                                        start=k == 0, stop=k == K - 1)
                last.then_inc(product_ready, 1)
            pipelined(pe, NB, [(0, turn), (1, multiply)], R)

        @block.scalar
        def _(act):
            a = nc.scalar

            def relu(i, r):
                act.wait_ge(hn_ready, i + 1)
                if late(i, R):
                    act.wait_ge(turned, i - (R - 1))
                    if layer == 1:
                        act.wait_ge(h_sent[r], (i - r) * (16 // R))
                a.activation(h[:, r], hn[:, r % 2], ACT.Relu).then_inc(h_ready, 1)
                if layer == 3:
                    if late(i, 2):
                        act.wait_ge(h2_ready, i - 1)
                    act.wait_ge(h_ready, i + 1)
                    a.activation(expd[:, r % 2], h[:, r], ACT.Exp, scale=-1.0).then_inc(exp_ready, 1)
                    act.wait_ge(exp_ready, i + 1)
                    a.activation(expd[:, r % 2], expd[:, r % 2], ACT.Ln, bias=1.0).then_inc(ln_ready, 1)

            def copy_hT(i, r):
                act.wait_ge(turned, i + 1)
                if late(i, 2):
                    act.wait_ge(product_ready, i - 1)
                a.copy(hT[:, r % 2].rearrange("p k n -> p (k n)"), bank_t[:, 0:F]).then_inc(hT_ready, 1)

            def soften(i, r):
                act.wait_ge(evacuated, i + 1)
                if late(i, 2):
                    act.wait_ge(row_ready, i - 1)
                a.activation(made2[:, r % 2], made[:, r % 2], ACT.Abs).then_inc(abs_ready, 1)
                act.wait_ge(abs_ready, i + 1)
                a.activation(made2[:, r % 2], made2[:, r % 2], ACT.Exp, scale=-1.0).then_inc(made_exp, 1)
                act.wait_ge(made_exp, i + 1)
                a.activation(made2[:, r % 2], made2[:, r % 2], ACT.Ln, bias=1.0).then_inc(made_ln, 1)

            def send(i, r):
                act.wait_ge(row_ready, i + 1)
                act.dma_start(rows(d[f"L{layer}_table"], i), row[:, r]).then_inc(row_sent[r], 16)
                if layer != 2:
                    act.dma_start(rows(x_out, i), x[:, r]).then_inc(x_sent[r], 16)
                if layer == 1:
                    act.dma_start(rows(d["h1"], i), h[:, r]).then_inc(h_sent[r], 16)
                if layer == 3:
                    act.dma_start(rows(d["xi"], i), xi[:, r]).then_inc(xi_sent[r], 16)
            pipelined(act, NB, [(0, relu), (0, copy_hT)] + [(2, soften)] * (layer == 3) + [(3, send)], R)
            for r in range(R):
                blocks = len(range(r, NB, R))
                act.wait_ge(row_sent[r], 16 * blocks)
                if layer != 2:
                    act.wait_ge(x_sent[r], 16 * blocks)
                if layer == 1:
                    act.wait_ge(h_sent[r], 16 * blocks)
                if layer == 3:
                    act.wait_ge(xi_sent[r], 16 * blocks)

        @block.vector
        def _(dve):
            v = nc.vector
            dve.wait_ge(w_in, loads)
            if layer == 1:
                v.tensor_scalar(extra[:, 0], extra[:, 0], 0.1, None, ALU.mult).then_inc(extra_ready, 1)
                dve.wait_ge(extra_ready, 1)

            def normalise(i, r):
                dve.wait_ge(x_in_sem[r], landed(i, r, R))
                xr, two = x[:, r], r % 2
                if adds:
                    H = heads_before
                    C = F // H
                    mine = acc[:, bass.ds(i, 1), 0:H * (C + 1)].rearrange("p o (h c) -> p (o h) c", h=H)
                    v.tensor_scalar(inv[:, two, 0:H].unsqueeze(2), mine[:, :, C:C + 1], 1e-16, None, ALU.add).then_inc(s_ready, 1)
                    dve.wait_ge(s_ready, i + 1)
                    v.reciprocal(inv[:, two, 0:H], inv[:, two, 0:H]).then_inc(inv_ready, 1)
                    dve.wait_ge(inv_ready, i + 1)
                    v.tensor_tensor(part[:, two].rearrange("p (h c) -> p h c", h=H), mine[:, :, 0:C],
                                    inv[:, two, 0:H].unsqueeze(2).to_broadcast([P, H, C]), ALU.mult).then_inc(part_ready, 1)
                    dve.wait_ge(part_ready, i + 1)
                    v.tensor_tensor(xr, xr, part[:, two], ALU.add).then_inc(x_ready, 1)
                    dve.wait_ge(x_ready, i + 1)
                v.bn_stats(stats[:, two], xr).then_inc(stats_ready, 1)
                dve.wait_ge(stats_ready, i + 1)
                step_aside(dve, passed)
                v.bn_aggr(mean[:, two], stats[:, two]).then_inc(mean_ready, 1)
                dve.wait_ge(mean_ready, i + 1)
                dve.wait_ge(rstd_ready, i + 1)
                if late(i, 2):
                    dve.wait_ge(h_ready, i - 1)
                v.tensor_scalar(hn[:, two], xr, mean[:, two, 0:1], rstd[:, two], ALU.subtract, ALU.mult).then_inc(hn_ready, 1)

            def operand(i, r):
                dve.wait_ge(ln_ready if layer == 3 else h_ready, i + 1)
                if late(i, 2):
                    dve.wait_ge(turned, i - 1)
                if layer == 1:
                    v.tensor_tensor(h2[:, r % 2], h[:, r], extra[:, 0], ALU.add).then_inc(h2_ready, 1)
                else:
                    v.scalar_tensor_tensor(out=h2[:, r % 2], in0=h[:, r], scalar=-0.6931471805599453, in1=expd[:, r % 2],
                                           op0=ALU.add, op1=ALU.add).then_inc(h2_ready, 1)

            def make(i, r):
                dve.wait_ge(product_ready, i + 1)
                if late(i, R):
                    dve.wait_ge(row_sent[r], (i - r) * (16 // R))
                b0, b1 = banks[0][r % 2], banks[1][r % 2]
                mine = q[:, bass.ds(i, 1), :].rearrange("p o f -> p (o f)")
                if layer in (0, 1):
                    v.tensor_tensor(mine, b0[:, 0:F], bias[:, 0], ALU.add)
                    if layer == 0:
                        v.tensor_tensor(made[:, r % 2, 0:F], b0[:, F:2 * F], bias[:, 1], ALU.add).then_inc(chain, 1)
                        dve.wait_ge(chain, i + 1)
                        v.tensor_tensor(x[:, r], x[:, r], made[:, r % 2, 0:F], ALU.add)
                    v.tensor_tensor(row[:, r], b1[:], bias[:, W - 2:W].rearrange("p a f -> p (a f)"), ALU.add).then_inc(evacuated, 1)
                if layer == 2:
                    hm, one = made[:, 0, 0:F], made[:, 1, 0:F]
                    if late(i, 1):
                        dve.wait_ge(row_ready, i)
                    v.memset(hm, 0.0).then_inc(chain, 1)
                    v.tensor_copy(one, b0[:, 0:F]).then_inc(chain, 1)
                    dve.wait_ge(chain, i * 5 + 2)
                    v.tensor_tensor(same[:], one, one, ALU.is_equal).then_inc(chain, 1)
                    dve.wait_ge(chain, i * 5 + 3)
                    step_aside(dve, passed)
                    v.copy_predicated(hm, same[:], one).then_inc(evacuated, 1)
                    dve.wait_ge(evacuated, i + 1)
                    v.tensor_copy(row[:, r, 0:F], hm)
                    for n in range(2):
                        out = (mine[:, 0:4], row[:, r, F:F + 4])[n]
                        v.tensor_tensor(made2[:, n, 0:F], hm, extra[:, n], ALU.mult).then_inc(chain, 1)
                        dve.wait_ge(chain, i * 5 + (4 + n))
                        last = v.tensor_reduce(out, made2[:, n, 0:F].rearrange("p (h c) -> p h c", h=4), AX.X, ALU.add)
                    last.then_inc(row_ready, 1)
                if layer == 3:
                    if late(i, 2):
                        dve.wait_ge(row_ready, i - 1)
                    v.tensor_tensor(made[:, r % 2], b0[:], bias[:].rearrange("p a f -> p (a f)"), ALU.add).then_inc(evacuated, 1)

            def finish(i, r):
                dve.wait_ge(made_ln, i + 1)
                if late(i, R):
                    dve.wait_ge(xi_sent[r], (i - r) * (16 // R))
                v.scalar_tensor_tensor(out=xi[:, r], in0=made[:, r % 2, 0:F], scalar=0.0, in1=made2[:, r % 2, 0:F], op0=ALU.max, op1=ALU.add)
                v.scalar_tensor_tensor(out=row[:, r], in0=made[:, r % 2, F:2 * F], scalar=0.0, in1=made2[:, r % 2, F:2 * F],
                                       op0=ALU.max, op1=ALU.add).then_inc(row_ready, 1)

            pipelined(dve, NB, [(0, normalise), (2, make)] + [(0, operand)] * (layer in (1, 3))
                      + [(3, finish)] * (layer == 3), R)


def relational_out_phase(nc, d, keep):
    acc, ident = keep["acc"], keep["ident"]
    H, K, R = 4, F // P, 4
    C = F // H
    with ExitStack() as ctx:
        sb = lambda n, shape, dt=F32: ctx.enter_context(nc.sbuf_tensor(f"o1_{n}", shape, dt))
        sem = phase_semaphores(nc, ctx, lambda n: f"o1_{n}")
        psum = lambda n: ctx.enter_context(nc.psum_tensor(f"o1_{n}", [P, 512], F32))
        w = sb("w", [P, K, F])
        vec = sb("vec", [P, 3, F])
        value, h, x = (sb(n, [P, R, F]) for n in ("value", "h", "x"))
        none = sb("none", [P, 2, H])
        inv = sb("inv", [P, 2, H])
        msg, own, y = (sb(n, [P, 2, F]) for n in ("msg", "own", "y"))
        msgT = sb("msgT", [P, 2, K, P])
        stats = sb("stats", [P, 2, 6])
        mean = sb("mean", [P, 2, 2])
        rstd = sb("rstd", [P, 2, 1])
        bank_t = psum("ps_t")
        bank_y = [psum(f"ps_y{r}") for r in range(2)]
        w_in = sem("w_in")
        tiles_in = [sem(f"tiles_in{r}") for r in range(R)]
        sent = [sem(f"sent{r}") for r in range(R)]
        head, msg_ready, turned, msgT_ready, product_ready = (sem(n) for n in ("head", "msg_ready", "turned", "msgT_ready", "product_ready"))
        eps_added, passed, pool_passed = sem("eps_added"), sem("passed"), sem("pool_passed")
        tail, x_ready, cleared = sem("tail"), sem("x_ready"), sem("cleared")
        block = ctx.enter_context(nc.Block())
        rows = lambda t, i: t[bass.ds(i * P, P), :]

        @block.sync
        def _(sp):
            sp.dma_start(w[:], d["L1_gnn_Wo"].rearrange("(k p) f -> p k f", p=P)).then_inc(w_in, 16)
            for n, name in enumerate(("L1_gnn_bo", "L1_gnn_gamma", "L1_gnn_beta")):
                sp.dma_start(vec[:, n], d[name].partition_broadcast(P)).then_inc(w_in, 16)

            def load(i, r):
                if late(i, R):
                    sp.wait_ge(sent[r], (i - r) * (16 // R))
                sp.dma_start(value[:, r], rows(d["L1_table"], i)[:, F:2 * F]).then_inc(tiles_in[r], 16)
                sp.dma_start(h[:, r], rows(d["h1"], i)).then_inc(tiles_in[r], 16)
                sp.dma_start(x[:, r], rows(d["xs"][2], i)).then_inc(tiles_in[r], 16)
            pipelined(sp, NB, [(0, load)], R)

        @block.gpsimd
        def _(pool):
            def clear(i, r):
                pool.wait_ge(msg_ready, i + 1)
                nc.gpsimd.tensor_copy(acc[:, bass.ds(i, 1), :], keep["zeros"][:].unsqueeze(1)).then_inc(cleared, 1)

            def inverse_deviation(i, r):
                pool.wait_ge(tail, i * 8 + 4)
                step_aside(pool, pool_passed)
                nc.gpsimd.tensor_scalar(rstd[:, r % 2], mean[:, r % 2, 1:2], 1e-5, None, ALU.add).then_inc(eps_added, 1)
                pool.wait_ge(eps_added, i + 1)
                nc.gpsimd.tensor_tensor(rstd[:, r % 2], rstd[:, r % 2], keep["minus_half"][:], ALU.pow).then_inc(tail, 1)
            pipelined(pool, NB, [(0, clear), (2, inverse_deviation)], R)

        @block.tensor
        def _(pe):
            t = nc.tensor
            pe.wait_ge(w_in, 64)

            def turn(i, r):
                pe.wait_ge(msg_ready, i + 1)
                if late(i, 1):
                    pe.wait_ge(msgT_ready, i)
                for k in range(K):
                    last = t.transpose(bank_t[:, k * P:(k + 1) * P], msg[:, r % 2, k * P:(k + 1) * P], ident[:])
                last.then_inc(turned, 1)

            def multiply(i, r):
                pe.wait_ge(msgT_ready, i + 1)
                if late(i, 2):
                    pe.wait_ge(x_ready, i - 1)
                for k in range(K):
                    last = t.matmul(bank_y[r % 2][:, 0:F], msgT[:, r % 2, k, :], w[:, k, :], start=k == 0, stop=k == K - 1)
                last.then_inc(product_ready, 1)
            pipelined(pe, NB, [(0, turn), (1, multiply)], R)

        @block.scalar
        def _(act):
            def copy_msgT(i, r):
                act.wait_ge(turned, i + 1)
                if late(i, 2):
                    act.wait_ge(product_ready, i - 1)
                nc.scalar.copy(msgT[:, r % 2].rearrange("p k n -> p (k n)"), bank_t[:, 0:F]).then_inc(msgT_ready, 1)

            def send(i, r):
                act.wait_ge(x_ready, i + 1)
                act.dma_start(rows(d["xs"][2], i), x[:, r]).then_inc(sent[r], 16)
            pipelined(act, NB, [(0, copy_msgT), (2, send)], R)
            for r in range(R):
                act.wait_ge(sent[r], 16 * len(range(r, NB, R)))

        @block.vector
        def _(dve):
            v = nc.vector
            dve.wait_ge(w_in, 64)

            def message(i, r):
                dve.wait_ge(tiles_in[r], (i - r) * (48 // R) + 48)
                two = r % 2
                mine = acc[:, bass.ds(i, 1), 0:H * (C + 1)].rearrange("p o (h c) -> p (o h) c", h=H)
                by_head = lambda ap: ap.rearrange("p (h c) -> p h c", h=H)
                wide = lambda ap: ap.unsqueeze(2).to_broadcast([P, H, C])
                v.tensor_scalar(none[:, two].unsqueeze(2), mine[:, :, C:C + 1], 0.0, None, ALU.is_equal).then_inc(head, 1)
                dve.wait_ge(head, i * 5 + 1)
                v.tensor_tensor(inv[:, two].unsqueeze(2), mine[:, :, C:C + 1], none[:, two].unsqueeze(2), ALU.add).then_inc(head, 1)
                dve.wait_ge(head, i * 5 + 2)
                v.reciprocal(inv[:, two], inv[:, two]).then_inc(head, 1)
                dve.wait_ge(head, i * 5 + 3)
                if late(i, 2):
                    dve.wait_ge(turned, i - 1)
                v.tensor_tensor(by_head(msg[:, two]), mine[:, :, 0:C], wide(inv[:, two]), ALU.mult).then_inc(head, 1)
                v.tensor_tensor(by_head(own[:, two]), by_head(value[:, r]), wide(none[:, two]), ALU.mult).then_inc(head, 1)
                dve.wait_ge(head, i * 5 + 5)
                v.tensor_tensor(msg[:, two], msg[:, two], own[:, two], ALU.add).then_inc(msg_ready, 1)

            def finish(i, r):
                two = r % 2
                n = [0]

                def link(ins):
                    n[0] += 1
                    ins.then_inc(tail, 1)
                    dve.wait_ge(tail, i * 8 + n[0])

                dve.wait_ge(product_ready, i + 1)
                link(v.tensor_tensor(y[:, two], bank_y[two][:, 0:F], h[:, r], ALU.add))
                link(v.tensor_tensor(y[:, two], y[:, two], vec[:, 0], ALU.add))
                link(v.bn_stats(stats[:, two], y[:, two]))
                step_aside(dve, passed)
                link(v.bn_aggr(mean[:, two], stats[:, two]))
                n[0] += 1
                dve.wait_ge(tail, i * 8 + n[0])
                link(v.tensor_scalar(y[:, two], y[:, two], mean[:, two, 0:1], rstd[:, two], ALU.subtract, ALU.mult))
                link(v.tensor_tensor(y[:, two], y[:, two], vec[:, 1], ALU.mult))
                link(v.tensor_tensor(y[:, two], y[:, two], vec[:, 2], ALU.add))
                v.tensor_tensor(x[:, r], x[:, r], y[:, two], ALU.add).then_inc(x_ready, 1)
            pipelined(dve, NB, [(0, message), (2, finish)], R)




def atom_out_phase(nc, d, keep):
    acc, ident = keep["acc"], keep["ident"]
    T = 7
    BATCHES, COLS, K, HALF = NB // T, T * P, F // P, T * P // 2
    LAYERS = 3
    with ExitStack() as ctx:
        sb = lambda n, shape, dt=F32: ctx.enter_context(nc.sbuf_tensor(f"o3_{n}", shape, dt))
        sem = phase_semaphores(nc, ctx, lambda n: f"o3_{n}")
        w1, w2 = sb("w1", [P, LAYERS, K, F]), sb("w2", [P, LAYERS, K, F])
        wv = sb("wv", [P, K, F])
        b1, b2 = sb("b1", [P, LAYERS, K]), sb("b2", [P, LAYERS, K])
        bv = sb("bv", [P, F])
        xi, x = sb("xi", [P, T, F]), sb("x", [P, T, F])
        v_rows = sb("v_rows", [P, T, F])
        vT, hT, logT = (sb(n, [P, K, COLS]) for n in ("vT", "hT", "logT"))
        y = sb("y", [P, T, F])
        bank = [[ctx.enter_context(nc.psum_tensor(f"o3_ps{s}{c}", [P, 512], F32)) for c in range(K)] for s in range(2)]
        bank_t = [ctx.enter_context(nc.psum_tensor(f"o3_pt{s}", [P, 512], F32)) for s in range(2)]
        bank_y = [ctx.enter_context(nc.psum_tensor(f"o3_py{s}", [P, 512], F32)) for s in range(2)]
        w_in, tiles_in, sent = sem("w_in"), sem("tiles_in"), sem("sent")
        rows_ready, turned, vT_ready = sem("rows_ready"), sem("turned"), sem("vT_ready")
        up_ready = [sem(f"up_ready{s}") for s in range(2)]
        abs_ready = [sem(f"abs_ready{s}") for s in range(2)]
        exp_ready = [sem(f"exp_ready{s}") for s in range(2)]
        log_ready = [sem(f"log_ready{s}") for s in range(2)]
        max_ready = [sem(f"max_ready{s}") for s in range(2)]
        h_ready = [sem(f"h_ready{s}") for s in range(2)]
        down_ready = [sem(f"down_ready{s}") for s in range(2)]
        v_ready = [sem(f"v_ready{s}") for s in range(2)]
        y_ready, y_biased, y_done = sem("y_ready"), sem("y_biased"), sem("y_done")
        block = ctx.enter_context(nc.Block())
        half = lambda s: slice(s * HALF, (s + 1) * HALF)
        SP_N = LAYERS + 1

        @block.sync
        def _(sp):
            for n in range(LAYERS):
                for w, name in ((w1, "L3_gnn_res_w1"), (w2, "L3_gnn_res_w2")):
                    sp.dma_start(w[:, n], d[name][n].rearrange("(k p) f -> p k f", p=P)).then_inc(w_in, 16)
                for b, name in ((b1, "L3_gnn_res_b1"), (b2, "L3_gnn_res_b2")):
                    for k in range(K):
                        sp.dma_start(b[:, n, k:k + 1], d[name][n:n + 1, k * P:(k + 1) * P].rearrange("o p -> p o")).then_inc(w_in, 16)
            sp.dma_start(wv[:], d["L3_gnn_Wv"].rearrange("(k p) f -> p k f", p=P)).then_inc(w_in, 16)
            sp.dma_start(bv[:], d["L3_gnn_bv"].partition_broadcast(P)).then_inc(w_in, 16)

            def send(i):
                sp.wait_ge(y_done, i * T + T)
                sp.dma_start(d["out"][bass.ds(i * COLS, COLS), :].rearrange("(t p) f -> p t f", p=P), y[:]).then_inc(sent, 16)

            def batch(i):
                if i is not None:
                    send(i)
                m = 0 if i is None else i + 1
                for t, src in ((xi, d["xi"]), (x, d["x3"])):
                    sp.dma_start(t[:], src[bass.ds(m * COLS, COLS), :].rearrange("(t p) f -> p t f", p=P)).then_inc(tiles_in, 16)
            batch(None)
            with sp.Fori(0, BATCHES - 1) as i:
                batch(i)
            send(BATCHES - 1)
            sp.wait_ge(sent, 16 * BATCHES)

        weights = 16 * (6 * LAYERS + 2)

        @block.tensor
        def _(pe):
            t = nc.tensor
            pe.wait_ge(w_in, weights)

            def batch(i):
                for j in range(T):
                    pe.wait_ge(rows_ready, i + 1)
                    if late(i, 1) or j >= 2:
                        pe.wait_ge(vT_ready, i * T + (j - 1))
                    for k in range(K):
                        last = t.transpose(bank_t[j % 2][:, k * P:(k + 1) * P], v_rows[:, j, k * P:(k + 1) * P], ident[:])
                    last.then_inc(turned, 1)

                def product(s, w, n, src, done):
                    for c in range(K):
                        for k in range(K):
                            last = t.matmul(bank[s][c][:, 0:HALF], w[:, n, k, c * P:(c + 1) * P], src[:, k, half(s)],
                                            start=k == 0, stop=k == K - 1)
                    last.then_inc(done, 1)

                for n in range(LAYERS):
                    for s in range(2):
                        if n == 0:
                            pe.wait_ge(vT_ready, (i + 1) * T)
                        else:
                            pe.wait_ge(v_ready[s], i * LAYERS + n)
                        product(s, w1, n, vT, up_ready[s])
                    for s in range(2):
                        pe.wait_ge(h_ready[s], i * SP_N + (n + 1))
                        product(s, w2, n, hT, down_ready[s])
                for s in range(2):
                    pe.wait_ge(h_ready[s], (i + 1) * SP_N)
                for j in range(T):
                    if late(i, 1) or j >= 2:
                        pe.wait_ge(y_biased, i * T + (j - 1))
                    for k in range(K):
                        last = t.matmul(bank_y[j % 2][:, 0:F], hT[:, k, j * P:(j + 1) * P], wv[:, k, :], start=k == 0, stop=k == K - 1)
                    last.then_inc(y_ready, 1)
            batch(0)
            with pe.Fori(1, BATCHES) as i:
                batch(i)

        @block.scalar
        def _(act):
            a = nc.scalar
            act.wait_ge(w_in, weights)

            def batch(i):
                for n in range(SP_N):
                    for s in range(2):
                        m = i * SP_N + (n + 1)
                        if n < LAYERS:
                            act.wait_ge(up_ready[s], i * LAYERS + (n + 1))
                            for c in range(K):
                                last = a.activation(logT[:, c, half(s)], bank[s][c][:, 0:HALF], ACT.Abs, bias=b1[:, n, c:c + 1])
                        else:
                            act.wait_ge(v_ready[s], (i + 1) * LAYERS)
                            last = a.activation(logT[:, :, half(s)], vT[:, :, half(s)], ACT.Abs)
                        last.then_inc(abs_ready[s], 1)
                        act.wait_ge(abs_ready[s], m)
                        a.activation(logT[:, :, half(s)], logT[:, :, half(s)], ACT.Exp, scale=-1.0).then_inc(exp_ready[s], 1)
                        act.wait_ge(exp_ready[s], m)
                        a.activation(logT[:, :, half(s)], logT[:, :, half(s)], ACT.Ln, bias=1.0).then_inc(log_ready[s], 1)
            with act.Fori(0, BATCHES) as i:
                batch(i)

        @block.vector
        def _(dve):
            v = nc.vector
            dve.wait_ge(w_in, weights)

            def batch(i):
                dve.wait_ge(tiles_in, i * 32 + 32)
                v.tensor_tensor(v_rows[:], xi[:], acc[:, bass.ds(i * T, T), 0:F], ALU.add).then_inc(rows_ready, 1)
                for j in range(T):
                    dve.wait_ge(turned, i * T + (j + 1))
                    v.tensor_copy(vT[:, :, j * P:(j + 1) * P], bank_t[j % 2][:, 0:F].rearrange("p (k n) -> p k n", k=K)).then_inc(vT_ready, 1)
                for n in range(SP_N):
                    for s in range(2):
                        m = i * SP_N + (n + 1)
                        dve.wait_ge(log_ready[s], m)
                        if n < LAYERS:
                            for c in range(K):
                                last = v.tensor_scalar(hT[:, c, half(s)], bank[s][c][:, 0:HALF], b1[:, n, c:c + 1], 0.0, ALU.add, ALU.max)
                            last.then_inc(max_ready[s], 1)
                            dve.wait_ge(max_ready[s], i * LAYERS + (n + 1))
                            v.tensor_tensor(hT[:, :, half(s)], hT[:, :, half(s)], logT[:, :, half(s)], ALU.add).then_inc(h_ready[s], 1)
                        else:
                            v.scalar_tensor_tensor(out=hT[:, :, half(s)], in0=vT[:, :, half(s)], scalar=0.0, in1=logT[:, :, half(s)],
                                                   op0=ALU.max, op1=ALU.add).then_inc(h_ready[s], 1)
                    if n < LAYERS:
                        for s in range(2):
                            dve.wait_ge(down_ready[s], i * LAYERS + (n + 1))
                            for c in range(K):
                                last = v.scalar_tensor_tensor(out=vT[:, c, half(s)], in0=bank[s][c][:, 0:HALF], scalar=b2[:, n, c:c + 1],
                                                              in1=vT[:, c, half(s)], op0=ALU.add, op1=ALU.add)
                            last.then_inc(v_ready[s], 1)
                for j in range(T):
                    dve.wait_ge(y_ready, i * T + (j + 1))
                    if late(i, 1):
                        dve.wait_ge(sent, i * 16)
                    v.tensor_tensor(y[:, j], bank_y[j % 2][:, 0:F], bv[:], ALU.add).then_inc(y_biased, 1)
                    dve.wait_ge(y_biased, i * T + (j + 1))
                    v.tensor_tensor(y[:, j], y[:, j], x[:, j], ALU.add).then_inc(y_done, 1)
            batch(0)
            with dve.Fori(1, BATCHES) as i:
                batch(i)


def consts_phase(nc, keep):
    ident, ident_b, iota = keep["ident"], keep["ident_b"], keep["iota"]
    with ExitStack() as ctx:
        sem = phase_semaphores(nc, ctx, lambda n: f"c_{n}")
        iota_i = ctx.enter_context(nc.sbuf_tensor("c_iota_i", [P, P], I32))
        zeroed, set_, made, copied = sem("zeroed"), sem("set"), sem("made"), sem("copied")
        block = ctx.enter_context(nc.Block())

        @block.gpsimd
        def _(pool):
            pool.iota(iota_i[:], pattern=[[1, P]], base=0, channel_multiplier=0).then_inc(made, 1)
            pool.memset(keep["zeros"][:], 0.0).then_inc(made, 1)
            pool.memset(keep["minus_half"][:], -0.5).then_inc(made, 1)
            pool.memset(keep["lowest"][:], MMIN).then_inc(made, 1)
            pool.memset(ident[:], 0.0).then_inc(zeroed, 1)
            pool.wait_ge(zeroed, 1)
            pool.affine_select(out=ident[:], in_=ident[:], compare_op=ALU.not_equal, fill=1.0, base=0,
                               pattern=[[-1, P]], channel_multiplier=1).then_inc(set_, 1)

        @block.vector
        def _(dve):
            dve.wait_ge(made, 1)
            nc.vector.tensor_copy(iota[:], iota_i[:]).then_inc(copied, 1)
            dve.wait_ge(set_, 1)
            nc.vector.tensor_copy(ident_b[:], ident[:]).then_inc(copied, 1)




def gnn_program(nc, d, out):
    dram = lambda name, cols, rows=NB * P: nc.dram_tensor(name, (rows, cols), F32, kind="Internal").ap()
    d["rec"] = [dram(f"rec{k}", RW, S * SE) for k in range(2)]
    for name, width in (("L0", 2 * F), ("L1", 2 * F), ("L2", F + 4), ("L3", F)):
        d[f"{name}_table"] = dram(f"{name}_table", width)
    x1, x2, d["x3"], d["h1"], d["xi"] = (dram(n, F) for n in ("x1", "x2", "x3", "h1", "xi"))
    d["xs"] = [d["x"], x1, x2, x2]
    d["xs_updated"] = [x1, x2, None, d["x3"]]
    d["out"] = out
    with ExitStack() as ctx:
        sb = lambda name, shape, dt=F32: ctx.enter_context(nc.sbuf_tensor(name, shape, dt))
        keep = {"steps": sb("steps", [1, 2, S], I32), "ident": sb("ident", [P, P]), "ident_b": sb("ident_b", [P, P], BF16),
                "iota": sb("iota", [P, P]), "zeros": sb("zeros", [P, 264]), "lowest": sb("lowest", [P, 8]),
                "minus_half": sb("minus_half", [P, 1])}
        keep["scatter_dma"] = [ctx.enter_context(nc.semaphore(f"scatter_dma{r}")) for r in range(2)]
        keep["pool_dma"] = [ctx.enter_context(nc.semaphore(f"pool_dma{r}")) for r in range(4)]
        keep["edge_phases"] = 0
        with ExitStack() as inner:
            sbi = lambda name, shape, dt=F32: inner.enter_context(nc.sbuf_tensor(name, shape, dt))
            keep |= {"pos": sbi("pos", [EP, 2, EC], I32), "gidx": sbi("gidx", [EP, 2, EC], I32),
                     "local": sbi("local", [EP, 2, EC]), "rel": sbi("rel", [EP, EC])}
            consts_phase(nc, keep)
            sort_phase(nc, d, keep)
            scatter_phase(nc, d, keep)
        keep |= {"q": sb("q", [P, NB, F]), "acc": sb("acc", [P, NB, 264]), "mx": sb("mx", [P, NB, 8])}
        phases = [
            lambda: node_phase(nc, d, keep, 0),
            lambda: edge_phase(nc, d, keep, "L0", 0, 8, "edge"),
            lambda: node_phase(nc, d, keep, 1),
            lambda: edge_phase(nc, d, keep, "L1", 0, 4, "rel"),
            lambda: relational_out_phase(nc, d, keep),
            lambda: node_phase(nc, d, keep, 2),
            lambda: edge_phase(nc, d, keep, "L2", 1, 4, "gat"),
            lambda: node_phase(nc, d, keep, 3),
            lambda: edge_phase(nc, d, keep, "L3", 1, 1, "conv"),
            lambda: atom_out_phase(nc, d, keep),
        ]
        for phase in phases:
            phase()


TRANSPOSED = ("L0_gnn_Wq", "L0_gnn_Wk", "L0_gnn_Wv", "L0_gnn_We", "L0_gnn_Wskip", "L3_gnn_G", "L3_gnn_Wi",
              "L3_gnn_Wj", "L3_gnn_res_w1", "L3_gnn_res_w2", "L3_gnn_Wv")




def kernel(**inputs):
    import numpy as np
    import concourse.bacc as bacc
    from concourse.bass_utils import run_bass_kernel_spmd

    nc = bacc.Bacc("TRN2", target_bir_lowering=False, num_devices=1)
    arrays, args = {}, {}
    for name, value in inputs.items():
        a = np.asarray(value)
        if name in TRANSPOSED:
            a = np.swapaxes(a, -1, -2)
        if name == "x":
            a = np.concatenate([a, np.zeros((NB * P - N, F), a.dtype)])
        a = np.ascontiguousarray(a)
        arrays[f"in_{name}"] = a
        args[name] = nc.dram_tensor(f"in_{name}", a.shape, mybir.dt.from_np(a.dtype), kind="ExternalInput").ap()
    out = nc.dram_tensor("out_x", (NB * P, F), F32, kind="ExternalOutput").ap()
    gnn_program(nc, args, out)
    result = run_bass_kernel_spmd(nc, [arrays], core_ids=[0])
    return result.results[0]["out_x"][:N]
```

```python
import concourse.bass as bass
from concourse import mybir
from contextlib import ExitStack

F32 = mybir.dt.float32
BF16 = mybir.dt.bfloat16
I32 = mybir.dt.int32
U8 = mybir.dt.uint8
ALU = mybir.AluOpType
ACT = mybir.ActivationFunctionType
AX = mybir.AxisListType

P = 128
N = 6250
F = 256
E = 100000
EA = 64
NB = -(-N // P)
G = 2
SE = G * P
S = -(-((E + NB * (SE - 1)) // SE) // 4) * 4
EP = 125
EC = E // EP
RW = EA + 4
CH = 8
BIG = float(2 ** 100)
MMIN = -float(2 ** 99)
KEY_SHIFT = 7
STEP_SHIFT = 8
assert 1 << KEY_SHIFT == P and 1 << STEP_SHIFT == SE and EP * EC == E and EC % (2 * CH) == 0 and S <= EC <= 2 * S




def pipelined(e, n, stages, unroll, table=None):
    most = max(stage[0] for stage in stages)
    asked = [stage[0] for stage in stages if stage[2:]]
    first = most + unroll
    loops = (n - first) // unroll
    last = first + loops * unroll

    def turn(t, r, loaded=None):
        for lag, stage, *asks in stages:
            if isinstance(t, int) and not 0 <= t - lag < n:
                continue
            more = [loaded(lag) if loaded else entry(e, table, t - lag)] if asks else []
            stage(t - lag, (r - lag) % unroll, *more)

    for t in range(first):
        turn(t, t % unroll)
    with e.Fori(0, loops) as k:
        values = None
        if asked:
            values = entries(e, table, k * unroll + (first - max(asked)), unroll + max(asked) - min(asked))
        for u in range(unroll):
            turn(k * unroll + (first + u), (first + u) % unroll,
                 values and (lambda lag: values[u + max(asked) - lag]))
    for t in range(last, n + most):
        turn(t, t % unroll)


def entry(e, table, i):
    return e.value_load(table[0:1, i:i + 1], min_val=0, max_val=NB - 1)




def entries(e, table, i, count):
    return e.bass.values_load_multi_w_load_instructions(
        table[0:1, bass.ds(i, count)], engines=[e.engine], min_val=0, max_val=NB - 1,
        skip_runtime_bounds_check_because="the sort clamps them")[1]




def phase_semaphores(nc, ctx, named):
    given = []

    def give(name):
        given.append(nc.alloc_semaphore(named(name)))
        return given[-1]

    def clear():
        with nc.Block() as block:
            @block.gpsimd
            def _(pool):
                for semaphore in given:
                    pool.sem_clear(semaphore)
        for semaphore in given:
            nc.release_semaphore(semaphore)

    ctx.callback(clear)
    return give


def step_aside(e, passed):
    e.sem_inc(passed, 1)


def late(i, k):
    return not isinstance(i, int) or i >= k




def landed(i, r, ring):
    return (i - r) * (16 // ring) + 16




def sort_phase(nc, d, keep):
    pos, gidx, local, rel, steps = keep["pos"], keep["gidx"], keep["local"], keep["rel"], keep["steps"]
    with ExitStack() as ctx:
        sb = lambda name, shape, dt: ctx.enter_context(nc.sbuf_tensor(name, shape, dt))
        sem = phase_semaphores(nc, ctx, lambda name: name)
        key_i = sb("key_i", [EP, 2, EC], I32)
        typ_i = sb("typ_i", [EP, EC], I32)
        blk_i = sb("blk_i", [EP, EC], I32)
        blk_f = sb("blk_f", [EP, EC], F32)
        eq = sb("eq", [EP, EC], U8)
        rank = sb("rank", [EP, EC], F32)
        pos_f = sb("pos_f", [EP, EC], F32)
        cnt = sb("cnt", [EP, NB], F32)
        offs = sb("offs", [EP, NB], F32)
        iota_i = sb("iota_i", [P, S], I32)
        iota_f = sb("iota_f", [P, S], F32)
        ones = sb("ones", [P, P], F32)
        below = sb("below", [P, P], F32)
        tot_i = sb("tot_i", [P, NB], I32)
        need = sb("need", [P, NB], F32)
        ends = sb("ends", [P, NB], F32)
        zero = sb("zero", [P, NB], F32)
        endT = sb("endT", [NB, 1], F32)
        past = sb("past", [NB, S], F32)
        blank = sb("blank", [P, 2, CH * RW], F32)
        ps_off = ctx.enter_context(nc.psum_tensor("ps_off", [P, 512], F32))
        ps_tot = ctx.enter_context(nc.psum_tensor("ps_tot", [P, 512], F32))
        ps_end = ctx.enter_context(nc.psum_tensor("ps_end", [P, 512], F32))
        ps_blk = ctx.enter_context(nc.psum_tensor("ps_blk", [P, 512], F32))
        edges_in = sem("sort_edges_in")
        consts = sem("sort_consts")
        iota_done = sem("sort_iota")
        blanked = sem("sort_blank")
        filled = sem("sort_filled")
        chain = sem("sort_chain")
        passed = sem("sort_passed")
        row = sb("sc_row", [EP, 2, CH, RW], F32)
        idx = sb("sc_idx", [EP, 2, CH], I32)
        late_meta = sb("late_meta", [EP, EC, 5], F32)
        attr = d["edge_attr_64"].rearrange("(p c) w -> p c w", p=EP)
        attr_in = [sem(f"sc_attr{r}") for r in range(2)]
        sent = keep["scatter_dma"]
        zeroed, meta_done, scatter_passed = sem("sc_zeroed"), sem("sc_meta"), sem("sc_passed")
        late_ready, late_sent = sem("late_ready"), sem("late_sent")
        cnt_ready = sem("sort_cnt")
        off_ready = sem("sort_off")
        end_ready = sem("sort_end")
        endT_ready = sem("sort_endT")
        past_ready = sem("sort_past")
        blk_ready = sem("sort_blk")
        def order_products(pe, k):
            pe.wait_ge(cnt_ready, k + 1)
            nc.tensor.matmul(ps_off[0:EP, 0:NB], below[0:EP, 0:EP], cnt[:], start=True, stop=True).then_inc(off_ready, 1)
            nc.tensor.matmul(ps_tot[:, 0:NB], ones[0:EP, :], cnt[:], start=True, stop=True).then_inc(off_ready, 1)
            pe.wait_ge(end_ready, k + 1)
            nc.tensor.matmul(ps_end[0:NB, 0:1], ends[0:1, :], ones[0:1, 0:1], start=True, stop=True).then_inc(endT_ready, 1)
            pe.wait_ge(past_ready, k + 1)
            nc.tensor.matmul(ps_blk[:, 0:S], ones[0:NB, :], past[:], start=True, stop=True).then_inc(blk_ready, 1)

        links = [0]

        def link(dve, ins):
            links[0] += 1
            ins.then_inc(chain, 1)
            dve.wait_ge(chain, links[0])

        def order(dve, k):
            v = nc.vector
            other = 1 - k
            link(dve, v.tensor_copy(gidx[:, k, :], key_i[:, other, :]))
            link(dve, v.tensor_scalar(blk_i[:], key_i[:, k, :], P - 1, None, ALU.bitwise_and))
            link(dve, v.tensor_copy(local[:, k, :], blk_i[:]))
            link(dve, v.tensor_scalar(blk_i[:], key_i[:, k, :], KEY_SHIFT, None, ALU.logical_shift_right))
            link(dve, v.tensor_copy(blk_f[:], blk_i[:]))
            start = links[0]
            with dve.Fori(0, NB) as b:
                v.tensor_tensor(eq[:], blk_f[:], iota_f[0:EP, bass.ds(b, 1)].to_broadcast([EP, EC]),
                                ALU.is_equal).then_inc(chain, 1)
                dve.wait_ge(chain, b * 2 + (start + 1))
                v.tensor_reduce(cnt[:, bass.ds(b, 1)], eq[:], AX.X, ALU.add).then_inc(chain, 1)
                dve.wait_ge(chain, b * 2 + (start + 2))
            links[0] += 2 * NB
            v.engine_nop().then_inc(cnt_ready, 1)
            dve.wait_ge(off_ready, 2 * k + 2)
            link(dve, v.tensor_copy(tot_i[:], ps_tot[:, 0:NB]))
            link(dve, v.tensor_scalar(tot_i[:], tot_i[:], SE - 1, None, ALU.add))
            link(dve, v.tensor_scalar(tot_i[:], tot_i[:], STEP_SHIFT, None, ALU.logical_shift_right))
            link(dve, v.tensor_copy(need[:], tot_i[:]))
            link(dve, v.tensor_tensor_scan(ends[:], need[:], zero[:], 0.0, ALU.add, ALU.add))
            v.engine_nop().then_inc(end_ready, 1)
            link(dve, v.tensor_tensor(need[:], ends[:], need[:], ALU.subtract))
            link(dve, v.tensor_scalar(need[:], need[:], float(SE), -1.0, ALU.mult, ALU.add))
            link(dve, v.tensor_tensor(offs[:], ps_off[0:EP, 0:NB], need[0:EP, :], ALU.add))
            start = links[0]
            with dve.Fori(0, NB) as b:
                v.tensor_tensor(eq[:], blk_f[:], iota_f[0:EP, bass.ds(b, 1)].to_broadcast([EP, EC]),
                                ALU.is_equal).then_inc(chain, 1)
                dve.wait_ge(chain, b * 3 + (start + 1))
                v.tensor_tensor_scan(rank[:], eq[:], blk_f[:], offs[:, bass.ds(b, 1)],
                                     ALU.add, ALU.bypass).then_inc(chain, 1)
                dve.wait_ge(chain, b * 3 + (start + 2))
                step_aside(dve, passed)
                v.copy_predicated(pos_f[:], eq[:], rank[:]).then_inc(chain, 1)
                dve.wait_ge(chain, b * 3 + (start + 3))
            links[0] += 3 * NB
            link(dve, v.tensor_copy(pos[:, k, :], pos_f[:]))
            dve.wait_ge(endT_ready, k + 1)
            link(dve, v.tensor_copy(endT[:], ps_end[0:NB, 0:1]))
            v.tensor_scalar(past[:], iota_f[0:NB, :], endT[:], None, ALU.is_ge).then_inc(past_ready, 1)
            dve.wait_ge(blk_ready, k + 1)
            link(dve, v.tensor_scalar(steps[0:1, k, :], ps_blk[0:1, 0:S], float(NB - 1), None, ALU.min))
        first = nc.Block()
        block = first.__enter__()

        @block.sync
        def _(sp):
            sp.dma_start(key_i[:, 0, :], d["dst"].rearrange("(p c) -> p c", p=EP)).then_inc(edges_in, 16)
            sp.dma_start(key_i[:, 1, :], d["src"].rearrange("(p c) -> p c", p=EP)).then_inc(edges_in, 16)
            sp.dma_start(typ_i[:], d["edge_type_64"].rearrange("(p c) -> p c", p=EP)).then_inc(edges_in, 16)
            sp.wait_ge(blanked, 3)
            rows = S * SE // P
            for k in range(2):
                sp.dma_start(
                    d["rec"][k].rearrange("(p a c) w -> p a (c w)", p=P, c=CH),
                    blank[:, k, :].unsqueeze(1).to_broadcast([P, rows // CH, CH * RW]),
                ).then_inc(filled, 16)
            sp.wait_ge(filled, 32)

        @block.gpsimd
        def _(pool):
            pool.iota(iota_i[:], pattern=[[1, S]], base=0, channel_multiplier=0).then_inc(iota_done, 1)
            pool.memset(below[:], 1.0).then_inc(consts, 1)
            pool.memset(ones[:], 1.0).then_inc(consts, 1)
            pool.wait_ge(consts, 2)
            pool.affine_select(out=below[:], in_=below[:], compare_op=ALU.is_gt, fill=0.0, base=0,
                               pattern=[[1, P]], channel_multiplier=-1).then_inc(consts, 1)
            pool.memset(blank[:], 0.0).then_inc(blanked, 1)
            pool.wait_ge(blanked, 1)
            for k, word in enumerate((1, EA + 1)):
                pool.memset(blank[:, k, :].rearrange("p (c w) -> p c w", c=CH)[:, :, word:word + 1], -1.0).then_inc(blanked, 1)

        @block.tensor
        def _(pe):
            pe.wait_ge(consts, 3)
            order_products(pe, 0)

        @block.vector
        def _(dve):
            v = nc.vector
            dve.wait_ge(iota_done, 1)
            link(dve, v.tensor_copy(iota_f[:], iota_i[:]))
            link(dve, v.memset(zero[:], 0.0))
            dve.wait_ge(edges_in, 48)
            link(dve, v.tensor_copy(rel[:], typ_i[:]))
            order(dve, 0)
        first.__exit__(None, None, None)

        block = ctx.enter_context(nc.Block())

        def free(e, c, r):
            if late(c, 2):
                e.wait_ge(sent[r], (c - r) * (16 * CH // 2))

        @block.sync
        def _(sp):
            def load(c, r):
                free(sp, c, r)
                sp.dma_start(row[:, r, :, 4:4 + EA], attr[:, bass.ds(c * CH, CH), :]).then_inc(attr_in[r], 16)
            pipelined(sp, EC // CH, [(0, load)], 2)
            sp.wait_ge(late_ready, 1)
            sp.dma_start(d["late"], late_meta[:]).then_inc(late_sent, 16)
            sp.wait_ge(late_sent, 16)

        @block.scalar
        def _(act):
            a = nc.scalar

            def meta(c, r):
                free(act, c, r)
                cols = bass.ds(c * CH, CH)
                one = lambda w: row[:, r, :, w:w + 1].rearrange("p c o -> p (c o)")
                a.copy(one(0).bitcast(I32), gidx[:, 0, cols])
                a.copy(one(1), local[:, 0, cols])
                a.copy(one(2), rel[:, cols])
                a.copy(idx[:, r, :], pos[:, 0, cols]).then_inc(meta_done, 1)
            act.wait_ge(zeroed, 1)
            pipelined(act, EC // CH, [(0, meta)], 2)

        @block.gpsimd
        def _(pool):
            pool.memset(row[:, :, :, 0:4], 0.0).then_inc(zeroed, 1)

            def send(c, r):
                pool.wait_ge(attr_in[r], landed(c, r, 2))
                pool.wait_ge(meta_done, c + 1)
                step_aside(pool, scatter_passed)
                for j in range(CH):
                    pool.indirect_dma_start(
                        d["rec"][0], bass.IndirectOffsetOnAxis(ap=idx[:, r, j:j + 1], axis=0),
                        row[:, r, j, :], None).then_inc(sent[r], 16)
            pipelined(pool, EC // CH, [(0, send)], 2)
            for r in range(2):
                pool.wait_ge(sent[r], EC // CH // 2 * CH * 16)

        @block.tensor
        def _(pe):
            order_products(pe, 1)

        @block.vector
        def _(dve):
            v = nc.vector
            order(dve, 1)
            link(dve, v.memset(late_meta[:], 0.0))
            one = lambda w: late_meta[:, :, w:w + 1].rearrange("p c o -> p (c o)")
            link(dve, v.tensor_copy(one(0).bitcast(I32), gidx[:, 1, :]))
            link(dve, v.tensor_copy(one(1), local[:, 1, :]))
            link(dve, v.tensor_copy(one(4).bitcast(I32), pos[:, 1, :]))
            v.engine_nop().then_inc(late_ready, 1)


def edge_phase(nc, d, keep, name, order, heads, kind):
    C = F // heads
    attention = kind != "conv"
    attrs = kind != "gat"
    width = {"edge": 2 * F, "rel": 2 * F, "gat": F + heads, "conv": F}[kind]
    v0 = F if kind in ("edge", "rel") else 0
    meta, ao = ((0, 4), (EA, 0))[order]
    acc_w = heads * (C + 1) if attention else F
    q_scale = float(C) ** -0.5
    steps = keep["steps"][:, order, :]
    acc, q, mx = keep["acc"], keep["q"], keep["mx"]
    iota, ident, ident_b = keep["iota"], keep["ident"], keep["ident_b"]
    rec_d = d["rec"][order].rearrange("(s p g) w -> s p g w", p=P, g=G)
    R = 8
    with ExitStack() as ctx:
        sb = lambda n, shape, dt: ctx.enter_context(nc.sbuf_tensor(f"{name}_{n}", shape, dt))
        psum = lambda n, dt=F32: ctx.enter_context(
            nc.psum_tensor(f"{name}_{n}", [P, 512 if dt is F32 else 1024], dt))
        sem = phase_semaphores(nc, ctx, lambda n: f"{name}_{n}")
        rec = sb("rec", [P, R, G, RW], F32)
        kv = sb("kv", [P, R, G, width], F32)
        oh = sb("oh", [P, R, G, P], F32)
        oht = sb("oht", [P, R, SE], F32)
        away = sb("away", [P, 2, G, P], F32)
        mask = sb("mask", [P, R, SE], BF16)
        attrT = sb("attrT", [EA, 2, SE], F32)
        e_sb = sb("e_sb", [P, 2, G, F], F32)
        prod = sb("prod", [P, G, F], F32)
        alpha = sb("alpha", [P, 4, G, heads], F32)
        split = sb("split", [P, 2, G, 2 * heads], BF16)
        aT = sb("aT", [2 * heads, 2, SE], BF16)
        sel = sb("sel", [2 * heads, heads, P], BF16)
        tmax = sb("tmax", [P, 2, heads], F32)
        mnew = sb("mnew", [P, 2, heads], F32)
        mdiff = sb("mdiff", [P, 2, heads], F32)
        scale = sb("scale", [P, 4, heads], F32)
        down = sb("down", [P, 2, G, heads], F32)
        pv = sb("pv", [P, 4, G, acc_w], F32)
        w_e = sb("w_e", [EA, F], F32)
        bank_t, bank_q, bank_e, bank_o, bank_x = (psum(n) for n in ("ps_t", "ps_q", "ps_e", "ps_o", "ps_x"))
        bank_m = [psum(f"ps_m{i}") for i in range(2)]
        bank_a = psum("ps_a", BF16)
        banks_e = [bank_e, bank_e if attention else bank_m[0]]
        banks_o = [bank_o, bank_o if attention else bank_m[1]]
        ring_b = 1 if attention else 2
        away_ready = sem("away_ready")
        passed, pe_passed = sem("passed"), sem("pe_passed")
        we_in, we_scaled, sel_done = sem("we_in"), sem("we_scaled"), sem("sel_done")
        rec_in = [sem(f"rec_in{r}") for r in range(R)]
        kv_in = keep["pool_dma"]
        before = keep["edge_phases"] * (S // R) * 16 * G
        keep["edge_phases"] += 1
        gathered = lambda i, r: (i - r) * (16 * G // R) + (16 * G + before)
        scatters = kind in ("edge", "rel")
        if scatters:
            column = sb("column", [P, R, RW + 1], F32)
            column_in = [sem(f"column_in{r}") for r in range(R)]
            column_dma = keep["column_dma"]
            first_column = 0 if kind == "edge" else EC - S
            columns_before = 0 if kind == "edge" else S // R * 16
            scattered = lambda i, r: (i - r) * (16 // R) + (16 + columns_before)
            attr_d = d["edge_attr_64"].rearrange("(p c) w -> p c w", p=EP)
        oh_ready, rel_ready = sem("oh_ready"), sem("rel_ready")
        turned, oht_ready = sem("turned"), sem("oht_ready")
        q_ready, e_ready, e_copied, kv_ready = sem("q_ready"), sem("e_ready"), sem("e_copied"), sem("kv_ready")
        multiplied, alpha_ready, hi_ready, split_ready = sem("multiplied"), sem("alpha_ready"), sem("hi_ready"), sem("split_ready")
        aT_turned, aT_ready = sem("aT_turned"), sem("aT_ready")
        m_filled, m_read = sem("m_filled"), sem("m_read")
        mnew_ready, mdiff_ready, mx_kept = sem("mnew_ready"), sem("mdiff_ready"), sem("mx_kept")
        mexp_ready, down_ready, scale_ready, p_ready = sem("mexp_ready"), sem("down_ready"), sem("scale_ready"), sem("p_ready")
        pv_ready, out_ready, acc_scaled, acc_done = sem("pv_ready"), sem("out_ready"), sem("acc_scaled"), sem("acc_done")
        by_head = lambda ap: ap.rearrange("p g (h c) -> p g h c", h=heads)
        pv_view = lambda i2: by_head(pv[:, i2])
        banks = heads // 2
        block = ctx.enter_context(nc.Block())

        @block.sync
        def _(sp):
            if attrs:
                if kind == "rel":
                    sp.dma_start(w_e[:].rearrange("k (h c) -> k h c", h=heads), d["L1_gnn_rel_w"].unsqueeze(1).to_broadcast([EA, heads, C])).then_inc(we_in, 16)
                else:
                    sp.dma_start(w_e[:], d["L0_gnn_We" if kind == "edge" else "L3_gnn_G"]).then_inc(we_in, 16)

            def load(i, r):
                if late(i, R):
                    sp.wait_ge(oh_ready, i - (R - 1))
                    if attrs:
                        sp.wait_ge(turned, i - (R - 1))
                    sp.wait_ge(kv_in[r], gathered(i, r) - 16 * G)
                if kind in ("rel", "gat"):
                    sp.dma_start(rec[:, r, :, meta:meta + 4], rec_d[bass.ds(i, 1), :, :, meta:meta + 4].rearrange("s p g w -> (s p) g w")).then_inc(rec_in[r], 16)
                else:
                    sp.dma_start(rec[:, r], rec_d[bass.ds(i, 1)].rearrange("s p g w -> (s p) g w")).then_inc(rec_in[r], 16)

            def load_column(i, r):
                if late(i, R):
                    sp.wait_ge(column_dma[r], scattered(i, r) - 16)
                sp.dma_start(column[0:EP, r, 0:EA], attr_d[:, bass.ds(i + first_column, 1), :].rearrange("p c w -> p (c w)")).then_inc(column_in[r], 16)
                sp.dma_start(column[0:EP, r, EA:EA + 5], d["late"][:, bass.ds(i + first_column, 1), :].rearrange("p c w -> p (c w)")).then_inc(column_in[r], 16)
            pipelined(sp, S, [(0, load)] + [(0, load_column)] * scatters, R)

        @block.gpsimd
        def _(pool):
            if attention:
                pool.memset(sel[:], 0.0).then_inc(sel_done, 1)
                for k in range(2):
                    pool.wait_ge(sel_done, k + 1)
                    pool.affine_select(out=sel[:], in_=sel[:], compare_op=ALU.not_equal, fill=1.0,
                                       base=-heads * k, pattern=[[-1, heads], [0, P]],
                                       channel_multiplier=1).then_inc(sel_done, 1)

            def gather(i, r):
                pool.wait_ge(rec_in[r], landed(i, r, R))
                if late(i, R):
                    pool.wait_ge(pv_ready, i - (R - 1))
                step_aside(pool, passed)
                for g in range(G):
                    pool.indirect_dma_start(
                        kv[:, r, g, :], None, d[f"{name}_table"],
                        bass.IndirectOffsetOnAxis(ap=rec[:, r, g, meta:meta + 1].bitcast(I32), axis=0),
                    ).then_inc(kv_in[r], 16)

            def add_edge(i, r):
                pool.wait_ge(e_copied, i + 1)
                pool.wait_ge(kv_in[r], gathered(i, r))
                if kind == "edge":
                    both = kv[:, r].rearrange("p g (k f) -> p g k f", k=2)
                    nc.gpsimd.tensor_tensor(both, both, e_sb[:, r % 2].unsqueeze(2).to_broadcast([P, G, 2, F]), ALU.add).then_inc(kv_ready, 1)
                else:
                    nc.gpsimd.tensor_tensor(kv[:, r, :, 0:F], kv[:, r, :, 0:F], e_sb[:, r % 2], ALU.add).then_inc(kv_ready, 1)

            def scatter_column(i, r):
                pool.wait_ge(column_in[r], landed(i, r, R) * 2)
                step_aside(pool, passed)
                pool.indirect_dma_start(
                    d["rec"][1], bass.IndirectOffsetOnAxis(ap=column[0:EP, r, RW:RW + 1].bitcast(I32), axis=0),
                    column[0:EP, r, 0:RW], None).then_inc(column_dma[r], 16)
            pipelined(pool, S, [(0, gather)] + [(2, add_edge), (2, scatter_column)] * scatters, R)
            if scatters:
                for r in range(R):
                    pool.wait_ge(column_dma[r], scattered(S - R + r, r))

        @block.scalar
        def _(act):
            a = nc.scalar

            def select(i, r):
                act.wait_ge(rec_in[r], landed(i, r, R))
                if late(i, R):
                    act.wait_ge(out_ready, i - (R - 1))
                for g in range(G):
                    last = a.activation(away[:, r % 2, g, :], iota[:], ACT.Abs, bias=rec[:, r, g, meta + 1:meta + 2], scale=-1.0)
                last.then_inc(away_ready, 1)
                act.wait_ge(away_ready, i + 1)
                a.activation(oh[:, r], away[:, r % 2], ACT.Relu, bias=1.0, scale=-1.0).then_inc(oh_ready, 1)

            def copy_turned(i, r):
                act.wait_ge(turned, i + 1)
                if late(i, R) and attention:
                    act.wait_ge(mexp_ready, i - (R - 1))
                if attention:
                    a.copy(oht[:, r, :], bank_t[:, 0:SE])
                    last = a.activation(mask[:, r, :], bank_t[:, 0:SE], ACT.Copy, bias=-BIG, scale=BIG)
                if attrs:
                    if late(i, 2):
                        act.wait_ge(e_ready, i - 1)
                    last = a.copy(attrT[:, r % 2, :], bank_t[0:EA, SE:2 * SE])
                last.then_inc(oht_ready, 1)

            def copy_e(i, r):
                act.wait_ge(e_ready, i + 1)
                if late(i, 2):
                    act.wait_ge(kv_ready, i - 1)
                a.copy(e_sb[:, r % 2].rearrange("p g f -> p (g f)"), bank_e[:]).then_inc(e_copied, 1)

            def rescale(i, r):
                act.wait_ge(mdiff_ready, i + 1)
                if late(i, 4):
                    act.wait_ge(acc_scaled, i - 3)
                a.activation(scale[:, r % 4, :], mdiff[:, r % 2, :], ACT.Exp).then_inc(scale_ready, 1)

            def weights(i, r):
                act.wait_ge(down_ready, i + 1)
                if late(i, 4):
                    act.wait_ge(out_ready, i - 3)
                a.activation(pv_view(r % 4)[:, :, :, C:C + 1].rearrange("p g h o -> p g (h o)"), down[:, r % 2], ACT.Exp).then_inc(p_ready, 1)

            def copy_aT(i, r):
                act.wait_ge(aT_turned, i + 1)
                if late(i, 2):
                    act.wait_ge(m_filled, (i - 1) * banks)
                a.copy(aT[:, r % 2, :], bank_a[0:2 * heads, 0:SE]).then_inc(aT_ready, 1)

            stages = [(1, copy_turned), (0, select)]
            if attention:
                stages = ([(4, copy_aT)] + [(2, copy_e)] * (kind != "gat")
                          + [(6, rescale), (6, weights), (0, select), (1, copy_turned)])
            pipelined(act, S, stages, R)

        @block.tensor
        def _(pe):
            t = nc.tensor
            if attrs:
                pe.wait_ge(we_scaled, 1)
            if attention:
                pe.wait_ge(sel_done, 3)

            def fill_max(i, r, these):
                pe.wait_ge(aT_ready, i + 1)
                for b in these:
                    if late(i, 1) or b >= 2:
                        pe.wait_ge(m_read, i * banks + (b - 1))
                    bank = bank_m[b % 2]
                    t.matmul(bank[:].rearrange("p (h e) -> p h e", h=2), ident_b[:],
                             mask[:, r, :].unsqueeze(1).to_broadcast([P, 2, SE]), start=True, stop=False)
                    for h in range(2):
                        last = t.matmul(bank[:, h * SE:(h + 1) * SE], sel[:, 2 * b + h, :], aT[:, r % 2, :],
                                        start=False, stop=h == 1)
                    last.then_inc(m_filled, 1)

            def turn_edges(i, r):
                pe.wait_ge(oh_ready, i + 1)
                if attrs:
                    pe.wait_ge(rel_ready if kind == "rel" else rec_in[r], i + 1 if kind == "rel" else landed(i, r, R))
                if late(i, 1):
                    pe.wait_ge(oht_ready, i)
                if not attention:
                    step_aside(pe, pe_passed)
                for g in range(G):
                    if attention:
                        last = t.transpose(bank_t[:, g * P:(g + 1) * P], oh[:, r, g, :], ident[:])
                    if attrs:
                        last = t.transpose(bank_t[0:EA, SE + g * P:SE + (g + 1) * P], rec[:, r, g, ao:ao + EA], ident[:])
                last.then_inc(turned, 1)

            def sum_nodes(i, r):
                pe.wait_ge(pv_ready, i + 1)
                if late(i, ring_b):
                    pe.wait_ge(acc_done, i - (ring_b - 1))
                for g in range(G):
                    last = t.matmul(banks_o[r % 2][:, 0:acc_w], oh[:, r, g, :], pv[:, r % 4, g, :], start=g == 0, stop=g == G - 1)
                last.then_inc(out_ready, 1)

            def spread_max(i, r):
                pe.wait_ge(mnew_ready, i + 1)
                if late(i, 1):
                    pe.wait_ge(down_ready, i)
                for g in range(G):
                    last = t.matmul(bank_x[:, g * heads:(g + 1) * heads], oht[:, r, g * P:(g + 1) * P],
                                    mnew[:, r % 2, :], start=True, stop=True)
                last.then_inc(mexp_ready, 1)

            def products(i, r, *b):
                pe.wait_ge(oht_ready, i + 1)
                if attrs:
                    if late(i, ring_b):
                        pe.wait_ge(pv_ready if kind == "conv" else e_copied, i - (ring_b - 1))
                    for g in range(G):
                        last = t.matmul(banks_e[r % 2][:, g * F:(g + 1) * F], attrT[:, r % 2, g * P:(g + 1) * P], w_e[:],
                                        start=True, stop=True)
                    last.then_inc(e_ready, 1)
                if attention:
                    if late(i, 1):
                        pe.wait_ge(multiplied, i)
                    w = F if kind != "gat" else heads
                    for g in range(G):
                        last = t.matmul(bank_q[:, g * w:(g + 1) * w], oht[:, r, g * P:(g + 1) * P],
                                        q[:, bass.ds(b[0], 1), 0:w].rearrange("p o f -> p (o f)"), start=True, stop=True)
                    last.then_inc(q_ready, 1)

            def turn_scores(i, r):
                pe.wait_ge(split_ready, i + 1)
                if late(i, 1):
                    pe.wait_ge(aT_ready, i)
                for g in range(G):
                    last = t.transpose(bank_a[0:2 * heads, g * P:(g + 1) * P], split[:, r % 2, g, :], ident_b[:])
                last.then_inc(aT_turned, 1)

            if attention:
                early = lambda i, r: fill_max(i, r, range(2))
                later = lambda i, r: fill_max(i, r, range(2, banks))
                last_two = [(8, sum_nodes), (1, turn_edges)] if attrs else [(1, turn_edges), (8, sum_nodes)]
                pipelined(pe, S, [(5, early), (6, spread_max), (4, turn_scores), (2, products, True)]
                          + [(5, later)] * (banks > 2) + last_two, R, steps)
            else:
                pipelined(pe, S, [(2, products), (1, turn_edges), (4, sum_nodes)], R)

        @block.vector
        def _(dve):
            v = nc.vector
            if attrs:
                dve.wait_ge(we_in, 16)
                v.tensor_scalar(w_e[:], w_e[:], 0.2 if kind == "rel" else 1.0, None, ALU.mult).then_inc(we_scaled, 1)

            def select_relation(i, r):
                dve.wait_ge(rec_in[r], landed(i, r, R))
                v.tensor_tensor(rec[:, r, :, ao:ao + EA], iota[:, 0:EA].unsqueeze(1).to_broadcast([P, G, EA]),
                                rec[:, r, :, meta + 2:meta + 3].to_broadcast([P, G, EA]), ALU.is_equal).then_inc(rel_ready, 1)

            def weigh(i, r):
                dve.wait_ge(p_ready, i + 1)
                v.tensor_tensor(pv_view(r % 4)[:, :, :, 0:C], by_head(kv[:, r, :, v0:v0 + F]),
                                pv_view(r % 4)[:, :, :, C:C + 1].to_broadcast([P, G, heads, C]), ALU.mult).then_inc(pv_ready, 1)

            def multiply(i, r):
                dve.wait_ge(e_ready, i + 1)
                dve.wait_ge(kv_in[r], gathered(i, r))
                if late(i, 4):
                    dve.wait_ge(out_ready, i - 3)
                v.tensor_tensor(pv[:, r % 4], kv[:, r], banks_e[r % 2][:].rearrange("p (g f) -> p g f", g=G), ALU.mult).then_inc(pv_ready, 1)

            def acc_of(b):
                return acc[:, bass.ds(b, 1), 0:acc_w].rearrange("p o (h c) -> p (o h) c", h=heads)

            def rescale(i, r, b):
                mine = acc_of(b)
                dve.wait_ge(scale_ready, i + 1)
                if late(i, 1):
                    dve.wait_ge(acc_done, i)
                v.tensor_tensor(mine, mine, scale[:, r % 4, :].unsqueeze(2).to_broadcast([P, heads, C + 1]), ALU.mult).then_inc(acc_scaled, 1)

            def accumulate(i, r, b):
                dve.wait_ge(out_ready, i + 1)
                if attention:
                    mine = acc_of(b)
                    dve.wait_ge(acc_scaled, i + 1)
                    v.tensor_tensor(mine, mine, bank_o[:, 0:acc_w].rearrange("p (h c) -> p h c", h=heads), ALU.add).then_inc(acc_done, 1)
                else:
                    if late(i, 1):
                        dve.wait_ge(acc_done, i)
                    mine = acc[:, bass.ds(b, 1), 0:acc_w].rearrange("p o f -> p (o f)")
                    v.tensor_tensor(mine, mine, banks_o[r % 2][:, 0:acc_w], ALU.add).then_inc(acc_done, 1)

            def reduce_banks(i, r, these):
                for k in these:
                    dve.wait_ge(m_filled, i * banks + (k + 1))
                    if k == 0 and late(i, 2):
                        dve.wait_ge(mnew_ready, i - 1)
                    v.tensor_reduce(tmax[:, r % 2, 2 * k:2 * k + 2], bank_m[k % 2][:].rearrange("p (h e) -> p h e", h=2),
                                    AX.X, ALU.max).then_inc(m_read, 1)

            def new_maximum(i, r, b):
                dve.wait_ge(m_read, (i + 1) * banks)
                old = mx[:, bass.ds(b, 1), 0:heads].rearrange("p o h -> p (o h)")
                if late(i, 1):
                    dve.wait_ge(mx_kept, i)
                if late(i, 2):
                    dve.wait_ge(mexp_ready, i - 1)
                    dve.wait_ge(scale_ready, i - 1)
                v.tensor_tensor(mnew[:, r % 2, :], old, tmax[:, r % 2, :], ALU.max).then_inc(mnew_ready, 1)

            def maximum_change(i, r, b):
                old = mx[:, bass.ds(b, 1), 0:heads].rearrange("p o h -> p (o h)")
                dve.wait_ge(mnew_ready, i + 1)
                v.tensor_tensor(mdiff[:, r % 2, :], old, mnew[:, r % 2, :], ALU.subtract).then_inc(mdiff_ready, 1)

            def keep_maximum(i, r, b):
                old = mx[:, bass.ds(b, 1), 0:heads].rearrange("p o h -> p (o h)")
                dve.wait_ge(mdiff_ready, i + 1)
                v.tensor_tensor(old, mnew[:, r % 2, :], mnew[:, r % 2, :], ALU.max).then_inc(mx_kept, 1)

            def score(i, r):
                dve.wait_ge(q_ready, i + 1)
                if late(i, 1):
                    dve.wait_ge(alpha_ready, i)
                if kind == "gat":
                    dve.wait_ge(kv_in[r], gathered(i, r))
                    part = prod[:, :, 0:heads]
                    v.tensor_tensor(part, kv[:, r, :, F:F + heads], bank_q[:, 0:G * heads].rearrange("p (g h) -> p g h", g=G),
                                    ALU.add).then_inc(multiplied, 1)
                else:
                    dve.wait_ge(kv_ready, i + 1)
                    v.scalar_tensor_tensor(out=prod[:], in0=bank_q[:].rearrange("p (g f) -> p g f", g=G), scalar=q_scale,
                                           in1=kv[:, r, :, 0:F], op0=ALU.mult, op1=ALU.mult).then_inc(multiplied, 1)

            def finish_score(i, r):
                dve.wait_ge(multiplied, i + 1)
                if late(i, 4):
                    dve.wait_ge(down_ready, i - 3)
                if kind == "gat":
                    v.scalar_tensor_tensor(out=alpha[:, r % 4], in0=prod[:, :, 0:heads], scalar=0.2, in1=prod[:, :, 0:heads], op0=ALU.mult, op1=ALU.max).then_inc(alpha_ready, 1)
                else:
                    v.tensor_reduce(alpha[:, r % 4].rearrange("p g h -> p (g h)"),
                                    prod[:].rearrange("p g (h c) -> p (g h) c", h=heads), AX.X, ALU.add).then_inc(alpha_ready, 1)

            def split_scores(i, r):
                dve.wait_ge(alpha_ready, i + 1)
                if late(i, 2):
                    dve.wait_ge(aT_turned, i - 1)
                v.tensor_copy(split[:, r % 2, :, 0:heads], alpha[:, r % 4]).then_inc(hi_ready, 1)

            def split_rest(i, r):
                dve.wait_ge(hi_ready, i + 1)
                v.tensor_tensor(split[:, r % 2, :, heads:2 * heads], alpha[:, r % 4], split[:, r % 2, :, 0:heads], ALU.subtract).then_inc(split_ready, 1)

            def lower(i, r):
                dve.wait_ge(mexp_ready, i + 1)
                if late(i, 2):
                    dve.wait_ge(p_ready, i - 1)
                v.tensor_tensor(down[:, r % 2], alpha[:, r % 4], bank_x[:, 0:G * heads].rearrange("p (g h) -> p g h", g=G),
                                ALU.subtract).then_inc(down_ready, 1)

            if attention:
                early = lambda i, r: reduce_banks(i, r, range(2))
                later = lambda i, r: reduce_banks(i, r, range(2, banks))
                pipelined(dve, S, [(9, rescale, True), (3, score), (9, accumulate, True), (6, lower), (5, early),
                                   (3, finish_score), (7, weigh)] + [(5, later)] * (banks > 2)
                          + [(3, split_scores), (5, new_maximum, True), (3, split_rest), (5, maximum_change, True),
                             (5, keep_maximum, True)] + [(0, select_relation)] * (kind == "rel"), R, steps)
            else:
                pipelined(dve, S, [(3, multiply), (5, accumulate, True)], R, steps)


def node_phase(nc, d, keep, layer):
    acc, q, mx, ident = keep["acc"], keep["q"], keep["mx"], keep["ident"]
    adds = layer in (1, 3)
    heads_before, heads = (0, 8, 4, 4)[layer], (8, 4, 4, 1)[layer]
    x_in, x_out = d["xs"][layer], d["xs_updated"][layer]
    weights = ([("L0_gnn_Wq", "L0_gnn_bq"), ("L0_gnn_Wskip", "L0_gnn_bskip"), ("L0_gnn_Wk", "L0_gnn_bk"), ("L0_gnn_Wv", "L0_gnn_bv")],
               [("L1_gnn_Wq", "L1_gnn_bq"), ("L1_gnn_Wk", "L1_gnn_bk"), ("L1_gnn_Wv", "L1_gnn_bv")],
               [("L2_gnn_W", None)],
               [("L3_gnn_Wi", "L3_gnn_bi"), ("L3_gnn_Wj", "L3_gnn_bj")])[layer]
    first_bank = (2, 1, 1, 2)[layer]
    W = len(weights)
    width = (2 * F, 2 * F, F + 4, F)[layer]
    K = F // P
    R = 8
    name = f"n{layer}"
    more = layer in (1, 3)
    with ExitStack() as ctx:
        sb = lambda n, shape, dt=F32: ctx.enter_context(nc.sbuf_tensor(f"{name}_{n}", shape, dt))
        sem = phase_semaphores(nc, ctx, lambda n: f"{name}_{n}")
        psum = lambda n: ctx.enter_context(nc.psum_tensor(f"{name}_{n}", [P, 512], F32))
        w = sb("w", [P, W, K, F])
        bias = sb("bias", [P, W, F])
        extra = sb("extra", [P, 2, F])
        x = sb("x", [P, R, F])
        stats = sb("stats", [P, 2, 6])
        mean = sb("mean", [P, 2, 2])
        rstd = sb("rstd", [P, 2, 1])
        inv = sb("inv", [P, 2, 8])
        part = sb("part", [P, 2, F])
        hn = sb("hn", [P, 2, F])
        h = sb("h", [P, R, F])
        h2 = sb("h2", [P, 2, F])
        expd = sb("expd", [P, 2, F])
        hT = sb("hT", [P, 2, K, P])
        row = sb("row", [P, R, width])
        made = sb("made", [P, 2, 2 * F])
        made2 = sb("made2", [P, 2, 2 * F])
        same = sb("same", [P, F], I32)
        xi = sb("xi", [P, R, F])
        bank_t = psum("ps_t")
        banks = [[psum(f"ps_{b}{r}") for r in range(2)] for b in range(2)]
        eps_added, passed, pool_passed = sem("eps_added"), sem("passed"), sem("pool_passed")
        w_in, extra_ready = sem("w_in"), sem("extra_ready")
        x_in_sem = [sem(f"x_in{r}") for r in range(R)]
        x_sent = [sem(f"x_sent{r}") for r in range(R)]
        xi_sent = [sem(f"xi_sent{r}") for r in range(R)]
        h_sent = [sem(f"h_sent{r}") for r in range(R)]
        row_sent = [sem(f"row_sent{r}") for r in range(R)]
        s_ready, inv_ready, part_ready, x_ready = sem("s_ready"), sem("inv_ready"), sem("part_ready"), sem("x_ready")
        cleared, stats_ready, mean_ready, rstd_ready = sem("cleared"), sem("stats_ready"), sem("mean_ready"), sem("rstd_ready")
        hn_ready, h_ready, h2_ready, exp_ready, ln_ready = sem("hn_ready"), sem("h_ready"), sem("h2_ready"), sem("exp_ready"), sem("ln_ready")
        turned, hT_ready, product_ready = sem("turned"), sem("hT_ready"), sem("product_ready")
        evacuated, row_ready, chain = sem("evacuated"), sem("row_ready"), sem("chain")
        if layer in (0, 1):
            row_ready = evacuated
        abs_ready, made_exp, made_ln = sem("abs_ready"), sem("made_exp"), sem("made_ln")
        block = ctx.enter_context(nc.Block())
        rows = lambda t, i: t[bass.ds(i * P, P), :]
        operand_ready = h2_ready if more else h_ready

        @block.sync
        def _(sp):
            for n, (wn, bn) in enumerate(weights):
                sp.dma_start(w[:, n], d[wn].rearrange("(k p) f -> p k f", p=P)).then_inc(w_in, 16)
                if bn:
                    sp.dma_start(bias[:, n], d[bn].partition_broadcast(P)).then_inc(w_in, 16)
            if layer == 1:
                sp.dma_start(extra[:, 0], d["L1_gnn_query_emb"].partition_broadcast(P)).then_inc(w_in, 16)
            if layer == 2:
                for n, an in enumerate(("L2_gnn_a_l", "L2_gnn_a_r")):
                    sp.dma_start(extra[:, n], d[an].rearrange("o h c -> (o h c)").partition_broadcast(P)).then_inc(w_in, 16)

            def load(i, r):
                if late(i, R):
                    sp.wait_ge(hn_ready, i - (R - 1))
                    if x_out is not None:
                        sp.wait_ge(x_sent[r], (i - r) * (16 // R))
                sp.dma_start(x[:, r], rows(x_in, i)).then_inc(x_in_sem[r], 16)
            pipelined(sp, NB, [(0, load)], R)

        loads = 16 * (sum(1 + bool(bn) for _, bn in weights) + (0, 1, 2, 0)[layer])

        @block.gpsimd
        def _(pool):
            def clear(i, r):
                if adds:
                    pool.wait_ge(part_ready, i + 1)
                if layer != 2:
                    nc.gpsimd.tensor_copy(acc[:, bass.ds(i, 1), :], keep["zeros"][:].unsqueeze(1))
                nc.gpsimd.tensor_copy(mx[:, bass.ds(i, 1), :], keep["lowest"][:].unsqueeze(1)).then_inc(cleared, 1)

            def inverse_deviation(i, r):
                pool.wait_ge(mean_ready, i + 1)
                step_aside(pool, pool_passed)
                nc.gpsimd.tensor_scalar(rstd[:, r % 2], mean[:, r % 2, 1:2], 1e-5, None, ALU.add).then_inc(eps_added, 1)
                pool.wait_ge(eps_added, i + 1)
                nc.gpsimd.tensor_tensor(rstd[:, r % 2], rstd[:, r % 2], keep["minus_half"][:], ALU.pow).then_inc(rstd_ready, 1)

            pipelined(pool, NB, [(0, inverse_deviation), (0, clear)], R)

        @block.tensor
        def _(pe):
            t = nc.tensor
            pe.wait_ge(w_in, loads)

            def turn(i, r):
                pe.wait_ge(operand_ready, i + 1)
                if late(i, 1):
                    pe.wait_ge(hT_ready, i)
                src = h2[:, r % 2] if more else h[:, r]
                for k in range(K):
                    last = t.transpose(bank_t[:, k * P:(k + 1) * P], src[:, k * P:(k + 1) * P], ident[:])
                last.then_inc(turned, 1)

            def multiply(i, r):
                pe.wait_ge(hT_ready, i + 1)
                if late(i, 2):
                    pe.wait_ge(evacuated, i - 1)
                for n in range(W):
                    bank = banks[n >= first_bank][r % 2]
                    c = n - first_bank * (n >= first_bank)
                    for k in range(K):
                        last = t.matmul(bank[:, c * F:(c + 1) * F], hT[:, r % 2, k, :], w[:, n, k, :],
                                        start=k == 0, stop=k == K - 1)
                last.then_inc(product_ready, 1)
            pipelined(pe, NB, [(4 + more, multiply), (3 + more, turn)], R)

        @block.scalar
        def _(act):
            a = nc.scalar
            if layer == 3:
                a.preload_act_table_set("natural_log_exp_and_others")

            def relu(i, r):
                act.wait_ge(hn_ready, i + 1)
                if late(i, R):
                    act.wait_ge(turned, i - (R - 1))
                    if layer == 1:
                        act.wait_ge(h_sent[r], (i - r) * (16 // R))
                a.activation(h[:, r], hn[:, r % 2], ACT.Relu).then_inc(h_ready, 1)
                if layer == 3:
                    if late(i, 2):
                        act.wait_ge(h2_ready, i - 1)
                    act.wait_ge(h_ready, i + 1)
                    a.activation(expd[:, r % 2], h[:, r], ACT.Exp, scale=-1.0).then_inc(exp_ready, 1)
                    act.wait_ge(exp_ready, i + 1)
                    a.activation(expd[:, r % 2], expd[:, r % 2], ACT.Ln, bias=1.0).then_inc(ln_ready, 1)

            def copy_hT(i, r):
                act.wait_ge(turned, i + 1)
                if late(i, 2):
                    act.wait_ge(product_ready, i - 1)
                a.copy(hT[:, r % 2].rearrange("p k n -> p (k n)"), bank_t[:, 0:F]).then_inc(hT_ready, 1)

            def soften(i, r):
                act.wait_ge(evacuated, i + 1)
                if late(i, 2):
                    act.wait_ge(row_ready, i - 1)
                a.activation(made2[:, r % 2], made[:, r % 2], ACT.Abs).then_inc(abs_ready, 1)
                act.wait_ge(abs_ready, i + 1)
                a.activation(made2[:, r % 2], made2[:, r % 2], ACT.Exp, scale=-1.0).then_inc(made_exp, 1)
                act.wait_ge(made_exp, i + 1)
                a.activation(made2[:, r % 2], made2[:, r % 2], ACT.Ln, bias=1.0).then_inc(made_ln, 1)

            def send(i, r):
                act.wait_ge(row_ready, i + 1)
                act.dma_start(rows(d[f"L{layer}_table"], i), row[:, r]).then_inc(row_sent[r], 16)
                if layer != 2:
                    act.dma_start(rows(x_out, i), x[:, r]).then_inc(x_sent[r], 16)
                if layer == 1:
                    act.dma_start(rows(d["h1"], i), h[:, r]).then_inc(h_sent[r], 16)
                if layer == 3:
                    act.dma_start(rows(d["xi"], i), xi[:, r]).then_inc(xi_sent[r], 16)
            pipelined(act, NB, [(2, relu), (3 + more, copy_hT)] + [(6, soften)] * (layer == 3) + [(8, send)], R)
            for r in range(R):
                blocks = len(range(r, NB, R))
                act.wait_ge(row_sent[r], 16 * blocks)
                if layer != 2:
                    act.wait_ge(x_sent[r], 16 * blocks)
                if layer == 1:
                    act.wait_ge(h_sent[r], 16 * blocks)
                if layer == 3:
                    act.wait_ge(xi_sent[r], 16 * blocks)

        @block.vector
        def _(dve):
            v = nc.vector
            dve.wait_ge(w_in, loads)
            if layer == 1:
                v.tensor_scalar(extra[:, 0], extra[:, 0], 0.1, None, ALU.mult).then_inc(extra_ready, 1)
                dve.wait_ge(extra_ready, 1)

            def deviation(i, r):
                dve.wait_ge(x_in_sem[r], landed(i, r, R))
                xr, two = x[:, r], r % 2
                if adds:
                    H = heads_before
                    C = F // H
                    mine = acc[:, bass.ds(i, 1), 0:H * (C + 1)].rearrange("p o (h c) -> p (o h) c", h=H)
                    v.tensor_scalar(inv[:, two, 0:H].unsqueeze(2), mine[:, :, C:C + 1], 1e-16, None, ALU.add).then_inc(s_ready, 1)
                    dve.wait_ge(s_ready, i + 1)
                    v.reciprocal(inv[:, two, 0:H], inv[:, two, 0:H]).then_inc(inv_ready, 1)
                    dve.wait_ge(inv_ready, i + 1)
                    v.tensor_tensor(part[:, two].rearrange("p (h c) -> p h c", h=H), mine[:, :, 0:C],
                                    inv[:, two, 0:H].unsqueeze(2).to_broadcast([P, H, C]), ALU.mult).then_inc(part_ready, 1)
                    dve.wait_ge(part_ready, i + 1)
                    v.tensor_tensor(xr, xr, part[:, two], ALU.add).then_inc(x_ready, 1)
                    dve.wait_ge(x_ready, i + 1)
                v.bn_stats(stats[:, two], xr).then_inc(stats_ready, 1)
                dve.wait_ge(stats_ready, i + 1)
                step_aside(dve, passed)
                v.bn_aggr(mean[:, two], stats[:, two]).then_inc(mean_ready, 1)

            def normalise(i, r):
                two = r % 2
                dve.wait_ge(mean_ready, i + 1)
                dve.wait_ge(rstd_ready, i + 1)
                if late(i, 2):
                    dve.wait_ge(h_ready, i - 1)
                v.tensor_scalar(hn[:, two], x[:, r], mean[:, two, 0:1], rstd[:, two], ALU.subtract, ALU.mult).then_inc(hn_ready, 1)

            def operand(i, r):
                dve.wait_ge(ln_ready if layer == 3 else h_ready, i + 1)
                if late(i, 2):
                    dve.wait_ge(turned, i - 1)
                if layer == 1:
                    v.tensor_tensor(h2[:, r % 2], h[:, r], extra[:, 0], ALU.add).then_inc(h2_ready, 1)
                else:
                    v.scalar_tensor_tensor(out=h2[:, r % 2], in0=h[:, r], scalar=-0.6931471805599453, in1=expd[:, r % 2],
                                           op0=ALU.add, op1=ALU.add).then_inc(h2_ready, 1)

            def make(i, r):
                dve.wait_ge(product_ready, i + 1)
                if late(i, R):
                    dve.wait_ge(row_sent[r], (i - r) * (16 // R))
                b0, b1 = banks[0][r % 2], banks[1][r % 2]
                mine = q[:, bass.ds(i, 1), :].rearrange("p o f -> p (o f)")
                if layer in (0, 1):
                    v.tensor_tensor(mine, b0[:, 0:F], bias[:, 0], ALU.add)
                    if layer == 0:
                        v.tensor_tensor(made[:, r % 2, 0:F], b0[:, F:2 * F], bias[:, 1], ALU.add).then_inc(chain, 1)
                        dve.wait_ge(chain, i + 1)
                        v.tensor_tensor(x[:, r], x[:, r], made[:, r % 2, 0:F], ALU.add)
                    v.tensor_tensor(row[:, r], b1[:], bias[:, W - 2:W].rearrange("p a f -> p (a f)"), ALU.add).then_inc(evacuated, 1)
                if layer == 2:
                    hm, one = made[:, 0, 0:F], made[:, 1, 0:F]
                    if late(i, 1):
                        dve.wait_ge(row_ready, i)
                    v.memset(hm, 0.0).then_inc(chain, 1)
                    v.tensor_copy(one, b0[:, 0:F]).then_inc(chain, 1)
                    dve.wait_ge(chain, i * 5 + 2)
                    v.tensor_tensor(same[:], one, one, ALU.is_equal).then_inc(chain, 1)
                    dve.wait_ge(chain, i * 5 + 3)
                    step_aside(dve, passed)
                    v.copy_predicated(hm, same[:], one).then_inc(evacuated, 1)
                    dve.wait_ge(evacuated, i + 1)
                    v.tensor_copy(row[:, r, 0:F], hm)
                    for n in range(2):
                        out = (mine[:, 0:4], row[:, r, F:F + 4])[n]
                        v.tensor_tensor(made2[:, n, 0:F], hm, extra[:, n], ALU.mult).then_inc(chain, 1)
                        dve.wait_ge(chain, i * 5 + (4 + n))
                        last = v.tensor_reduce(out, made2[:, n, 0:F].rearrange("p (h c) -> p h c", h=4), AX.X, ALU.add)
                    last.then_inc(row_ready, 1)
                if layer == 3:
                    if late(i, 2):
                        dve.wait_ge(row_ready, i - 1)
                    v.tensor_tensor(made[:, r % 2], b0[:], bias[:].rearrange("p a f -> p (a f)"), ALU.add).then_inc(evacuated, 1)

            def finish(i, r):
                dve.wait_ge(made_ln, i + 1)
                if late(i, R):
                    dve.wait_ge(xi_sent[r], (i - r) * (16 // R))
                v.scalar_tensor_tensor(out=xi[:, r], in0=made[:, r % 2, 0:F], scalar=0.0, in1=made2[:, r % 2, 0:F], op0=ALU.max, op1=ALU.add)
                v.scalar_tensor_tensor(out=row[:, r], in0=made[:, r % 2, F:2 * F], scalar=0.0, in1=made2[:, r % 2, F:2 * F],
                                       op0=ALU.max, op1=ALU.add).then_inc(row_ready, 1)

            pipelined(dve, NB, [(5 + more, make)] + [(7, finish)] * (layer == 3)
                      + [(3, operand)] * more + [(1, normalise), (0, deviation)], R)


def relational_out_phase(nc, d, keep):
    acc, ident = keep["acc"], keep["ident"]
    H, K, R = 4, F // P, 4
    C = F // H
    with ExitStack() as ctx:
        sb = lambda n, shape, dt=F32: ctx.enter_context(nc.sbuf_tensor(f"o1_{n}", shape, dt))
        sem = phase_semaphores(nc, ctx, lambda n: f"o1_{n}")
        psum = lambda n: ctx.enter_context(nc.psum_tensor(f"o1_{n}", [P, 512], F32))
        w = sb("w", [P, K, F])
        vec = sb("vec", [P, 3, F])
        value, h, x = (sb(n, [P, R, F]) for n in ("value", "h", "x"))
        none = sb("none", [P, 2, H])
        inv = sb("inv", [P, 2, H])
        msg, own, y = (sb(n, [P, 2, F]) for n in ("msg", "own", "y"))
        msgT = sb("msgT", [P, 2, K, P])
        stats = sb("stats", [P, 2, 6])
        mean = sb("mean", [P, 2, 2])
        rstd = sb("rstd", [P, 2, 1])
        bank_t = psum("ps_t")
        bank_y = [psum(f"ps_y{r}") for r in range(2)]
        w_in = sem("w_in")
        tiles_in = [sem(f"tiles_in{r}") for r in range(R)]
        sent = [sem(f"sent{r}") for r in range(R)]
        head, msg_ready, turned, msgT_ready, product_ready = (sem(n) for n in ("head", "msg_ready", "turned", "msgT_ready", "product_ready"))
        eps_added, passed, pool_passed = sem("eps_added"), sem("passed"), sem("pool_passed")
        tail, x_ready, cleared = sem("tail"), sem("x_ready"), sem("cleared")
        block = ctx.enter_context(nc.Block())
        rows = lambda t, i: t[bass.ds(i * P, P), :]

        @block.sync
        def _(sp):
            sp.dma_start(w[:], d["L1_gnn_Wo"].rearrange("(k p) f -> p k f", p=P)).then_inc(w_in, 16)
            for n, name in enumerate(("L1_gnn_bo", "L1_gnn_gamma", "L1_gnn_beta")):
                sp.dma_start(vec[:, n], d[name].partition_broadcast(P)).then_inc(w_in, 16)

            def load(i, r):
                if late(i, R):
                    sp.wait_ge(sent[r], (i - r) * (16 // R))
                sp.dma_start(value[:, r], rows(d["L1_table"], i)[:, F:2 * F]).then_inc(tiles_in[r], 16)
                sp.dma_start(h[:, r], rows(d["h1"], i)).then_inc(tiles_in[r], 16)
                sp.dma_start(x[:, r], rows(d["xs"][2], i)).then_inc(tiles_in[r], 16)
            pipelined(sp, NB, [(0, load)], R)

        @block.gpsimd
        def _(pool):
            def clear(i, r):
                pool.wait_ge(msg_ready, i + 1)
                nc.gpsimd.tensor_copy(acc[:, bass.ds(i, 1), :], keep["zeros"][:].unsqueeze(1)).then_inc(cleared, 1)

            def inverse_deviation(i, r):
                pool.wait_ge(tail, i * 8 + 4)
                step_aside(pool, pool_passed)
                nc.gpsimd.tensor_scalar(rstd[:, r % 2], mean[:, r % 2, 1:2], 1e-5, None, ALU.add).then_inc(eps_added, 1)
                pool.wait_ge(eps_added, i + 1)
                nc.gpsimd.tensor_tensor(rstd[:, r % 2], rstd[:, r % 2], keep["minus_half"][:], ALU.pow).then_inc(tail, 1)
            pipelined(pool, NB, [(0, clear), (2, inverse_deviation)], R)

        @block.tensor
        def _(pe):
            t = nc.tensor
            pe.wait_ge(w_in, 64)

            def turn(i, r):
                pe.wait_ge(msg_ready, i + 1)
                if late(i, 1):
                    pe.wait_ge(msgT_ready, i)
                for k in range(K):
                    last = t.transpose(bank_t[:, k * P:(k + 1) * P], msg[:, r % 2, k * P:(k + 1) * P], ident[:])
                last.then_inc(turned, 1)

            def multiply(i, r):
                pe.wait_ge(msgT_ready, i + 1)
                if late(i, 2):
                    pe.wait_ge(x_ready, i - 1)
                for k in range(K):
                    last = t.matmul(bank_y[r % 2][:, 0:F], msgT[:, r % 2, k, :], w[:, k, :], start=k == 0, stop=k == K - 1)
                last.then_inc(product_ready, 1)
            pipelined(pe, NB, [(0, turn), (1, multiply)], R)

        @block.scalar
        def _(act):
            def copy_msgT(i, r):
                act.wait_ge(turned, i + 1)
                if late(i, 2):
                    act.wait_ge(product_ready, i - 1)
                nc.scalar.copy(msgT[:, r % 2].rearrange("p k n -> p (k n)"), bank_t[:, 0:F]).then_inc(msgT_ready, 1)

            def send(i, r):
                act.wait_ge(x_ready, i + 1)
                act.dma_start(rows(d["xs"][2], i), x[:, r]).then_inc(sent[r], 16)
            pipelined(act, NB, [(0, copy_msgT), (2, send)], R)
            for r in range(R):
                act.wait_ge(sent[r], 16 * len(range(r, NB, R)))

        @block.vector
        def _(dve):
            v = nc.vector
            dve.wait_ge(w_in, 64)

            def message(i, r):
                dve.wait_ge(tiles_in[r], (i - r) * (48 // R) + 48)
                two = r % 2
                mine = acc[:, bass.ds(i, 1), 0:H * (C + 1)].rearrange("p o (h c) -> p (o h) c", h=H)
                by_head = lambda ap: ap.rearrange("p (h c) -> p h c", h=H)
                wide = lambda ap: ap.unsqueeze(2).to_broadcast([P, H, C])
                v.tensor_scalar(none[:, two].unsqueeze(2), mine[:, :, C:C + 1], 0.0, None, ALU.is_equal).then_inc(head, 1)
                dve.wait_ge(head, i * 5 + 1)
                v.tensor_tensor(inv[:, two].unsqueeze(2), mine[:, :, C:C + 1], none[:, two].unsqueeze(2), ALU.add).then_inc(head, 1)
                dve.wait_ge(head, i * 5 + 2)
                v.reciprocal(inv[:, two], inv[:, two]).then_inc(head, 1)
                dve.wait_ge(head, i * 5 + 3)
                if late(i, 2):
                    dve.wait_ge(turned, i - 1)
                v.tensor_tensor(by_head(msg[:, two]), mine[:, :, 0:C], wide(inv[:, two]), ALU.mult).then_inc(head, 1)
                v.tensor_tensor(by_head(own[:, two]), by_head(value[:, r]), wide(none[:, two]), ALU.mult).then_inc(head, 1)
                dve.wait_ge(head, i * 5 + 5)
                v.tensor_tensor(msg[:, two], msg[:, two], own[:, two], ALU.add).then_inc(msg_ready, 1)

            def finish(i, r):
                two = r % 2
                n = [0]

                def link(ins):
                    n[0] += 1
                    ins.then_inc(tail, 1)
                    dve.wait_ge(tail, i * 8 + n[0])

                dve.wait_ge(product_ready, i + 1)
                link(v.tensor_tensor(y[:, two], bank_y[two][:, 0:F], h[:, r], ALU.add))
                link(v.tensor_tensor(y[:, two], y[:, two], vec[:, 0], ALU.add))
                link(v.bn_stats(stats[:, two], y[:, two]))
                step_aside(dve, passed)
                link(v.bn_aggr(mean[:, two], stats[:, two]))
                n[0] += 1
                dve.wait_ge(tail, i * 8 + n[0])
                link(v.tensor_scalar(y[:, two], y[:, two], mean[:, two, 0:1], rstd[:, two], ALU.subtract, ALU.mult))
                link(v.tensor_tensor(y[:, two], y[:, two], vec[:, 1], ALU.mult))
                link(v.tensor_tensor(y[:, two], y[:, two], vec[:, 2], ALU.add))
                v.tensor_tensor(x[:, r], x[:, r], y[:, two], ALU.add).then_inc(x_ready, 1)
            pipelined(dve, NB, [(0, message), (2, finish)], R)




def atom_out_phase(nc, d, keep):
    acc, ident = keep["acc"], keep["ident"]
    T = 7
    BATCHES, COLS, K, HALF = NB // T, T * P, F // P, T * P // 2
    LAYERS = 3
    with ExitStack() as ctx:
        sb = lambda n, shape, dt=F32: ctx.enter_context(nc.sbuf_tensor(f"o3_{n}", shape, dt))
        sem = phase_semaphores(nc, ctx, lambda n: f"o3_{n}")
        w1, w2 = sb("w1", [P, LAYERS, K, F]), sb("w2", [P, LAYERS, K, F])
        wv = sb("wv", [P, K, F])
        b1, b2 = sb("b1", [P, LAYERS, K]), sb("b2", [P, LAYERS, K])
        bv = sb("bv", [P, F])
        xi, x = sb("xi", [P, T, F]), sb("x", [P, T, F])
        v_rows = sb("v_rows", [P, T, F])
        vT, hT, logT = (sb(n, [P, K, COLS]) for n in ("vT", "hT", "logT"))
        y = sb("y", [P, T, F])
        bank = [[ctx.enter_context(nc.psum_tensor(f"o3_ps{s}{c}", [P, 512], F32)) for c in range(K)] for s in range(2)]
        bank_t = [ctx.enter_context(nc.psum_tensor(f"o3_pt{s}", [P, 512], F32)) for s in range(2)]
        bank_y = [ctx.enter_context(nc.psum_tensor(f"o3_py{s}", [P, 512], F32)) for s in range(2)]
        w_in, tiles_in, sent = sem("w_in"), sem("tiles_in"), sem("sent")
        rows_ready, turned, vT_ready = sem("rows_ready"), sem("turned"), sem("vT_ready")
        up_ready = [sem(f"up_ready{s}") for s in range(2)]
        abs_ready = [sem(f"abs_ready{s}") for s in range(2)]
        exp_ready = [sem(f"exp_ready{s}") for s in range(2)]
        log_ready = [sem(f"log_ready{s}") for s in range(2)]
        max_ready = [sem(f"max_ready{s}") for s in range(2)]
        h_ready = [sem(f"h_ready{s}") for s in range(2)]
        down_ready = [sem(f"down_ready{s}") for s in range(2)]
        v_ready = [sem(f"v_ready{s}") for s in range(2)]
        y_ready, y_biased, y_done = sem("y_ready"), sem("y_biased"), sem("y_done")
        block = ctx.enter_context(nc.Block())
        half = lambda s: slice(s * HALF, (s + 1) * HALF)
        SP_N = LAYERS + 1

        @block.sync
        def _(sp):
            for n in range(LAYERS):
                for w, name in ((w1, "L3_gnn_res_w1"), (w2, "L3_gnn_res_w2")):
                    sp.dma_start(w[:, n], d[name][n].rearrange("(k p) f -> p k f", p=P)).then_inc(w_in, 16)
                for b, name in ((b1, "L3_gnn_res_b1"), (b2, "L3_gnn_res_b2")):
                    for k in range(K):
                        sp.dma_start(b[:, n, k:k + 1], d[name][n:n + 1, k * P:(k + 1) * P].rearrange("o p -> p o")).then_inc(w_in, 16)
            sp.dma_start(wv[:], d["L3_gnn_Wv"].rearrange("(k p) f -> p k f", p=P)).then_inc(w_in, 16)
            sp.dma_start(bv[:], d["L3_gnn_bv"].partition_broadcast(P)).then_inc(w_in, 16)

            def send(i):
                sp.wait_ge(y_done, i * T + T)
                sp.dma_start(d["out"][bass.ds(i * COLS, COLS), :].rearrange("(t p) f -> p t f", p=P), y[:]).then_inc(sent, 16)

            def batch(i):
                if i is not None:
                    send(i)
                m = 0 if i is None else i + 1
                for t, src in ((xi, d["xi"]), (x, d["x3"])):
                    sp.dma_start(t[:], src[bass.ds(m * COLS, COLS), :].rearrange("(t p) f -> p t f", p=P)).then_inc(tiles_in, 16)
            batch(None)
            with sp.Fori(0, BATCHES - 1) as i:
                batch(i)
            send(BATCHES - 1)
            sp.wait_ge(sent, 16 * BATCHES)

        weights = 16 * (6 * LAYERS + 2)

        @block.tensor
        def _(pe):
            t = nc.tensor
            pe.wait_ge(w_in, weights)

            def batch(i):
                for j in range(T):
                    pe.wait_ge(rows_ready, i + 1)
                    if late(i, 1) or j >= 2:
                        pe.wait_ge(vT_ready, i * T + (j - 1))
                    for k in range(K):
                        last = t.transpose(bank_t[j % 2][:, k * P:(k + 1) * P], v_rows[:, j, k * P:(k + 1) * P], ident[:])
                    last.then_inc(turned, 1)

                def product(s, w, n, src, done):
                    for c in range(K):
                        for k in range(K):
                            last = t.matmul(bank[s][c][:, 0:HALF], w[:, n, k, c * P:(c + 1) * P], src[:, k, half(s)],
                                            start=k == 0, stop=k == K - 1)
                    last.then_inc(done, 1)

                for n in range(LAYERS):
                    for s in range(2):
                        if n == 0:
                            pe.wait_ge(vT_ready, (i + 1) * T)
                        else:
                            pe.wait_ge(v_ready[s], i * LAYERS + n)
                        product(s, w1, n, vT, up_ready[s])
                    for s in range(2):
                        pe.wait_ge(h_ready[s], i * SP_N + (n + 1))
                        product(s, w2, n, hT, down_ready[s])
                for s in range(2):
                    pe.wait_ge(h_ready[s], (i + 1) * SP_N)
                for j in range(T):
                    if late(i, 1) or j >= 2:
                        pe.wait_ge(y_biased, i * T + (j - 1))
                    for k in range(K):
                        last = t.matmul(bank_y[j % 2][:, 0:F], hT[:, k, j * P:(j + 1) * P], wv[:, k, :], start=k == 0, stop=k == K - 1)
                    last.then_inc(y_ready, 1)
            batch(0)
            with pe.Fori(1, BATCHES) as i:
                batch(i)

        @block.scalar
        def _(act):
            a = nc.scalar
            a.preload_act_table_set("natural_log_exp_and_others")
            act.wait_ge(w_in, weights)

            def batch(i):
                for n in range(SP_N):
                    for s in range(2):
                        m = i * SP_N + (n + 1)
                        if n < LAYERS:
                            act.wait_ge(up_ready[s], i * LAYERS + (n + 1))
                            for c in range(K):
                                last = a.activation(logT[:, c, half(s)], bank[s][c][:, 0:HALF], ACT.Abs, bias=b1[:, n, c:c + 1])
                        else:
                            act.wait_ge(v_ready[s], (i + 1) * LAYERS)
                            last = a.activation(logT[:, :, half(s)], vT[:, :, half(s)], ACT.Abs)
                        last.then_inc(abs_ready[s], 1)
                        act.wait_ge(abs_ready[s], m)
                        a.activation(logT[:, :, half(s)], logT[:, :, half(s)], ACT.Exp, scale=-1.0).then_inc(exp_ready[s], 1)
                        act.wait_ge(exp_ready[s], m)
                        a.activation(logT[:, :, half(s)], logT[:, :, half(s)], ACT.Ln, bias=1.0).then_inc(log_ready[s], 1)
            with act.Fori(0, BATCHES) as i:
                batch(i)

        @block.vector
        def _(dve):
            v = nc.vector
            dve.wait_ge(w_in, weights)

            def batch(i):
                dve.wait_ge(tiles_in, i * 32 + 32)
                v.tensor_tensor(v_rows[:], xi[:], acc[:, bass.ds(i * T, T), 0:F], ALU.add).then_inc(rows_ready, 1)
                for j in range(T):
                    dve.wait_ge(turned, i * T + (j + 1))
                    v.tensor_copy(vT[:, :, j * P:(j + 1) * P], bank_t[j % 2][:, 0:F].rearrange("p (k n) -> p k n", k=K)).then_inc(vT_ready, 1)
                for n in range(SP_N):
                    for s in range(2):
                        m = i * SP_N + (n + 1)
                        dve.wait_ge(log_ready[s], m)
                        if n < LAYERS:
                            for c in range(K):
                                last = v.tensor_scalar(hT[:, c, half(s)], bank[s][c][:, 0:HALF], b1[:, n, c:c + 1], 0.0, ALU.add, ALU.max)
                            last.then_inc(max_ready[s], 1)
                            dve.wait_ge(max_ready[s], i * LAYERS + (n + 1))
                            v.tensor_tensor(hT[:, :, half(s)], hT[:, :, half(s)], logT[:, :, half(s)], ALU.add).then_inc(h_ready[s], 1)
                        else:
                            v.scalar_tensor_tensor(out=hT[:, :, half(s)], in0=vT[:, :, half(s)], scalar=0.0, in1=logT[:, :, half(s)],
                                                   op0=ALU.max, op1=ALU.add).then_inc(h_ready[s], 1)
                    if n < LAYERS:
                        for s in range(2):
                            dve.wait_ge(down_ready[s], i * LAYERS + (n + 1))
                            for c in range(K):
                                last = v.scalar_tensor_tensor(out=vT[:, c, half(s)], in0=bank[s][c][:, 0:HALF], scalar=b2[:, n, c:c + 1],
                                                              in1=vT[:, c, half(s)], op0=ALU.add, op1=ALU.add)
                            last.then_inc(v_ready[s], 1)
                for j in range(T):
                    dve.wait_ge(y_ready, i * T + (j + 1))
                    if late(i, 1):
                        dve.wait_ge(sent, i * 16)
                    v.tensor_tensor(y[:, j], bank_y[j % 2][:, 0:F], bv[:], ALU.add).then_inc(y_biased, 1)
                    dve.wait_ge(y_biased, i * T + (j + 1))
                    v.tensor_tensor(y[:, j], y[:, j], x[:, j], ALU.add).then_inc(y_done, 1)
            batch(0)
            with dve.Fori(1, BATCHES) as i:
                batch(i)


def consts_phase(nc, keep):
    ident, ident_b, iota = keep["ident"], keep["ident_b"], keep["iota"]
    with ExitStack() as ctx:
        sem = phase_semaphores(nc, ctx, lambda n: f"c_{n}")
        iota_i = ctx.enter_context(nc.sbuf_tensor("c_iota_i", [P, P], I32))
        zeroed, set_, made, copied = sem("zeroed"), sem("set"), sem("made"), sem("copied")
        block = ctx.enter_context(nc.Block())

        @block.gpsimd
        def _(pool):
            pool.iota(iota_i[:], pattern=[[1, P]], base=0, channel_multiplier=0).then_inc(made, 1)
            pool.memset(keep["zeros"][:], 0.0).then_inc(made, 1)
            pool.memset(keep["minus_half"][:], -0.5).then_inc(made, 1)
            pool.memset(keep["lowest"][:], MMIN).then_inc(made, 1)
            pool.memset(ident[:], 0.0).then_inc(zeroed, 1)
            pool.wait_ge(zeroed, 1)
            pool.affine_select(out=ident[:], in_=ident[:], compare_op=ALU.not_equal, fill=1.0, base=0,
                               pattern=[[-1, P]], channel_multiplier=1).then_inc(set_, 1)

        @block.vector
        def _(dve):
            dve.wait_ge(made, 1)
            nc.vector.tensor_copy(iota[:], iota_i[:]).then_inc(copied, 1)
            dve.wait_ge(set_, 1)
            nc.vector.tensor_copy(ident_b[:], ident[:]).then_inc(copied, 1)




def gnn_program(nc, d, out):
    dram = lambda name, cols, rows=NB * P: nc.dram_tensor(name, (rows, cols), F32, kind="Internal").ap()
    d["rec"] = [dram(f"rec{k}", RW, S * SE) for k in range(2)]
    d["late"] = nc.dram_tensor("late", (EP, EC, 5), F32, kind="Internal").ap()
    for name, width in (("L0", 2 * F), ("L1", 2 * F), ("L2", F + 4), ("L3", F)):
        d[f"{name}_table"] = dram(f"{name}_table", width)
    x1, x2, d["x3"], d["h1"], d["xi"] = (dram(n, F) for n in ("x1", "x2", "x3", "h1", "xi"))
    d["xs"] = [d["x"], x1, x2, x2]
    d["xs_updated"] = [x1, x2, None, d["x3"]]
    d["out"] = out
    with ExitStack() as ctx:
        sb = lambda name, shape, dt=F32: ctx.enter_context(nc.sbuf_tensor(name, shape, dt))
        keep = {"steps": sb("steps", [1, 2, S], I32), "ident": sb("ident", [P, P]), "ident_b": sb("ident_b", [P, P], BF16),
                "iota": sb("iota", [P, P]), "zeros": sb("zeros", [P, 264]), "lowest": sb("lowest", [P, 8]),
                "minus_half": sb("minus_half", [P, 1])}
        keep["scatter_dma"] = [ctx.enter_context(nc.semaphore(f"scatter_dma{r}")) for r in range(2)]
        keep["pool_dma"] = [ctx.enter_context(nc.semaphore(f"pool_dma{r}")) for r in range(8)]
        keep["column_dma"] = [ctx.enter_context(nc.semaphore(f"column_dma{r}")) for r in range(8)]
        keep["edge_phases"] = 0
        with ExitStack() as inner:
            sbi = lambda name, shape, dt=F32: inner.enter_context(nc.sbuf_tensor(name, shape, dt))
            keep |= {"pos": sbi("pos", [EP, 2, EC], I32), "gidx": sbi("gidx", [EP, 2, EC], I32),
                     "local": sbi("local", [EP, 2, EC]), "rel": sbi("rel", [EP, EC])}
            consts_phase(nc, keep)
            sort_phase(nc, d, keep)
        keep |= {"q": sb("q", [P, NB, F]), "acc": sb("acc", [P, NB, 264]), "mx": sb("mx", [P, NB, 8])}
        phases = [
            lambda: node_phase(nc, d, keep, 0),
            lambda: edge_phase(nc, d, keep, "L0", 0, 8, "edge"),
            lambda: node_phase(nc, d, keep, 1),
            lambda: edge_phase(nc, d, keep, "L1", 0, 4, "rel"),
            lambda: relational_out_phase(nc, d, keep),
            lambda: node_phase(nc, d, keep, 2),
            lambda: edge_phase(nc, d, keep, "L2", 1, 4, "gat"),
            lambda: node_phase(nc, d, keep, 3),
            lambda: edge_phase(nc, d, keep, "L3", 1, 1, "conv"),
            lambda: atom_out_phase(nc, d, keep),
        ]
        for phase in phases:
            phase()


TRANSPOSED = ("L0_gnn_Wq", "L0_gnn_Wk", "L0_gnn_Wv", "L0_gnn_We", "L0_gnn_Wskip", "L3_gnn_G", "L3_gnn_Wi",
              "L3_gnn_Wj", "L3_gnn_res_w1", "L3_gnn_res_w2", "L3_gnn_Wv")




def kernel(**inputs):
    import numpy as np
    import concourse.bacc as bacc
    from concourse.bass_utils import run_bass_kernel_spmd

    nc = bacc.Bacc("TRN2", target_bir_lowering=False, num_devices=1)
    arrays, args = {}, {}
    for name, value in inputs.items():
        a = np.asarray(value)
        if name in TRANSPOSED:
            a = np.swapaxes(a, -1, -2)
        if name == "x":
            a = np.concatenate([a, np.zeros((NB * P - N, F), a.dtype)])
        a = np.ascontiguousarray(a)
        arrays[f"in_{name}"] = a
        args[name] = nc.dram_tensor(f"in_{name}", a.shape, mybir.dt.from_np(a.dtype), kind="ExternalInput").ap()
    out = nc.dram_tensor("out_x", (NB * P, F), F32, kind="ExternalOutput").ap()
    gnn_program(nc, args, out)
    result = run_bass_kernel_spmd(nc, [arrays], core_ids=[0])
    return result.results[0]["out_x"][:N]
```

```python
import concourse.bass as bass
from concourse import mybir
from contextlib import ExitStack

F32 = mybir.dt.float32
BF16 = mybir.dt.bfloat16
I32 = mybir.dt.int32
U8 = mybir.dt.uint8
ALU = mybir.AluOpType
ACT = mybir.ActivationFunctionType
AX = mybir.AxisListType

P = 128
N = 6250
F = 256
E = 100000
EA = 64
NB = -(-N // P)
G = 2
SE = G * P
S = -(-((E + NB * (SE - 1)) // SE) // 4) * 4
EP = 125
EC = E // EP
RW = EA + 4
CH = 8
BIG = float(2 ** 100)
MMIN = -float(2 ** 99)
KEY_SHIFT = 7
STEP_SHIFT = 8
assert 1 << KEY_SHIFT == P and 1 << STEP_SHIFT == SE and EP * EC == E and EC % (2 * CH) == 0 and S <= EC <= 2 * S


def pipelined(e, n, stages, unroll, table=None):
    most = max(stage[0] for stage in stages)
    asked = [stage[0] for stage in stages if stage[2:]]
    first = most + unroll
    loops = (n - first) // unroll
    last = first + loops * unroll

    def turn(t, r, loaded=None):
        for lag, stage, *asks in stages:
            if isinstance(t, int) and not 0 <= t - lag < n:
                continue
            more = [loaded(lag) if loaded else entry(e, table, t - lag)] if asks else []
            stage(t - lag, (r - lag) % unroll, *more)

    for t in range(first):
        turn(t, t % unroll)
    with e.Fori(0, loops) as k:
        values = None
        if asked:
            values = entries(e, table, k * unroll + (first - max(asked)), unroll + max(asked) - min(asked))
        for u in range(unroll):
            turn(k * unroll + (first + u), (first + u) % unroll,
                 values and (lambda lag: values[u + max(asked) - lag]))
    for t in range(last, n + most):
        turn(t, t % unroll)


def entry(e, table, i):
    return e.value_load(table[0:1, i:i + 1], min_val=0, max_val=NB - 1)


def entries(e, table, i, count):
    return e.bass.values_load_multi_w_load_instructions(
        table[0:1, bass.ds(i, count)], engines=[e.engine], min_val=0, max_val=NB - 1,
        skip_runtime_bounds_check_because="the sort clamps them")[1]


def phase_semaphores(nc, ctx, named):
    given = []

    def give(name):
        given.append(nc.alloc_semaphore(named(name)))
        return given[-1]

    def clear():
        with nc.Block() as block:
            @block.gpsimd
            def _(pool):
                for semaphore in given:
                    pool.sem_clear(semaphore)
        for semaphore in given:
            nc.release_semaphore(semaphore)

    ctx.callback(clear)
    return give


def step_aside(e, passed):
    e.sem_inc(passed, 1)


def late(i, k):
    return not isinstance(i, int) or i >= k


def landed(i, r, ring):
    return (i - r) * (16 // ring) + 16


def sort_phase(nc, d, keep):
    pos, gidx, local, rel, steps = keep["pos"], keep["gidx"], keep["local"], keep["rel"], keep["steps"]
    with ExitStack() as ctx:
        sb = lambda name, shape, dt: ctx.enter_context(nc.sbuf_tensor(name, shape, dt))
        sem = phase_semaphores(nc, ctx, lambda name: name)
        key_i = sb("key_i", [EP, 2, EC], I32)
        typ_i = sb("typ_i", [EP, EC], I32)
        blk_i = sb("blk_i", [EP, EC], I32)
        blk_f = sb("blk_f", [EP, EC], F32)
        eq = sb("eq", [EP, EC], U8)
        rank = sb("rank", [EP, EC], F32)
        pos_f = sb("pos_f", [EP, EC], F32)
        cnt = sb("cnt", [EP, NB], F32)
        offs = sb("offs", [EP, NB], F32)
        iota_i = sb("iota_i", [P, S], I32)
        iota_f = sb("iota_f", [P, S], F32)
        ones = sb("ones", [P, P], F32)
        below = sb("below", [P, P], F32)
        tot_i = sb("tot_i", [P, NB], I32)
        need = sb("need", [P, NB], F32)
        ends = sb("ends", [P, NB], F32)
        zero = sb("zero", [P, NB], F32)
        endT = sb("endT", [NB, 1], F32)
        past = sb("past", [NB, S], F32)
        ps_off = ctx.enter_context(nc.psum_tensor("ps_off", [P, 512], F32))
        ps_tot = ctx.enter_context(nc.psum_tensor("ps_tot", [P, 512], F32))
        ps_blk = ctx.enter_context(nc.psum_tensor("ps_blk", [P, 512], F32))
        edges_in = sem("sort_edges_in")
        consts = sem("sort_consts")
        iota_done = sem("sort_iota")
        blanked = sem("sort_blank")
        filled = sem("sort_filled")
        chain = sem("sort_chain")
        passed = sem("sort_passed")
        row = sb("sc_row", [EP, 2, CH, RW], F32)
        idx = sb("sc_idx", [EP, 2, CH], I32)
        late_meta = sb("late_meta", [EP, EC, 5], F32)
        attr = d["edge_attr_64"].rearrange("(p c) w -> p c w", p=EP)
        attr_in = [sem(f"sc_attr{r}") for r in range(2)]
        sent = keep["scatter_dma"]
        zeroed, meta_done, scatter_passed = sem("sc_zeroed"), sem("sc_meta"), sem("sc_passed")
        late_ready, late_sent = sem("late_ready"), sem("late_sent")
        cnt_ready = sem("sort_cnt")
        off_ready = sem("sort_off")
        end_ready = sem("sort_end")
        endT_ready = sem("sort_endT")
        past_ready = sem("sort_past")
        blk_ready = sem("sort_blk")

        def order_products(pe, k):
            pe.wait_ge(cnt_ready, k + 1)
            nc.tensor.matmul(ps_off[0:EP, 0:NB], below[0:EP, 0:EP], cnt[:], start=True, stop=True).then_inc(off_ready, 1)
            nc.tensor.matmul(ps_tot[:, 0:NB], ones[0:EP, :], cnt[:], start=True, stop=True).then_inc(off_ready, 1)
            pe.wait_ge(end_ready, k + 1)
            nc.tensor.matmul(ps_tot[0:NB, NB:NB + 1], ends[0:1, :], ones[0:1, 0:1], start=True, stop=True).then_inc(endT_ready, 1)
            pe.wait_ge(past_ready, k + 1)
            nc.tensor.matmul(ps_blk[:, 0:S], ones[0:NB, :], past[:], start=True, stop=True).then_inc(blk_ready, 1)

        links = [0]

        def link(dve, ins):
            links[0] += 1
            ins.then_inc(chain, 1)
            dve.wait_ge(chain, links[0])

        def order(dve, k):
            v = nc.vector
            other = 1 - k
            link(dve, v.tensor_copy(gidx[:, k, :], key_i[:, other, :]))
            link(dve, v.tensor_scalar(blk_i[:], key_i[:, k, :], P - 1, None, ALU.bitwise_and))
            link(dve, v.tensor_copy(local[:, k, :], blk_i[:]))
            link(dve, v.tensor_scalar(blk_i[:], key_i[:, k, :], KEY_SHIFT, None, ALU.logical_shift_right))
            link(dve, v.tensor_copy(blk_f[:], blk_i[:]))
            start = links[0]
            with dve.Fori(0, NB) as b:
                v.tensor_tensor(eq[:], blk_f[:], iota_f[0:EP, bass.ds(b, 1)].to_broadcast([EP, EC]),
                                ALU.is_equal).then_inc(chain, 1)
                dve.wait_ge(chain, b * 2 + (start + 1))
                v.tensor_reduce(cnt[:, bass.ds(b, 1)], eq[:], AX.X, ALU.add).then_inc(chain, 1)
                dve.wait_ge(chain, b * 2 + (start + 2))
            links[0] += 2 * NB
            v.engine_nop().then_inc(cnt_ready, 1)
            dve.wait_ge(off_ready, 2 * k + 2)
            link(dve, v.tensor_copy(tot_i[:], ps_tot[:, 0:NB]))
            link(dve, v.tensor_scalar(tot_i[:], tot_i[:], SE - 1, None, ALU.add))
            link(dve, v.tensor_scalar(tot_i[:], tot_i[:], STEP_SHIFT, None, ALU.logical_shift_right))
            link(dve, v.tensor_copy(need[:], tot_i[:]))
            link(dve, v.tensor_tensor_scan(ends[:], need[:], zero[:], 0.0, ALU.add, ALU.add))
            v.engine_nop().then_inc(end_ready, 1)
            link(dve, v.tensor_tensor(need[:], ends[:], need[:], ALU.subtract))
            link(dve, v.tensor_scalar(need[:], need[:], float(SE), -1.0, ALU.mult, ALU.add))
            link(dve, v.tensor_tensor(offs[:], ps_off[0:EP, 0:NB], need[0:EP, :], ALU.add))
            start = links[0]
            with dve.Fori(0, NB) as b:
                v.tensor_tensor(eq[:], blk_f[:], iota_f[0:EP, bass.ds(b, 1)].to_broadcast([EP, EC]),
                                ALU.is_equal).then_inc(chain, 1)
                dve.wait_ge(chain, b * 3 + (start + 1))
                v.tensor_tensor_scan(rank[:], eq[:], blk_f[:], offs[:, bass.ds(b, 1)],
                                     ALU.add, ALU.bypass).then_inc(chain, 1)
                dve.wait_ge(chain, b * 3 + (start + 2))
                step_aside(dve, passed)
                v.copy_predicated(pos_f[:], eq[:], rank[:]).then_inc(chain, 1)
                dve.wait_ge(chain, b * 3 + (start + 3))
            links[0] += 3 * NB
            link(dve, v.tensor_copy(pos[:, k, :], pos_f[:]))
            dve.wait_ge(endT_ready, k + 1)
            link(dve, v.tensor_copy(endT[:], ps_tot[0:NB, NB:NB + 1]))
            v.tensor_scalar(past[:], iota_f[0:NB, :], endT[:], None, ALU.is_ge).then_inc(past_ready, 1)
            dve.wait_ge(blk_ready, k + 1)
            link(dve, v.tensor_scalar(steps[0:1, k, :], ps_blk[0:1, 0:S], float(NB - 1), None, ALU.min))

        with ExitStack() as first:
            blank = first.enter_context(nc.sbuf_tensor("blank", [P, 2, CH * RW], F32))
            block = first.enter_context(nc.Block())

            @block.sync
            def _(sp):
                sp.dma_start(key_i[:, 0, :], d["dst"].rearrange("(p c) -> p c", p=EP)).then_inc(edges_in, 16)
                sp.dma_start(key_i[:, 1, :], d["src"].rearrange("(p c) -> p c", p=EP)).then_inc(edges_in, 16)
                sp.dma_start(typ_i[:], d["edge_type_64"].rearrange("(p c) -> p c", p=EP)).then_inc(edges_in, 16)
                sp.wait_ge(blanked, 3)
                rows = S * SE // P
                for k in range(2):
                    sp.dma_start(
                        d["rec"][k].rearrange("(p a c) w -> p a (c w)", p=P, c=CH),
                        blank[:, k, :].unsqueeze(1).to_broadcast([P, rows // CH, CH * RW]),
                    ).then_inc(filled, 16)
                sp.wait_ge(filled, 32)

            @block.gpsimd
            def _(pool):
                pool.iota(iota_i[:], pattern=[[1, S]], base=0, channel_multiplier=0).then_inc(iota_done, 1)
                pool.memset(below[:], 1.0).then_inc(consts, 1)
                pool.memset(ones[:], 1.0).then_inc(consts, 1)
                pool.wait_ge(consts, 2)
                pool.affine_select(out=below[:], in_=below[:], compare_op=ALU.is_gt, fill=0.0, base=0,
                                   pattern=[[1, P]], channel_multiplier=-1).then_inc(consts, 1)
                pool.memset(blank[:], 0.0).then_inc(blanked, 1)
                pool.wait_ge(blanked, 1)
                for k, word in enumerate((1, EA + 1)):
                    pool.memset(blank[:, k, :].rearrange("p (c w) -> p c w", c=CH)[:, :, word:word + 1], -1.0).then_inc(blanked, 1)

            @block.tensor
            def _(pe):
                pe.wait_ge(consts, 3)
                order_products(pe, 0)

            @block.vector
            def _(dve):
                v = nc.vector
                dve.wait_ge(iota_done, 1)
                link(dve, v.tensor_copy(iota_f[:], iota_i[:]))
                link(dve, v.memset(zero[:], 0.0))
                dve.wait_ge(edges_in, 48)
                link(dve, v.tensor_copy(rel[:], typ_i[:]))
                order(dve, 0)

        chunks_alone = EC // CH - NB

        def free(e, c, r):
            if late(c, 2):
                e.wait_ge(sent[r], (c - r) * (16 * CH // 2))

        def load(sp, c, r):
            free(sp, c, r)
            sp.dma_start(row[:, r, :, 4:4 + EA], attr[:, bass.ds(c * CH, CH), :]).then_inc(attr_in[r], 16)

        def meta(act, c, r):
            free(act, c, r)
            cols = bass.ds(c * CH, CH)
            one = lambda w: row[:, r, :, w:w + 1].rearrange("p c o -> p (c o)")
            act.copy(one(0).bitcast(I32), gidx[:, 0, cols])
            act.copy(one(1), local[:, 0, cols])
            act.copy(one(2), rel[:, cols])
            act.copy(idx[:, r, :], pos[:, 0, cols]).then_inc(meta_done, 1)

        def send(pool, c, r):
            pool.wait_ge(attr_in[r], landed(c, r, 2))
            pool.wait_ge(meta_done, c + 1)
            step_aside(pool, scatter_passed)
            for j in range(CH):
                pool.indirect_dma_start(
                    d["rec"][0], bass.IndirectOffsetOnAxis(ap=idx[:, r, j:j + 1], axis=0),
                    row[:, r, j, :], None).then_inc(sent[r], 16)

        def alone(e, stage):
            pipelined(e, chunks_alone, [(0, lambda c, r: stage(e, c, r))], 2)

        def along(e, stage):
            return [(0, lambda i, r: stage(e, i + chunks_alone, (r + chunks_alone) % 2))]

        def sync_first(sp):
            alone(sp, load)
            sp.wait_ge(late_ready, 1)
            sp.dma_start(d["late"], late_meta[:]).then_inc(late_sent, 16)
            sp.wait_ge(late_sent, 16)

        def scalar_first(act):
            act.wait_ge(zeroed, 1)
            alone(act, meta)

        def pool_first(pool):
            pool.memset(row[:, :, :, 0:4], 0.0).then_inc(zeroed, 1)
            alone(pool, send)

        def pool_last(pool):
            for r in range(2):
                pool.wait_ge(sent[r], EC // CH // 2 * CH * 16)

        def vector_first(dve):
            v = nc.vector
            order(dve, 1)
            link(dve, v.memset(late_meta[:], 0.0))
            one = lambda w: late_meta[:, :, w:w + 1].rearrange("p c o -> p (c o)")
            link(dve, v.tensor_copy(one(0).bitcast(I32), gidx[:, 1, :]))
            link(dve, v.tensor_copy(one(1), local[:, 1, :]))
            link(dve, v.tensor_copy(one(4).bitcast(I32), pos[:, 1, :]))
            v.engine_nop().then_inc(late_ready, 1)

        node_phase(nc, d, keep, 0, {
            "sync": (sync_first, lambda e: along(e, load)),
            "scalar": (scalar_first, lambda e: along(e, meta)),
            "pool": (pool_first, lambda e: along(e, send), pool_last),
            "tensor": (lambda pe: order_products(pe, 1),),
            "vector": (vector_first,),
        })


def edge_phase(nc, d, keep, name, order, heads, kind):
    C = F // heads
    attention = kind != "conv"
    attrs = kind != "gat"
    width = {"edge": 2 * F, "rel": 2 * F, "gat": F + heads, "conv": F}[kind]
    v0 = F if kind in ("edge", "rel") else 0
    meta, ao = ((0, 4), (EA, 0))[order]
    acc_w = heads * (C + 1) if attention else F
    q_scale = float(C) ** -0.5
    steps = keep["steps"][:, order, :]
    acc, q, mx = keep["acc"], keep["q"], keep["mx"]
    iota, ident, ident_b = keep["iota"], keep["ident"], keep["ident_b"]
    rec_d = d["rec"][order].rearrange("(s p g) w -> s p g w", p=P, g=G)
    fused = heads == 4
    EW = C if kind == "rel" else F
    R = 8
    with ExitStack() as ctx:
        sb = lambda n, shape, dt: ctx.enter_context(nc.sbuf_tensor(f"{name}_{n}", shape, dt))
        psum = lambda n, dt=F32: ctx.enter_context(
            nc.psum_tensor(f"{name}_{n}", [P, 512 if dt is F32 else 1024], dt))
        sem = phase_semaphores(nc, ctx, lambda n: f"{name}_{n}")
        rec = sb("rec", [P, R, G, RW], F32)
        kv = sb("kv", [P, R, G, width], F32)
        oh = sb("oh", [P, R, G, P], F32)
        oht = sb("oht", [P, R, SE], F32)
        away = sb("away", [P, 2, G, P], F32)
        mask = sb("mask", [P, R, SE], BF16)
        attrT = sb("attrT", [EA, 2, SE], F32)
        e_sb = sb("e_sb", [P, 2, G, EW], F32)
        prod = sb("prod", [P, G, F], F32)
        alpha = sb("alpha", [P, 4, G, heads], F32)
        split = sb("split", [P, 2, G, 2 * heads], BF16)
        aT = sb("aT", [2 * heads, 2, SE], BF16)
        sel = sb("sel", [2 * heads, heads, P], BF16)
        tmax = sb("tmax", [P, 2, heads], F32)
        mnew = sb("mnew", [P, 2, heads], F32)
        rise = sb("rise", [P, 2, heads], F32)
        scale = sb("scale", [P, 4, heads], F32)
        down = sb("down", [P, 2, G, heads], F32)
        pv = sb("pv", [P, 4, G, acc_w], F32)
        w_e = sb("w_e", [EA, EW], F32)
        bank_t, bank_q, bank_e, bank_o, bank_x = (psum(n) for n in ("ps_t", "ps_q", "ps_e", "ps_o", "ps_x"))
        bank_m = [psum(f"ps_m{i}") for i in range(2)]
        bank_a = psum("ps_a", BF16)
        banks_e = [bank_e, bank_e if attention else bank_m[0]]
        banks_o = [bank_o, bank_o if attention else bank_m[1]]
        ring_b = 1 if attention else 2
        away_ready = sem("away_ready")
        passed, pe_passed = sem("passed"), sem("pe_passed")
        we_in, we_scaled, sel_done = sem("we_in"), sem("we_scaled"), sem("sel_done")
        rec_in = [sem(f"rec_in{r}") for r in range(R)]
        kv_in = keep["pool_dma"]
        before = keep["edge_phases"] * (S // R) * 16 * G
        keep["edge_phases"] += 1
        gathered = lambda i, r: (i - r) * (16 * G // R) + (16 * G + before)
        scatters = kind in ("edge", "rel")
        if scatters:
            column = sb("column", [P, R, RW + 1], F32)
            column_in = [sem(f"column_in{r}") for r in range(R)]
            column_dma = keep["column_dma"]
            first_column = 0 if kind == "edge" else EC - S
            columns_before = 0 if kind == "edge" else S // R * 16
            scattered = lambda i, r: (i - r) * (16 // R) + (16 + columns_before)
            attr_d = d["edge_attr_64"].rearrange("(p c) w -> p c w", p=EP)
        oh_ready, rel_ready = sem("oh_ready"), sem("rel_ready")
        turned, oht_ready = sem("turned"), sem("oht_ready")
        q_ready, e_ready, e_copied, kv_ready = sem("q_ready"), sem("e_ready"), sem("e_copied"), sem("kv_ready")
        multiplied, alpha_ready, hi_ready, split_ready = sem("multiplied"), sem("alpha_ready"), sem("hi_ready"), sem("split_ready")
        aT_turned, aT_ready = sem("aT_turned"), sem("aT_ready")
        m_filled, m_read = sem("m_filled"), sem("m_read")
        mnew_ready, rise_ready, mx_kept = sem("mnew_ready"), sem("rise_ready"), sem("mx_kept")
        clipped = sem("clipped")
        mexp_ready, down_ready, scale_ready, p_ready = sem("mexp_ready"), sem("down_ready"), sem("scale_ready"), sem("p_ready")
        pv_ready, out_ready, acc_scaled, acc_done = sem("pv_ready"), sem("out_ready"), sem("acc_scaled"), sem("acc_done")
        by_head = lambda ap: ap.rearrange("p g (h c) -> p g h c", h=heads)
        pv_view = lambda i2: by_head(pv[:, i2])
        banks = heads // 2

        def weigh(e, i, r):
            e.wait_ge(p_ready, i + 1)
            if kind == "gat":
                e.wait_ge(kv_in[r], gathered(i, r))
            e.tensor_tensor(pv_view(r % 4)[:, :, :, 0:C], by_head(kv[:, r, :, v0:v0 + F]),
                            pv_view(r % 4)[:, :, :, C:C + 1].to_broadcast([P, G, heads, C]), ALU.mult).then_inc(pv_ready, 1)

        block = ctx.enter_context(nc.Block())

        @block.sync
        def _(sp):
            if attrs:
                if kind == "rel":
                    sp.dma_start(w_e[:], d["L1_gnn_rel_w"]).then_inc(we_in, 16)
                else:
                    sp.dma_start(w_e[:], d["L0_gnn_We" if kind == "edge" else "L3_gnn_G"]).then_inc(we_in, 16)

            def load(i, r):
                if late(i, R):
                    sp.wait_ge(oh_ready, i - (R - 1))
                    if attrs:
                        sp.wait_ge(turned, i - (R - 1))
                    sp.wait_ge(kv_in[r], gathered(i, r) - 16 * G)
                if kind in ("rel", "gat"):
                    sp.dma_start(rec[:, r, :, meta:meta + 4], rec_d[bass.ds(i, 1), :, :, meta:meta + 4].rearrange("s p g w -> (s p) g w")).then_inc(rec_in[r], 16)
                else:
                    sp.dma_start(rec[:, r], rec_d[bass.ds(i, 1)].rearrange("s p g w -> (s p) g w")).then_inc(rec_in[r], 16)

            def load_column(i, r):
                if late(i, R):
                    sp.wait_ge(column_dma[r], scattered(i, r) - 16)
                sp.dma_start(column[0:EP, r, 0:EA], attr_d[:, bass.ds(i + first_column, 1), :].rearrange("p c w -> p (c w)")).then_inc(column_in[r], 16)
                sp.dma_start(column[0:EP, r, EA:EA + 5], d["late"][:, bass.ds(i + first_column, 1), :].rearrange("p c w -> p (c w)")).then_inc(column_in[r], 16)
            pipelined(sp, S, [(0, load)] + [(0, load_column)] * scatters, R)

        @block.gpsimd
        def _(pool):
            if attention:
                pool.memset(sel[:], 0.0).then_inc(sel_done, 1)
                for k in range(2):
                    pool.wait_ge(sel_done, k + 1)
                    pool.affine_select(out=sel[:], in_=sel[:], compare_op=ALU.not_equal, fill=1.0,
                                       base=-heads * k, pattern=[[-1, heads], [0, P]],
                                       channel_multiplier=1).then_inc(sel_done, 1)

            def gather(i, r):
                pool.wait_ge(rec_in[r], landed(i, r, R))
                if late(i, R):
                    pool.wait_ge(pv_ready, i - (R - 1))
                step_aside(pool, passed)
                for g in range(G):
                    pool.indirect_dma_start(
                        kv[:, r, g, :], None, d[f"{name}_table"],
                        bass.IndirectOffsetOnAxis(ap=rec[:, r, g, meta:meta + 1].bitcast(I32), axis=0),
                    ).then_inc(kv_in[r], 16)

            def add_edge(i, r):
                pool.wait_ge(e_copied, i + 1)
                pool.wait_ge(kv_in[r], gathered(i, r))
                if kind == "edge":
                    both = kv[:, r].rearrange("p g (k f) -> p g k f", k=2)
                    nc.gpsimd.tensor_tensor(both, both, e_sb[:, r % 2].unsqueeze(2).to_broadcast([P, G, 2, F]), ALU.add).then_inc(kv_ready, 1)
                else:
                    keys = by_head(kv[:, r, :, 0:F])
                    nc.gpsimd.tensor_tensor(keys, keys, e_sb[:, r % 2].unsqueeze(2).to_broadcast([P, G, heads, C]), ALU.add).then_inc(kv_ready, 1)

            def scatter_column(i, r):
                pool.wait_ge(column_in[r], landed(i, r, R) * 2)
                step_aside(pool, passed)
                pool.indirect_dma_start(
                    d["rec"][1], bass.IndirectOffsetOnAxis(ap=column[0:EP, r, RW:RW + 1].bitcast(I32), axis=0),
                    column[0:EP, r, 0:RW], None).then_inc(column_dma[r], 16)
            pipelined(pool, S, [(0, gather)] + [(6, lambda i, r: weigh(pool, i, r))] * (kind == "gat") + [(2, add_edge), (2, scatter_column)] * scatters, R)
            if scatters:
                for r in range(R):
                    pool.wait_ge(column_dma[r], scattered(S - R + r, r))

        @block.scalar
        def _(act):
            a = nc.scalar

            def select(i, r):
                act.wait_ge(rec_in[r], landed(i, r, R))
                if late(i, R):
                    act.wait_ge(out_ready, i - (R - 1))
                for g in range(G):
                    last = a.activation(away[:, r % 2, g, :], iota[:], ACT.Abs, bias=rec[:, r, g, meta + 1:meta + 2], scale=-1.0)
                last.then_inc(away_ready, 1)
                act.wait_ge(away_ready, i + 1)
                a.activation(oh[:, r], away[:, r % 2], ACT.Relu, bias=1.0, scale=-1.0).then_inc(oh_ready, 1)

            def copy_turned(i, r):
                act.wait_ge(turned, i + 1)
                if late(i, R) and attention:
                    act.wait_ge(mexp_ready, i - (R - 1))
                if attention:
                    a.copy(oht[:, r, :], bank_t[:, 0:SE])
                    last = a.activation(mask[:, r, :], bank_t[:, 0:SE], ACT.Copy, bias=-BIG, scale=BIG)
                if attrs:
                    if late(i, 2):
                        act.wait_ge(e_ready, i - 1)
                    last = a.copy(attrT[:, r % 2, :], bank_t[0:EA, SE:2 * SE])
                last.then_inc(oht_ready, 1)

            def copy_e(i, r):
                act.wait_ge(e_ready, i + 1)
                if late(i, 2):
                    act.wait_ge(kv_ready, i - 1)
                a.copy(e_sb[:, r % 2].rearrange("p g f -> p (g f)"), bank_e[:, 0:G * EW]).then_inc(e_copied, 1)

            def scale_of(i, r):
                act.wait_ge(rise_ready, i + 1)
                if late(i, 4):
                    act.wait_ge(acc_done if fused else acc_scaled, i - 3)
                a.activation(scale[:, r % 4, :], rise[:, r % 2, :], ACT.Relu).then_inc(clipped, 1)
                act.wait_ge(clipped, i + 1)
                a.activation(scale[:, r % 4, :], scale[:, r % 4, :], ACT.Exp, scale=-1.0).then_inc(scale_ready, 1)

            def rescale_sums(i, r, b):
                act.wait_ge(scale_ready, i + 1)
                if late(i, 1):
                    act.wait_ge(acc_done, i)
                for h in range(heads):
                    cols = slice(h * (C + 1), (h + 1) * (C + 1))
                    mine = acc[:, bass.ds(b, 1), cols].rearrange("p o c -> p (o c)")
                    last = a.activation(mine, mine, ACT.Copy, scale=scale[:, r % 4, h:h + 1])
                last.then_inc(acc_scaled, 1)

            def weights(i, r):
                act.wait_ge(down_ready, i + 1)
                if late(i, 4):
                    act.wait_ge(out_ready, i - 3)
                a.activation(pv_view(r % 4)[:, :, :, C:C + 1].rearrange("p g h o -> p g (h o)"), down[:, r % 2], ACT.Exp).then_inc(p_ready, 1)

            def copy_aT(i, r):
                act.wait_ge(aT_turned, i + 1)
                if late(i, 2):
                    act.wait_ge(m_filled, (i - 1) * banks)
                a.copy(aT[:, r % 2, :], bank_a[0:2 * heads, 0:SE]).then_inc(aT_ready, 1)

            stages = [(1, copy_turned), (0, select)]
            if attention:
                stages = {
                    "edge": [(8, rescale_sums, True), (4, copy_aT), (2, copy_e), (6, scale_of), (6, weights), (1, copy_turned), (0, select)],
                    "rel": [(2, copy_e), (4, copy_aT), (6, scale_of), (6, weights), (1, copy_turned), (0, select)],
                    "gat": [(4, copy_aT), (6, scale_of), (6, weights), (0, select), (1, copy_turned)],
                }[kind]
            pipelined(act, S, stages, R, steps)

        @block.tensor
        def _(pe):
            t = nc.tensor
            if attrs:
                pe.wait_ge(we_scaled, 1)
            if attention:
                pe.wait_ge(sel_done, 3)

            def fill_max(i, r, these):
                pe.wait_ge(aT_ready, i + 1)
                for b in these:
                    if late(i, 1) or b >= 2:
                        pe.wait_ge(m_read, i * banks + (b - 1))
                    bank = bank_m[b % 2]
                    t.matmul(bank[:].rearrange("p (h e) -> p h e", h=2), ident_b[:],
                             mask[:, r, :].unsqueeze(1).to_broadcast([P, 2, SE]), start=True, stop=False)
                    for h in range(2):
                        last = t.matmul(bank[:, h * SE:(h + 1) * SE], sel[:, 2 * b + h, :], aT[:, r % 2, :],
                                        start=False, stop=h == 1)
                    last.then_inc(m_filled, 1)

            def turn_edges(i, r):
                pe.wait_ge(oh_ready, i + 1)
                if attrs:
                    pe.wait_ge(rel_ready if kind == "rel" else rec_in[r], i + 1 if kind == "rel" else landed(i, r, R))
                if late(i, 1):
                    pe.wait_ge(oht_ready, i)
                if not attention:
                    step_aside(pe, pe_passed)
                for g in range(G):
                    if attention:
                        last = t.transpose(bank_t[:, g * P:(g + 1) * P], oh[:, r, g, :], ident[:])
                    if attrs:
                        last = t.transpose(bank_t[0:EA, SE + g * P:SE + (g + 1) * P], rec[:, r, g, ao:ao + EA], ident[:])
                last.then_inc(turned, 1)

            def sum_nodes(i, r):
                pe.wait_ge(pv_ready, i + 1)
                if late(i, ring_b):
                    pe.wait_ge(acc_done, i - (ring_b - 1))
                for g in range(G):
                    last = t.matmul(banks_o[r % 2][:, 0:acc_w], oh[:, r, g, :], pv[:, r % 4, g, :], start=g == 0, stop=g == G - 1)
                last.then_inc(out_ready, 1)

            def spread_max(i, r):
                pe.wait_ge(mnew_ready, i + 1)
                if late(i, 1):
                    pe.wait_ge(down_ready, i)
                for g in range(G):
                    last = t.matmul(bank_x[:, g * heads:(g + 1) * heads], oht[:, r, g * P:(g + 1) * P],
                                    mnew[:, r % 2, :], start=True, stop=True)
                last.then_inc(mexp_ready, 1)

            def products(i, r, *b):
                pe.wait_ge(oht_ready, i + 1)
                if attrs:
                    if late(i, ring_b):
                        pe.wait_ge(pv_ready if kind == "conv" else e_copied, i - (ring_b - 1))
                    for g in range(G):
                        last = t.matmul(banks_e[r % 2][:, g * EW:(g + 1) * EW], attrT[:, r % 2, g * P:(g + 1) * P], w_e[:],
                                        start=True, stop=True)
                    last.then_inc(e_ready, 1)
                if attention:
                    if late(i, 1):
                        pe.wait_ge(multiplied, i)
                    w = F if kind != "gat" else heads
                    for g in range(G):
                        last = t.matmul(bank_q[:, g * w:(g + 1) * w], oht[:, r, g * P:(g + 1) * P],
                                        q[:, bass.ds(b[0], 1), 0:w].rearrange("p o f -> p (o f)"), start=True, stop=True)
                    last.then_inc(q_ready, 1)

            def turn_scores(i, r):
                pe.wait_ge(split_ready, i + 1)
                if late(i, 1):
                    pe.wait_ge(aT_ready, i)
                for g in range(G):
                    last = t.transpose(bank_a[0:2 * heads, g * P:(g + 1) * P], split[:, r % 2, g, :], ident_b[:])
                last.then_inc(aT_turned, 1)

            if attention:
                early = lambda i, r: fill_max(i, r, range(2))
                later = lambda i, r: fill_max(i, r, range(2, banks))
                last_two = [(7, sum_nodes), (1, turn_edges)] if kind == "rel" else [(1, turn_edges), (7, sum_nodes)]
                pipelined(pe, S, [(5, early), (6, spread_max), (4, turn_scores), (2, products, True)]
                          + [(5, later)] * (banks > 2) + last_two, R, steps)
            else:
                pipelined(pe, S, [(2, products), (1, turn_edges), (4, sum_nodes)], R)

        @block.vector
        def _(dve):
            v = nc.vector
            if attrs:
                dve.wait_ge(we_in, 16)
                v.tensor_scalar(w_e[:], w_e[:], 0.2 if kind == "rel" else 1.0, None, ALU.mult).then_inc(we_scaled, 1)

            def select_relation(i, r):
                dve.wait_ge(rec_in[r], landed(i, r, R))
                v.tensor_tensor(rec[:, r, :, ao:ao + EA], iota[:, 0:EA].unsqueeze(1).to_broadcast([P, G, EA]),
                                rec[:, r, :, meta + 2:meta + 3].to_broadcast([P, G, EA]), ALU.is_equal).then_inc(rel_ready, 1)

            def multiply(i, r):
                dve.wait_ge(e_ready, i + 1)
                dve.wait_ge(kv_in[r], gathered(i, r))
                if late(i, 4):
                    dve.wait_ge(out_ready, i - 3)
                v.tensor_tensor(pv[:, r % 4], kv[:, r], banks_e[r % 2][:].rearrange("p (g f) -> p g f", g=G), ALU.mult).then_inc(pv_ready, 1)

            def acc_of(b):
                return acc[:, bass.ds(b, 1), 0:acc_w].rearrange("p o (h c) -> p (o h) c", h=heads)

            def accumulate(i, r, b):
                dve.wait_ge(out_ready, i + 1)
                if fused:
                    dve.wait_ge(scale_ready, i + 1)
                    if late(i, 1):
                        dve.wait_ge(acc_done, i)
                    for h in range(heads):
                        cols = slice(h * (C + 1), (h + 1) * (C + 1))
                        mine = acc[:, bass.ds(b, 1), cols].rearrange("p o c -> p (o c)")
                        last = v.scalar_tensor_tensor(out=mine, in0=mine, scalar=scale[:, r % 4, h:h + 1], in1=bank_o[:, cols],
                                                      op0=ALU.mult, op1=ALU.add)
                    last.then_inc(acc_done, 1)
                elif attention:
                    mine = acc_of(b)
                    dve.wait_ge(acc_scaled, i + 1)
                    v.tensor_tensor(mine, mine, bank_o[:, 0:acc_w].rearrange("p (h c) -> p h c", h=heads), ALU.add).then_inc(acc_done, 1)
                else:
                    if late(i, 1):
                        dve.wait_ge(acc_done, i)
                    mine = acc[:, bass.ds(b, 1), 0:acc_w].rearrange("p o f -> p (o f)")
                    v.tensor_tensor(mine, mine, banks_o[r % 2][:, 0:acc_w], ALU.add).then_inc(acc_done, 1)

            def reduce_banks(i, r, these):
                for k in these:
                    dve.wait_ge(m_filled, i * banks + (k + 1))
                    if k == 0 and late(i, 2):
                        dve.wait_ge(mnew_ready, i - 1)
                    v.tensor_reduce(tmax[:, r % 2, 2 * k:2 * k + 2], bank_m[k % 2][:].rearrange("p (h e) -> p h e", h=2),
                                    AX.X, ALU.max).then_inc(m_read, 1)

            def new_maximum(i, r, b):
                dve.wait_ge(m_read, (i + 1) * banks)
                old = mx[:, bass.ds(b, 1), 0:heads].rearrange("p o h -> p (o h)")
                if late(i, 1):
                    dve.wait_ge(mx_kept, i)
                if late(i, 2):
                    dve.wait_ge(mexp_ready, i - 1)
                    dve.wait_ge(scale_ready, i - 1)
                v.tensor_tensor(mnew[:, r % 2, :], old, tmax[:, r % 2, :], ALU.max).then_inc(mnew_ready, 1)
                v.tensor_tensor(rise[:, r % 2, :], tmax[:, r % 2, :], old, ALU.subtract).then_inc(rise_ready, 1)
                v.tensor_tensor(old, old, tmax[:, r % 2, :], ALU.max).then_inc(mx_kept, 1)

            def score(i, r):
                dve.wait_ge(q_ready, i + 1)
                if late(i, 1):
                    dve.wait_ge(alpha_ready, i)
                if kind == "gat":
                    dve.wait_ge(kv_in[r], gathered(i, r))
                    part = prod[:, :, 0:heads]
                    v.tensor_tensor(part, kv[:, r, :, F:F + heads], bank_q[:, 0:G * heads].rearrange("p (g h) -> p g h", g=G),
                                    ALU.add).then_inc(multiplied, 1)
                else:
                    dve.wait_ge(kv_ready, i + 1)
                    v.scalar_tensor_tensor(out=prod[:], in0=bank_q[:].rearrange("p (g f) -> p g f", g=G), scalar=q_scale,
                                           in1=kv[:, r, :, 0:F], op0=ALU.mult, op1=ALU.mult).then_inc(multiplied, 1)

            def finish_score(i, r):
                dve.wait_ge(multiplied, i + 1)
                if late(i, 4):
                    dve.wait_ge(down_ready, i - 3)
                if kind == "gat":
                    v.scalar_tensor_tensor(out=alpha[:, r % 4], in0=prod[:, :, 0:heads], scalar=0.2, in1=prod[:, :, 0:heads], op0=ALU.mult, op1=ALU.max).then_inc(alpha_ready, 1)
                else:
                    v.tensor_reduce(alpha[:, r % 4].rearrange("p g h -> p (g h)"),
                                    prod[:].rearrange("p g (h c) -> p (g h) c", h=heads), AX.X, ALU.add).then_inc(alpha_ready, 1)

            def split_scores(i, r):
                dve.wait_ge(alpha_ready, i + 1)
                if late(i, 2):
                    dve.wait_ge(aT_turned, i - 1)
                v.tensor_copy(split[:, r % 2, :, 0:heads], alpha[:, r % 4]).then_inc(hi_ready, 1)

            def split_rest(i, r):
                dve.wait_ge(hi_ready, i + 1)
                v.tensor_tensor(split[:, r % 2, :, heads:2 * heads], alpha[:, r % 4], split[:, r % 2, :, 0:heads], ALU.subtract).then_inc(split_ready, 1)

            def lower(i, r):
                dve.wait_ge(mexp_ready, i + 1)
                if late(i, 2):
                    dve.wait_ge(p_ready, i - 1)
                v.tensor_tensor(down[:, r % 2], alpha[:, r % 4], bank_x[:, 0:G * heads].rearrange("p (g h) -> p g h", g=G),
                                ALU.subtract).then_inc(down_ready, 1)

            if attention:
                early = lambda i, r: reduce_banks(i, r, range(2))
                later = lambda i, r: reduce_banks(i, r, range(2, banks))
                weigh_values = lambda i, r: weigh(v, i, r)
                stages = {
                    "edge": [(3, score), (6, lower), (5, early), (8, accumulate, True), (3, finish_score), (6, weigh_values), (5, later),
                             (3, split_scores), (5, new_maximum, True), (3, split_rest)],
                    "rel": [(3, score), (8, accumulate, True), (6, lower), (5, early), (3, finish_score), (6, weigh_values),
                            (3, split_scores), (5, new_maximum, True), (3, split_rest), (0, select_relation)],
                    "gat": [(3, score), (3, finish_score), (8, accumulate, True), (6, lower), (3, split_scores), (5, early),
                            (3, split_rest), (5, new_maximum, True)],
                }[kind]
                pipelined(dve, S, stages, R, steps)
            else:
                pipelined(dve, S, [(3, multiply), (5, accumulate, True)], R, steps)


def node_phase(nc, d, keep, layer, beside=None):
    acc, q, mx, ident = keep.get("acc"), keep["q"], keep.get("mx"), keep["ident"]
    adds = layer in (1, 3)
    heads_before, heads = (0, 8, 4, 4)[layer], (8, 4, 4, 1)[layer]
    x_in, x_out = d["xs"][layer], d["xs_updated"][layer]
    weights = ([("L0_gnn_Wq", "L0_gnn_bq"), ("L0_gnn_Wskip", "L0_gnn_bskip"), ("L0_gnn_Wk", "L0_gnn_bk"), ("L0_gnn_Wv", "L0_gnn_bv")],
               [("L1_gnn_Wq", "L1_gnn_bq"), ("L1_gnn_Wk", "L1_gnn_bk"), ("L1_gnn_Wv", "L1_gnn_bv")],
               [("L2_gnn_W", None)],
               [("L3_gnn_Wi", "L3_gnn_bi"), ("L3_gnn_Wj", "L3_gnn_bj")])[layer]
    first_bank = (2, 1, 1, 2)[layer]
    W = len(weights)
    width = (2 * F, 2 * F, F + 4, F)[layer]
    K = F // P
    R = 8
    name = f"n{layer}"
    more = layer in (1, 3)
    RH = R if layer == 1 else 4
    beside = beside or {}

    def first(e, engine):
        if engine in beside:
            beside[engine][0](e)

    def along(e, engine):
        return beside[engine][1](e) if len(beside.get(engine, ())) > 1 else []

    def last_of_all(e, engine):
        if len(beside.get(engine, ())) > 2:
            beside[engine][2](e)

    with ExitStack() as ctx:
        sb = lambda n, shape, dt=F32: ctx.enter_context(nc.sbuf_tensor(f"{name}_{n}", shape, dt))
        sem = phase_semaphores(nc, ctx, lambda n: f"{name}_{n}")
        psum = lambda n: ctx.enter_context(nc.psum_tensor(f"{name}_{n}", [P, 512], F32))
        w = sb("w", [P, W, K, F])
        bias = sb("bias", [P, W, F])
        extra = sb("extra", [P, 2, F]) if layer in (1, 2) else None
        x = sb("x", [P, R, F])
        stats = sb("stats", [P, 2, 6])
        mean = sb("mean", [P, 2, 2])
        rstd = sb("rstd", [P, 2, 1])
        inv = sb("inv", [P, 2, 8])
        part = sb("part", [P, 2, F]) if adds else None
        hn = sb("hn", [P, 2, F])
        h = sb("h", [P, RH, F])
        h2 = sb("h2", [P, 2, F]) if more else None
        expd = sb("expd", [P, 2, F]) if layer == 3 else None
        hT = sb("hT", [P, 2, K, P])
        row = sb("row", [P, R, width])
        made = sb("made", [P, 2, 2 * F])
        made2 = sb("made2", [P, 2, 2 * F]) if layer in (2, 3) else None
        same = sb("same", [P, F], I32) if layer == 2 else None
        xi = sb("xi", [P, R, F]) if layer == 3 else None
        bank_t = psum("ps_t")
        banks = [[psum(f"ps_{b}{r}") for r in range(2)] for b in range(2)]
        eps_added, passed, pool_passed = sem("eps_added"), sem("passed"), sem("pool_passed")
        w_in, extra_ready = sem("w_in"), sem("extra_ready")
        x_in_sem = [sem(f"x_in{r}") for r in range(R)]
        x_sent = [sem(f"x_sent{r}") for r in range(R)]
        xi_sent = [sem(f"xi_sent{r}") for r in range(R)]
        h_sent = [sem(f"h_sent{r}") for r in range(R)]
        row_sent = [sem(f"row_sent{r}") for r in range(R)]
        s_ready, inv_ready, part_ready, x_ready = sem("s_ready"), sem("inv_ready"), sem("part_ready"), sem("x_ready")
        cleared, stats_ready, mean_ready, rstd_ready = sem("cleared"), sem("stats_ready"), sem("mean_ready"), sem("rstd_ready")
        hn_ready, h_ready, h2_ready, exp_ready, ln_ready = sem("hn_ready"), sem("h_ready"), sem("h2_ready"), sem("exp_ready"), sem("ln_ready")
        turned, hT_ready, product_ready = sem("turned"), sem("hT_ready"), sem("product_ready")
        evacuated, row_ready, chain = sem("evacuated"), sem("row_ready"), sem("chain")
        if layer in (0, 1):
            row_ready = evacuated
        abs_ready, made_exp, made_ln = sem("abs_ready"), sem("made_exp"), sem("made_ln")
        block = ctx.enter_context(nc.Block())
        rows = lambda t, i: t[bass.ds(i * P, P), :]
        operand_ready = h2_ready if more else h_ready

        @block.sync
        def _(sp):
            for n, (wn, bn) in enumerate(weights):
                sp.dma_start(w[:, n], d[wn].rearrange("(k p) f -> p k f", p=P)).then_inc(w_in, 16)
                if bn:
                    sp.dma_start(bias[:, n], d[bn].partition_broadcast(P)).then_inc(w_in, 16)
            if layer == 1:
                sp.dma_start(extra[:, 0], d["L1_gnn_query_emb"].partition_broadcast(P)).then_inc(w_in, 16)
            if layer == 2:
                for n, an in enumerate(("L2_gnn_a_l", "L2_gnn_a_r")):
                    sp.dma_start(extra[:, n], d[an].rearrange("o h c -> (o h c)").partition_broadcast(P)).then_inc(w_in, 16)

            first(sp, "sync")

            def load(i, r):
                if late(i, R):
                    sp.wait_ge(hn_ready, i - (R - 1))
                    if x_out is not None:
                        sp.wait_ge(x_sent[r], (i - r) * (16 // R))
                sp.dma_start(x[:, r], rows(x_in, i)).then_inc(x_in_sem[r], 16)
            pipelined(sp, NB, [(0, load)] + along(sp, "sync"), R)

        loads = 16 * (sum(1 + bool(bn) for _, bn in weights) + (0, 1, 2, 0)[layer])

        @block.gpsimd
        def _(pool):
            first(pool, "pool")

            def clear(i, r):
                if adds:
                    pool.wait_ge(part_ready, i + 1)
                if layer != 2:
                    nc.gpsimd.tensor_copy(acc[:, bass.ds(i, 1), :], keep["zeros"][:].unsqueeze(1))
                nc.gpsimd.tensor_copy(mx[:, bass.ds(i, 1), :], keep["lowest"][:].unsqueeze(1)).then_inc(cleared, 1)

            def inverse_deviation(i, r):
                pool.wait_ge(mean_ready, i + 1)
                step_aside(pool, pool_passed)
                nc.gpsimd.tensor_scalar(rstd[:, r % 2], mean[:, r % 2, 1:2], 1e-5, None, ALU.add).then_inc(eps_added, 1)
                pool.wait_ge(eps_added, i + 1)
                nc.gpsimd.tensor_tensor(rstd[:, r % 2], rstd[:, r % 2], keep["minus_half"][:], ALU.pow).then_inc(rstd_ready, 1)

            pipelined(pool, NB, [(0, inverse_deviation)] + [(0, clear)] * (layer != 0) + along(pool, "pool"), R)
            last_of_all(pool, "pool")

        @block.tensor
        def _(pe):
            t = nc.tensor
            first(pe, "tensor")
            pe.wait_ge(w_in, loads)

            def turn(i, r):
                pe.wait_ge(operand_ready, i + 1)
                if late(i, 1):
                    pe.wait_ge(hT_ready, i)
                src = h2[:, r % 2] if more else h[:, r % RH]
                for k in range(K):
                    last = t.transpose(bank_t[:, k * P:(k + 1) * P], src[:, k * P:(k + 1) * P], ident[:])
                last.then_inc(turned, 1)

            def multiply(i, r):
                pe.wait_ge(hT_ready, i + 1)
                if late(i, 2):
                    pe.wait_ge(evacuated, i - 1)
                for n in range(W):
                    bank = banks[n >= first_bank][r % 2]
                    c = n - first_bank * (n >= first_bank)
                    for k in range(K):
                        last = t.matmul(bank[:, c * F:(c + 1) * F], hT[:, r % 2, k, :], w[:, n, k, :],
                                        start=k == 0, stop=k == K - 1)
                last.then_inc(product_ready, 1)
            pipelined(pe, NB, [(4 + more, multiply), (3 + more, turn)], R)

        @block.scalar
        def _(act):
            a = nc.scalar
            first(act, "scalar")
            if layer == 3:
                a.preload_act_table_set("natural_log_exp_and_others")

            def relu(i, r):
                act.wait_ge(hn_ready, i + 1)
                if late(i, RH):
                    act.wait_ge(turned, i - (RH - 1))
                    if layer == 1:
                        act.wait_ge(h_sent[r], (i - r) * (16 // R))
                a.activation(h[:, r % RH], hn[:, r % 2], ACT.Relu).then_inc(h_ready, 1)
                if layer == 3:
                    if late(i, 2):
                        act.wait_ge(h2_ready, i - 1)
                    act.wait_ge(h_ready, i + 1)
                    a.activation(expd[:, r % 2], h[:, r % RH], ACT.Exp, scale=-1.0).then_inc(exp_ready, 1)
                    act.wait_ge(exp_ready, i + 1)
                    a.activation(expd[:, r % 2], expd[:, r % 2], ACT.Ln, bias=1.0).then_inc(ln_ready, 1)

            def copy_hT(i, r):
                act.wait_ge(turned, i + 1)
                if late(i, 2):
                    act.wait_ge(product_ready, i - 1)
                a.copy(hT[:, r % 2].rearrange("p k n -> p (k n)"), bank_t[:, 0:F]).then_inc(hT_ready, 1)

            def soften(i, r):
                act.wait_ge(evacuated, i + 1)
                if late(i, 2):
                    act.wait_ge(row_ready, i - 1)
                a.activation(made2[:, r % 2], made[:, r % 2], ACT.Abs).then_inc(abs_ready, 1)
                act.wait_ge(abs_ready, i + 1)
                a.activation(made2[:, r % 2], made2[:, r % 2], ACT.Exp, scale=-1.0).then_inc(made_exp, 1)
                act.wait_ge(made_exp, i + 1)
                a.activation(made2[:, r % 2], made2[:, r % 2], ACT.Ln, bias=1.0).then_inc(made_ln, 1)

            def send_x(i, r):
                act.wait_ge(x_ready, i + 1)
                act.dma_start(rows(x_out, i), x[:, r]).then_inc(x_sent[r], 16)

            def send(i, r):
                act.wait_ge(row_ready, i + 1)
                act.dma_start(rows(d[f"L{layer}_table"], i), row[:, r]).then_inc(row_sent[r], 16)
                if layer == 0:
                    act.dma_start(rows(x_out, i), x[:, r]).then_inc(x_sent[r], 16)
                if layer == 1:
                    act.dma_start(rows(d["h1"], i), h[:, r % RH]).then_inc(h_sent[r], 16)
                if layer == 3:
                    act.dma_start(rows(d["xi"], i), xi[:, r]).then_inc(xi_sent[r], 16)
            pipelined(act, NB, [(2, relu), (3 + more, copy_hT)] + [(6, soften)] * (layer == 3) + [(8, send)] + [(1, send_x)] * adds
                      + along(act, "scalar"), R)
            for r in range(R):
                blocks = len(range(r, NB, R))
                act.wait_ge(row_sent[r], 16 * blocks)
                if layer != 2:
                    act.wait_ge(x_sent[r], 16 * blocks)
                if layer == 1:
                    act.wait_ge(h_sent[r], 16 * blocks)
                if layer == 3:
                    act.wait_ge(xi_sent[r], 16 * blocks)

        @block.vector
        def _(dve):
            v = nc.vector
            first(dve, "vector")
            dve.wait_ge(w_in, loads)
            if layer == 1:
                v.tensor_scalar(extra[:, 0], extra[:, 0], 0.1, None, ALU.mult).then_inc(extra_ready, 1)
                dve.wait_ge(extra_ready, 1)

            def deviation(i, r):
                dve.wait_ge(x_in_sem[r], landed(i, r, R))
                xr, two = x[:, r], r % 2
                if adds:
                    H = heads_before
                    C = F // H
                    mine = acc[:, bass.ds(i, 1), 0:H * (C + 1)].rearrange("p o (h c) -> p (o h) c", h=H)
                    v.tensor_scalar(inv[:, two, 0:H].unsqueeze(2), mine[:, :, C:C + 1], 1e-16, None, ALU.add).then_inc(s_ready, 1)
                    dve.wait_ge(s_ready, i + 1)
                    v.reciprocal(inv[:, two, 0:H], inv[:, two, 0:H]).then_inc(inv_ready, 1)
                    dve.wait_ge(inv_ready, i + 1)
                    v.tensor_tensor(part[:, two].rearrange("p (h c) -> p h c", h=H), mine[:, :, 0:C],
                                    inv[:, two, 0:H].unsqueeze(2).to_broadcast([P, H, C]), ALU.mult).then_inc(part_ready, 1)
                    dve.wait_ge(part_ready, i + 1)
                    v.tensor_tensor(xr, xr, part[:, two], ALU.add).then_inc(x_ready, 1)
                    dve.wait_ge(x_ready, i + 1)
                v.bn_stats(stats[:, two], xr).then_inc(stats_ready, 1)
                dve.wait_ge(stats_ready, i + 1)
                step_aside(dve, passed)
                v.bn_aggr(mean[:, two], stats[:, two]).then_inc(mean_ready, 1)

            def normalise(i, r):
                two = r % 2
                dve.wait_ge(mean_ready, i + 1)
                dve.wait_ge(rstd_ready, i + 1)
                if late(i, 2):
                    dve.wait_ge(h_ready, i - 1)
                v.tensor_scalar(hn[:, two], x[:, r], mean[:, two, 0:1], rstd[:, two], ALU.subtract, ALU.mult).then_inc(hn_ready, 1)

            def operand(i, r):
                dve.wait_ge(ln_ready if layer == 3 else h_ready, i + 1)
                if late(i, 2):
                    dve.wait_ge(turned, i - 1)
                if layer == 1:
                    v.tensor_tensor(h2[:, r % 2], h[:, r % RH], extra[:, 0], ALU.add).then_inc(h2_ready, 1)
                else:
                    v.scalar_tensor_tensor(out=h2[:, r % 2], in0=h[:, r % RH], scalar=-0.6931471805599453, in1=expd[:, r % 2],
                                           op0=ALU.add, op1=ALU.add).then_inc(h2_ready, 1)

            def make(i, r):
                dve.wait_ge(product_ready, i + 1)
                if late(i, R):
                    dve.wait_ge(row_sent[r], (i - r) * (16 // R))
                b0, b1 = banks[0][r % 2], banks[1][r % 2]
                mine = q[:, bass.ds(i, 1), :].rearrange("p o f -> p (o f)")
                if layer in (0, 1):
                    v.tensor_tensor(mine, b0[:, 0:F], bias[:, 0], ALU.add)
                    if layer == 0:
                        v.tensor_tensor(made[:, r % 2, 0:F], b0[:, F:2 * F], bias[:, 1], ALU.add).then_inc(chain, 1)
                        dve.wait_ge(chain, i + 1)
                        v.tensor_tensor(x[:, r], x[:, r], made[:, r % 2, 0:F], ALU.add)
                    v.tensor_tensor(row[:, r], b1[:], bias[:, W - 2:W].rearrange("p a f -> p (a f)"), ALU.add).then_inc(evacuated, 1)
                if layer == 2:
                    hm, one = made[:, 0, 0:F], made[:, 1, 0:F]
                    if late(i, 1):
                        dve.wait_ge(row_ready, i)
                    v.memset(hm, 0.0).then_inc(chain, 1)
                    v.tensor_copy(one, b0[:, 0:F]).then_inc(chain, 1)
                    dve.wait_ge(chain, i * 5 + 2)
                    v.tensor_tensor(same[:], one, one, ALU.is_equal).then_inc(chain, 1)
                    dve.wait_ge(chain, i * 5 + 3)
                    step_aside(dve, passed)
                    v.copy_predicated(hm, same[:], one).then_inc(evacuated, 1)
                    dve.wait_ge(evacuated, i + 1)
                    v.tensor_copy(row[:, r, 0:F], hm)
                    for n in range(2):
                        out = (mine[:, 0:4], row[:, r, F:F + 4])[n]
                        v.tensor_tensor(made2[:, n, 0:F], hm, extra[:, n], ALU.mult).then_inc(chain, 1)
                        dve.wait_ge(chain, i * 5 + (4 + n))
                        last = v.tensor_reduce(out, made2[:, n, 0:F].rearrange("p (h c) -> p h c", h=4), AX.X, ALU.add)
                    last.then_inc(row_ready, 1)
                if layer == 3:
                    if late(i, 2):
                        dve.wait_ge(row_ready, i - 1)
                    v.tensor_tensor(made[:, r % 2], b0[:], bias[:].rearrange("p a f -> p (a f)"), ALU.add).then_inc(evacuated, 1)

            def finish(i, r):
                dve.wait_ge(made_ln, i + 1)
                if late(i, R):
                    dve.wait_ge(xi_sent[r], (i - r) * (16 // R))
                v.scalar_tensor_tensor(out=xi[:, r], in0=made[:, r % 2, 0:F], scalar=0.0, in1=made2[:, r % 2, 0:F], op0=ALU.max, op1=ALU.add)
                v.scalar_tensor_tensor(out=row[:, r], in0=made[:, r % 2, F:2 * F], scalar=0.0, in1=made2[:, r % 2, F:2 * F],
                                       op0=ALU.max, op1=ALU.add).then_inc(row_ready, 1)

            pipelined(dve, NB, [(5 + more, make)] + [(7, finish)] * (layer == 3)
                      + [(3, operand)] * more + [(1, normalise), (0, deviation)], R)


def relational_out_phase(nc, d, keep):
    acc, ident = keep["acc"], keep["ident"]
    H, K, R = 4, F // P, 8
    C = F // H
    with ExitStack() as ctx:
        sb = lambda n, shape, dt=F32: ctx.enter_context(nc.sbuf_tensor(f"o1_{n}", shape, dt))
        sem = phase_semaphores(nc, ctx, lambda n: f"o1_{n}")
        psum = lambda n: ctx.enter_context(nc.psum_tensor(f"o1_{n}", [P, 512], F32))
        w = sb("w", [P, K, F])
        vec = sb("vec", [P, 3, F])
        value, h, x = (sb(n, [P, R, F]) for n in ("value", "h", "x"))
        none = sb("none", [P, 2, H])
        inv = sb("inv", [P, 2, H])
        msg, own, y = (sb(n, [P, 2, F]) for n in ("msg", "own", "y"))
        msgT = sb("msgT", [P, 2, K, P])
        stats = sb("stats", [P, 2, 6])
        mean = sb("mean", [P, 2, 2])
        rstd = sb("rstd", [P, 2, 1])
        bank_t = psum("ps_t")
        bank_y = [psum(f"ps_y{r}") for r in range(2)]
        w_in = sem("w_in")
        tiles_in = [sem(f"tiles_in{r}") for r in range(R)]
        sent = [sem(f"sent{r}") for r in range(R)]
        head, msg_ready, turned, msgT_ready, product_ready = (sem(n) for n in ("head", "msg_ready", "turned", "msgT_ready", "product_ready"))
        eps_added, passed, pool_passed = sem("eps_added"), sem("passed"), sem("pool_passed")
        mean_ready, rstd_ready = sem("mean_ready"), sem("rstd_ready")
        summing, scaling, x_ready, cleared = sem("summing"), sem("scaling"), sem("x_ready"), sem("cleared")
        block = ctx.enter_context(nc.Block())
        rows = lambda t, i: t[bass.ds(i * P, P), :]

        @block.sync
        def _(sp):
            sp.dma_start(w[:], d["L1_gnn_Wo"].rearrange("(k p) f -> p k f", p=P)).then_inc(w_in, 16)
            for n, name in enumerate(("L1_gnn_bo", "L1_gnn_gamma", "L1_gnn_beta")):
                sp.dma_start(vec[:, n], d[name].partition_broadcast(P)).then_inc(w_in, 16)

            def load(i, r):
                if late(i, R):
                    sp.wait_ge(sent[r], (i - r) * (16 // R))
                sp.dma_start(value[:, r], rows(d["L1_table"], i)[:, F:2 * F]).then_inc(tiles_in[r], 16)
                sp.dma_start(h[:, r], rows(d["h1"], i)).then_inc(tiles_in[r], 16)
                sp.dma_start(x[:, r], rows(d["xs"][2], i)).then_inc(tiles_in[r], 16)
            pipelined(sp, NB, [(0, load)], R)

        @block.gpsimd
        def _(pool):
            def clear(i, r):
                pool.wait_ge(msg_ready, i + 1)
                nc.gpsimd.tensor_copy(acc[:, bass.ds(i, 1), :], keep["zeros"][:].unsqueeze(1)).then_inc(cleared, 1)

            def inverse_deviation(i, r):
                pool.wait_ge(mean_ready, i + 1)
                step_aside(pool, pool_passed)
                nc.gpsimd.tensor_scalar(rstd[:, r % 2], mean[:, r % 2, 1:2], 1e-5, None, ALU.add).then_inc(eps_added, 1)
                pool.wait_ge(eps_added, i + 1)
                nc.gpsimd.tensor_tensor(rstd[:, r % 2], rstd[:, r % 2], keep["minus_half"][:], ALU.pow).then_inc(rstd_ready, 1)
            pipelined(pool, NB, [(3, inverse_deviation), (0, clear)], R)

        @block.tensor
        def _(pe):
            t = nc.tensor
            pe.wait_ge(w_in, 64)

            def turn(i, r):
                pe.wait_ge(msg_ready, i + 1)
                if late(i, 1):
                    pe.wait_ge(msgT_ready, i)
                for k in range(K):
                    last = t.transpose(bank_t[:, k * P:(k + 1) * P], msg[:, r % 2, k * P:(k + 1) * P], ident[:])
                last.then_inc(turned, 1)

            def multiply(i, r):
                pe.wait_ge(msgT_ready, i + 1)
                if late(i, 2):
                    pe.wait_ge(summing, i * 3 - 5)
                for k in range(K):
                    last = t.matmul(bank_y[r % 2][:, 0:F], msgT[:, r % 2, k, :], w[:, k, :], start=k == 0, stop=k == K - 1)
                last.then_inc(product_ready, 1)
            pipelined(pe, NB, [(2, multiply), (1, turn)], R)

        @block.scalar
        def _(act):
            def copy_msgT(i, r):
                act.wait_ge(turned, i + 1)
                if late(i, 2):
                    act.wait_ge(product_ready, i - 1)
                nc.scalar.copy(msgT[:, r % 2].rearrange("p k n -> p (k n)"), bank_t[:, 0:F]).then_inc(msgT_ready, 1)

            def send(i, r):
                act.wait_ge(x_ready, i + 1)
                act.dma_start(rows(d["xs"][2], i), x[:, r]).then_inc(sent[r], 16)
            pipelined(act, NB, [(1, copy_msgT), (5, send)], R)
            for r in range(R):
                act.wait_ge(sent[r], 16 * len(range(r, NB, R)))

        @block.vector
        def _(dve):
            v = nc.vector
            dve.wait_ge(w_in, 64)

            def message(i, r):
                dve.wait_ge(tiles_in[r], (i - r) * (48 // R) + 48)
                two = r % 2
                mine = acc[:, bass.ds(i, 1), 0:H * (C + 1)].rearrange("p o (h c) -> p (o h) c", h=H)
                by_head = lambda ap: ap.rearrange("p (h c) -> p h c", h=H)
                wide = lambda ap: ap.unsqueeze(2).to_broadcast([P, H, C])
                v.tensor_scalar(none[:, two].unsqueeze(2), mine[:, :, C:C + 1], 0.0, None, ALU.is_equal).then_inc(head, 1)
                dve.wait_ge(head, i * 5 + 1)
                v.tensor_tensor(inv[:, two].unsqueeze(2), mine[:, :, C:C + 1], none[:, two].unsqueeze(2), ALU.add).then_inc(head, 1)
                dve.wait_ge(head, i * 5 + 2)
                v.reciprocal(inv[:, two], inv[:, two]).then_inc(head, 1)
                dve.wait_ge(head, i * 5 + 3)
                if late(i, 2):
                    dve.wait_ge(turned, i - 1)
                v.tensor_tensor(by_head(msg[:, two]), mine[:, :, 0:C], wide(inv[:, two]), ALU.mult).then_inc(head, 1)
                v.tensor_tensor(by_head(own[:, two]), by_head(value[:, r]), wide(none[:, two]), ALU.mult).then_inc(head, 1)
                dve.wait_ge(head, i * 5 + 5)
                v.tensor_tensor(msg[:, two], msg[:, two], own[:, two], ALU.add).then_inc(msg_ready, 1)

            def residual(i, r):
                two = r % 2
                dve.wait_ge(product_ready, i + 1)
                if late(i, 2):
                    dve.wait_ge(x_ready, i - 1)
                v.tensor_tensor(y[:, two], bank_y[two][:, 0:F], h[:, r], ALU.add).then_inc(summing, 1)
                dve.wait_ge(summing, i * 3 + 1)
                v.tensor_tensor(y[:, two], y[:, two], vec[:, 0], ALU.add).then_inc(summing, 1)
                dve.wait_ge(summing, i * 3 + 2)
                v.bn_stats(stats[:, two], y[:, two]).then_inc(summing, 1)
                dve.wait_ge(summing, i * 3 + 3)
                step_aside(dve, passed)
                v.bn_aggr(mean[:, two], stats[:, two]).then_inc(mean_ready, 1)

            def finish(i, r):
                two = r % 2
                dve.wait_ge(rstd_ready, i + 1)
                v.tensor_scalar(y[:, two], y[:, two], mean[:, two, 0:1], rstd[:, two], ALU.subtract, ALU.mult).then_inc(scaling, 1)
                dve.wait_ge(scaling, i * 3 + 1)
                v.tensor_tensor(y[:, two], y[:, two], vec[:, 1], ALU.mult).then_inc(scaling, 1)
                dve.wait_ge(scaling, i * 3 + 2)
                v.tensor_tensor(y[:, two], y[:, two], vec[:, 2], ALU.add).then_inc(scaling, 1)
                dve.wait_ge(scaling, i * 3 + 3)
                v.tensor_tensor(x[:, r], x[:, r], y[:, two], ALU.add).then_inc(x_ready, 1)
            pipelined(dve, NB, [(3, residual), (4, finish), (0, message)], R)


def atom_out_phase(nc, d, keep):
    acc, ident = keep["acc"], keep["ident"]
    T = 7
    BATCHES, COLS, K, HALF = NB // T, T * P, F // P, T * P // 2
    LAYERS = 3
    with ExitStack() as ctx:
        sb = lambda n, shape, dt=F32: ctx.enter_context(nc.sbuf_tensor(f"o3_{n}", shape, dt))
        sem = phase_semaphores(nc, ctx, lambda n: f"o3_{n}")
        w1, w2 = sb("w1", [P, LAYERS, K, F]), sb("w2", [P, LAYERS, K, F])
        wv = sb("wv", [P, K, F])
        b1, b2 = sb("b1", [P, LAYERS, K]), sb("b2", [P, LAYERS, K])
        bv = sb("bv", [P, F])
        xi, x = sb("xi", [P, 2, T, F]), sb("x", [P, 2, T, F])
        v_rows = sb("v_rows", [P, T, F])
        vT, hT, logT = (sb(n, [P, K, COLS]) for n in ("vT", "hT", "logT"))
        y = sb("y", [P, T, F])
        bank = [[ctx.enter_context(nc.psum_tensor(f"o3_ps{s}{c}", [P, 512], F32)) for c in range(K)] for s in range(2)]
        bank_t = [ctx.enter_context(nc.psum_tensor(f"o3_pt{s}", [P, 512], F32)) for s in range(2)]
        bank_y = [ctx.enter_context(nc.psum_tensor(f"o3_py{s}", [P, 512], F32)) for s in range(2)]
        w_in, sent = sem("w_in"), sem("sent")
        tiles_in = [sem(f"tiles_in{r}") for r in range(2)]
        rows_ready, turned, vT_ready = sem("rows_ready"), sem("turned"), sem("vT_ready")
        up_ready = [sem(f"up_ready{s}") for s in range(2)]
        abs_ready = [sem(f"abs_ready{s}") for s in range(2)]
        exp_ready = [sem(f"exp_ready{s}") for s in range(2)]
        log_ready = [sem(f"log_ready{s}") for s in range(2)]
        max_ready = [sem(f"max_ready{s}") for s in range(2)]
        h_ready = [sem(f"h_ready{s}") for s in range(2)]
        down_ready = [sem(f"down_ready{s}") for s in range(2)]
        v_ready = [sem(f"v_ready{s}") for s in range(2)]
        y_ready, y_biased, y_done = sem("y_ready"), sem("y_biased"), sem("y_done")
        block = ctx.enter_context(nc.Block())
        half = lambda s: slice(s * HALF, (s + 1) * HALF)
        SP_N = LAYERS + 1

        @block.sync
        def _(sp):
            for n in range(LAYERS):
                for w, name in ((w1, "L3_gnn_res_w1"), (w2, "L3_gnn_res_w2")):
                    sp.dma_start(w[:, n], d[name][n].rearrange("(k p) f -> p k f", p=P)).then_inc(w_in, 16)
                for b, name in ((b1, "L3_gnn_res_b1"), (b2, "L3_gnn_res_b2")):
                    for k in range(K):
                        sp.dma_start(b[:, n, k:k + 1], d[name][n:n + 1, k * P:(k + 1) * P].rearrange("o p -> p o")).then_inc(w_in, 16)
            sp.dma_start(wv[:], d["L3_gnn_Wv"].rearrange("(k p) f -> p k f", p=P)).then_inc(w_in, 16)
            sp.dma_start(bv[:], d["L3_gnn_bv"].partition_broadcast(P)).then_inc(w_in, 16)

            def send(i):
                sp.wait_ge(y_done, i * T + T)
                sp.dma_start(d["out"][bass.ds(i * COLS, COLS), :].rearrange("(t p) f -> p t f", p=P), y[:]).then_inc(sent, 16)

            def load(m, r):
                for t, src in ((xi, d["xi"]), (x, d["x3"])):
                    sp.dma_start(t[:, r], src[bass.ds(m * COLS, COLS), :].rearrange("(t p) f -> p t f", p=P)).then_inc(tiles_in[r], 16)

            def batch(i, r):
                send(i)
                load(i + 2, r)
            load(0, 0)
            load(1, 1)
            batch(0, 0)
            with sp.Fori(0, (BATCHES - 3) // 2) as pair:
                for r in range(2):
                    batch(pair * 2 + (1 + r), (1 + r) % 2)
            for i in range(BATCHES - 2, BATCHES):
                send(i)
            sp.wait_ge(sent, 16 * BATCHES)

        weights = 16 * (6 * LAYERS + 2)

        @block.tensor
        def _(pe):
            t = nc.tensor
            pe.wait_ge(w_in, weights)

            def batch(i):
                for j in range(T):
                    pe.wait_ge(rows_ready, i + 1)
                    if late(i, 1) or j >= 2:
                        pe.wait_ge(vT_ready, i * T + (j - 1))
                    for k in range(K):
                        last = t.transpose(bank_t[j % 2][:, k * P:(k + 1) * P], v_rows[:, j, k * P:(k + 1) * P], ident[:])
                    last.then_inc(turned, 1)

                def product(s, w, n, src, done):
                    for c in range(K):
                        for k in range(K):
                            last = t.matmul(bank[s][c][:, 0:HALF], w[:, n, k, c * P:(c + 1) * P], src[:, k, half(s)],
                                            start=k == 0, stop=k == K - 1)
                    last.then_inc(done, 1)

                for n in range(LAYERS):
                    for s in range(2):
                        if n == 0:
                            pe.wait_ge(vT_ready, (i + 1) * T)
                        else:
                            pe.wait_ge(v_ready[s], i * LAYERS + n)
                        product(s, w1, n, vT, up_ready[s])
                    for s in range(2):
                        pe.wait_ge(h_ready[s], i * SP_N + (n + 1))
                        product(s, w2, n, hT, down_ready[s])
                for s in range(2):
                    pe.wait_ge(h_ready[s], (i + 1) * SP_N)
                for j in range(T):
                    if late(i, 1) or j >= 2:
                        pe.wait_ge(y_biased, i * T + (j - 1))
                    for k in range(K):
                        last = t.matmul(bank_y[j % 2][:, 0:F], hT[:, k, j * P:(j + 1) * P], wv[:, k, :], start=k == 0, stop=k == K - 1)
                    last.then_inc(y_ready, 1)
            batch(0)
            with pe.Fori(1, BATCHES) as i:
                batch(i)

        @block.scalar
        def _(act):
            a = nc.scalar
            a.preload_act_table_set("natural_log_exp_and_others")
            act.wait_ge(w_in, weights)

            def batch(i):
                for n in range(SP_N):
                    for s in range(2):
                        m = i * SP_N + (n + 1)
                        if n < LAYERS:
                            act.wait_ge(up_ready[s], i * LAYERS + (n + 1))
                            for c in range(K):
                                last = a.activation(logT[:, c, half(s)], bank[s][c][:, 0:HALF], ACT.Abs, bias=b1[:, n, c:c + 1])
                        else:
                            act.wait_ge(v_ready[s], (i + 1) * LAYERS)
                            last = a.activation(logT[:, :, half(s)], vT[:, :, half(s)], ACT.Abs)
                        last.then_inc(abs_ready[s], 1)
                        act.wait_ge(abs_ready[s], m)
                        a.activation(logT[:, :, half(s)], logT[:, :, half(s)], ACT.Exp, scale=-1.0).then_inc(exp_ready[s], 1)
                        act.wait_ge(exp_ready[s], m)
                        a.activation(logT[:, :, half(s)], logT[:, :, half(s)], ACT.Ln, bias=1.0).then_inc(log_ready[s], 1)
            with act.Fori(0, BATCHES) as i:
                batch(i)

        @block.vector
        def _(dve):
            v = nc.vector
            dve.wait_ge(w_in, weights)

            def batch(i, r):
                dve.wait_ge(tiles_in[r], (i - r) * 16 + 32)
                v.tensor_tensor(v_rows[:], xi[:, r], acc[:, bass.ds(i * T, T), 0:F], ALU.add).then_inc(rows_ready, 1)
                for j in range(T):
                    dve.wait_ge(turned, i * T + (j + 1))
                    v.tensor_copy(vT[:, :, j * P:(j + 1) * P], bank_t[j % 2][:, 0:F].rearrange("p (k n) -> p k n", k=K)).then_inc(vT_ready, 1)
                for n in range(SP_N):
                    for s in range(2):
                        m = i * SP_N + (n + 1)
                        dve.wait_ge(log_ready[s], m)
                        if n < LAYERS:
                            for c in range(K):
                                last = v.tensor_scalar(hT[:, c, half(s)], bank[s][c][:, 0:HALF], b1[:, n, c:c + 1], 0.0, ALU.add, ALU.max)
                            last.then_inc(max_ready[s], 1)
                            dve.wait_ge(max_ready[s], i * LAYERS + (n + 1))
                            v.tensor_tensor(hT[:, :, half(s)], hT[:, :, half(s)], logT[:, :, half(s)], ALU.add).then_inc(h_ready[s], 1)
                        else:
                            v.scalar_tensor_tensor(out=hT[:, :, half(s)], in0=vT[:, :, half(s)], scalar=0.0, in1=logT[:, :, half(s)],
                                                   op0=ALU.max, op1=ALU.add).then_inc(h_ready[s], 1)
                    if n < LAYERS:
                        for s in range(2):
                            dve.wait_ge(down_ready[s], i * LAYERS + (n + 1))
                            for c in range(K):
                                last = v.scalar_tensor_tensor(out=vT[:, c, half(s)], in0=bank[s][c][:, 0:HALF], scalar=b2[:, n, c:c + 1],
                                                              in1=vT[:, c, half(s)], op0=ALU.add, op1=ALU.add)
                            last.then_inc(v_ready[s], 1)
                for j in range(T):
                    dve.wait_ge(y_ready, i * T + (j + 1))
                    if late(i, 1):
                        dve.wait_ge(sent, i * 16)
                    v.tensor_tensor(y[:, j], bank_y[j % 2][:, 0:F], bv[:], ALU.add).then_inc(y_biased, 1)
                    dve.wait_ge(y_biased, i * T + (j + 1))
                    v.tensor_tensor(y[:, j], y[:, j], x[:, r, j], ALU.add).then_inc(y_done, 1)
            batch(0, 0)
            with dve.Fori(0, (BATCHES - 1) // 2) as pair:
                for r in range(2):
                    batch(pair * 2 + (1 + r), (1 + r) % 2)


def consts_phase(nc, keep):
    ident, ident_b, iota = keep["ident"], keep["ident_b"], keep["iota"]
    with ExitStack() as ctx:
        sem = phase_semaphores(nc, ctx, lambda n: f"c_{n}")
        iota_i = ctx.enter_context(nc.sbuf_tensor("c_iota_i", [P, P], I32))
        zeroed, set_, made, copied = sem("zeroed"), sem("set"), sem("made"), sem("copied")
        block = ctx.enter_context(nc.Block())

        @block.gpsimd
        def _(pool):
            pool.iota(iota_i[:], pattern=[[1, P]], base=0, channel_multiplier=0).then_inc(made, 1)
            pool.memset(keep["zeros"][:], 0.0).then_inc(made, 1)
            pool.memset(keep["minus_half"][:], -0.5).then_inc(made, 1)
            pool.memset(keep["lowest"][:], MMIN).then_inc(made, 1)
            pool.memset(ident[:], 0.0).then_inc(zeroed, 1)
            pool.wait_ge(zeroed, 1)
            pool.affine_select(out=ident[:], in_=ident[:], compare_op=ALU.not_equal, fill=1.0, base=0,
                               pattern=[[-1, P]], channel_multiplier=1).then_inc(set_, 1)

        @block.vector
        def _(dve):
            dve.wait_ge(made, 1)
            nc.vector.tensor_copy(iota[:], iota_i[:]).then_inc(copied, 1)
            dve.wait_ge(set_, 1)
            nc.vector.tensor_copy(ident_b[:], ident[:]).then_inc(copied, 1)


def clear_phase(nc, keep):
    acc, mx = keep["acc"], keep["mx"]
    with ExitStack() as ctx:
        sem = phase_semaphores(nc, ctx, lambda n: f"z_{n}")
        cleared = sem("cleared")
        block = ctx.enter_context(nc.Block())

        @block.vector
        def _(dve):
            nc.vector.memset(acc[:, 0:NB // 2], 0.0).then_inc(cleared, 1)
            nc.vector.memset(mx[:], MMIN).then_inc(cleared, 1)

        @block.gpsimd
        def _(pool):
            pool.memset(acc[:, NB // 2:NB], 0.0).then_inc(cleared, 1)


def gnn_program(nc, d, out):
    dram = lambda name, cols, rows=NB * P: nc.dram_tensor(name, (rows, cols), F32, kind="Internal").ap()
    d["rec"] = [dram(f"rec{k}", RW, S * SE) for k in range(2)]
    d["late"] = nc.dram_tensor("late", (EP, EC, 5), F32, kind="Internal").ap()
    for name, width in (("L0", 2 * F), ("L1", 2 * F), ("L2", F + 4), ("L3", F)):
        d[f"{name}_table"] = dram(f"{name}_table", width)
    x1, x2, d["x3"], d["h1"], d["xi"] = (dram(n, F) for n in ("x1", "x2", "x3", "h1", "xi"))
    d["xs"] = [d["x"], x1, x2, x2]
    d["xs_updated"] = [x1, x2, None, d["x3"]]
    d["out"] = out
    with ExitStack() as ctx:
        sb = lambda name, shape, dt=F32: ctx.enter_context(nc.sbuf_tensor(name, shape, dt))
        keep = {"steps": sb("steps", [1, 2, S], I32), "ident": sb("ident", [P, P]), "ident_b": sb("ident_b", [P, P], BF16),
                "iota": sb("iota", [P, P]), "zeros": sb("zeros", [P, 264]), "lowest": sb("lowest", [P, 8]),
                "minus_half": sb("minus_half", [P, 1])}
        keep["scatter_dma"] = [ctx.enter_context(nc.semaphore(f"scatter_dma{r}")) for r in range(2)]
        keep["pool_dma"] = [ctx.enter_context(nc.semaphore(f"pool_dma{r}")) for r in range(8)]
        keep["column_dma"] = [ctx.enter_context(nc.semaphore(f"column_dma{r}")) for r in range(8)]
        keep["edge_phases"] = 0
        keep["q"] = sb("q", [P, NB, F])
        with ExitStack() as inner:
            sbi = lambda name, shape, dt=F32: inner.enter_context(nc.sbuf_tensor(name, shape, dt))
            keep |= {"pos": sbi("pos", [EP, 2, EC], I32), "gidx": sbi("gidx", [EP, 2, EC], I32),
                     "local": sbi("local", [EP, 2, EC]), "rel": sbi("rel", [EP, EC])}
            consts_phase(nc, keep)
            sort_phase(nc, d, keep)
        keep |= {"acc": sb("acc", [P, NB, 264]), "mx": sb("mx", [P, NB, 8])}
        phases = [
            lambda: clear_phase(nc, keep),
            lambda: edge_phase(nc, d, keep, "L0", 0, 8, "edge"),
            lambda: node_phase(nc, d, keep, 1),
            lambda: edge_phase(nc, d, keep, "L1", 0, 4, "rel"),
            lambda: relational_out_phase(nc, d, keep),
            lambda: node_phase(nc, d, keep, 2),
            lambda: edge_phase(nc, d, keep, "L2", 1, 4, "gat"),
            lambda: node_phase(nc, d, keep, 3),
            lambda: edge_phase(nc, d, keep, "L3", 1, 1, "conv"),
            lambda: atom_out_phase(nc, d, keep),
        ]
        for phase in phases:
            phase()


TRANSPOSED = ("L0_gnn_Wq", "L0_gnn_Wk", "L0_gnn_Wv", "L0_gnn_We", "L0_gnn_Wskip", "L3_gnn_G", "L3_gnn_Wi",
              "L3_gnn_Wj", "L3_gnn_res_w1", "L3_gnn_res_w2", "L3_gnn_Wv")


def kernel(**inputs):
    import numpy as np
    import concourse.bacc as bacc
    from concourse.bass_utils import run_bass_kernel_spmd

    nc = bacc.Bacc("TRN2", target_bir_lowering=False, num_devices=1)
    arrays, args = {}, {}
    for name, value in inputs.items():
        a = np.asarray(value)
        if name in TRANSPOSED:
            a = np.swapaxes(a, -1, -2)
        if name == "x":
            a = np.concatenate([a, np.zeros((NB * P - N, F), a.dtype)])
        a = np.ascontiguousarray(a)
        arrays[f"in_{name}"] = a
        args[name] = nc.dram_tensor(f"in_{name}", a.shape, mybir.dt.from_np(a.dtype), kind="ExternalInput").ap()
    out = nc.dram_tensor("out_x", (NB * P, F), F32, kind="ExternalOutput").ap()
    gnn_program(nc, args, out)
    result = run_bass_kernel_spmd(nc, [arrays], core_ids=[0])
    return result.results[0]["out_x"][:N]
```
